# Optimizing a Trainium2 kernel written in Bass

```python
import numpy as np
import jax
import jax.numpy as jnp

def _softmax(x, axis=-1):
    return jax.nn.softmax(x, axis=axis)

def _gelu(x):
    return jax.nn.gelu(x, approximate=True)

def _silu(x):
    return jax.nn.silu(x)

def _sigmoid(x):
    return jax.nn.sigmoid(x)

def _layernorm(x, axis=-1, eps=1e-05):
    m = jnp.mean(x, axis=axis, keepdims=True)
    v = jnp.var(x, axis=axis, keepdims=True)
    return (x - m) / jnp.sqrt(v + eps)

def _scatter_add(tgt, idx, src, axis=0):
    return tgt.at[idx].add(src)

def _segment_sum(src, seg, n):
    return jax.ops.segment_sum(src, seg, n)
kernel_name = 'mk_prb_d1_jaxref_r8_00089e'

def setup_inputs(seed: int=0):
    np.random.seed(seed)
    _w = jnp.asarray

    def _L0_attn_setup():
        import jax, jax.numpy as jnp
        from jax import lax
        import numpy as np
        B, L, D_MODEL = (1, 128, 256)
        H, P, G, S = (32, 64, 8, 32)
        D_SSM = H * P
        CONV_DIM = D_SSM + 2 * G * S
        PROJ_DIM = 2 * D_SSM + 2 * G * S + H
        K = 4
        EPS = 1e-05

        def _forward(hidden_states, W_in, b_in, conv_w, conv_b, A_log, D_param, dt_bias, norm_w, W_out, b_out, mup_vector):
            Bb, Ll, _ = hidden_states.shape
            zxbcdt = (hidden_states @ W_in + b_in) * mup_vector
            z = zxbcdt[..., :D_SSM]
            xBC = zxbcdt[..., D_SSM:D_SSM + CONV_DIM]
            dt = zxbcdt[..., D_SSM + CONV_DIM:]
            xBC_t = jnp.transpose(xBC, (0, 2, 1))
            conv = lax.conv_general_dilated(xBC_t, conv_w[:, None, :], (1,), [(K - 1, 0)], dimension_numbers=('NCH', 'OIH', 'NCH'), feature_group_count=CONV_DIM)
            xBC = jnp.transpose(jax.nn.silu(conv + conv_b[None, :, None]), (0, 2, 1))
            x = xBC[..., :D_SSM].reshape(Bb, Ll, H, P)
            Bm = xBC[..., D_SSM:D_SSM + G * S].reshape(Bb, Ll, G, S)
            Cm = xBC[..., D_SSM + G * S:].reshape(Bb, Ll, G, S)
            rep = H // G
            Bh = jnp.repeat(Bm, rep, axis=2)
            Ch = jnp.repeat(Cm, rep, axis=2)
            dt = jax.nn.softplus(dt + dt_bias)
            a = jnp.exp(dt * -jnp.exp(A_log))
            db = dt[..., None, None] * x[..., None] * Bh[:, :, :, None, :]

            def combine(e1, e2):
                a1, s1 = e1
                a2, s2 = e2
                return (a1 * a2, a2[..., None, None] * s1 + s2)
            states = lax.associative_scan(combine, (a, db), axis=1)[1]
            y = jnp.einsum('blhps,blhs->blhp', states, Ch) + D_param[None, None, :, None] * x
            y = y.reshape(Bb, Ll, D_SSM) * jax.nn.silu(z)
            yg = y.reshape(Bb, Ll, G, D_SSM // G)
            var = jnp.mean(yg * yg, axis=-1, keepdims=True)
            y = (yg * lax.rsqrt(var + EPS)).reshape(Bb, Ll, D_SSM) * norm_w
            return y @ W_out + b_out
        key = jax.random.key(seed)
        ks = jax.random.split(key, 12)
        mults = np.array([0.9, 1.1, 0.8, 1.2, 1.0], dtype=np.float32)
        mv = np.ones(PROJ_DIM, dtype=np.float32)
        mv[:D_SSM] *= mults[0]
        mv[D_SSM:2 * D_SSM] *= mults[1]
        mv[2 * D_SSM:2 * D_SSM + G * S] *= mults[2]
        mv[2 * D_SSM + G * S:2 * D_SSM + 2 * G * S] *= mults[3]
        mv[2 * D_SSM + 2 * G * S:] *= mults[4]
        return {'hidden_states': jax.random.normal(ks[0], (B, L, D_MODEL), jnp.float32), 'W_in': jax.random.normal(ks[1], (D_MODEL, PROJ_DIM), jnp.float32) * 0.02, 'b_in': jax.random.normal(ks[2], (PROJ_DIM,), jnp.float32) * 0.01, 'conv_w': jax.random.normal(ks[3], (CONV_DIM, K), jnp.float32) * 0.2, 'conv_b': jax.random.normal(ks[4], (CONV_DIM,), jnp.float32) * 0.01, 'A_log': jnp.log(jax.random.uniform(ks[5], (H,), jnp.float32, 1.0, 16.0)), 'D_param': jax.random.normal(ks[6], (H,), jnp.float32) * 0.5 + 1.0, 'dt_bias': jax.random.normal(ks[7], (H,), jnp.float32) * 0.5, 'norm_w': jnp.ones((D_SSM,), jnp.float32) + 0.01 * jax.random.normal(ks[8], (D_SSM,), jnp.float32), 'W_out': jax.random.normal(ks[9], (D_SSM, D_MODEL), jnp.float32) * 0.02, 'b_out': jnp.zeros((D_MODEL,), jnp.float32), 'mup_vector': jnp.asarray(mv)}
    _L0_attn_in = _L0_attn_setup()

    def _L0_ffn_setup():
        import jax, jax.numpy as jnp
        import numpy as np
        H = 256
        I_MOE = 176
        I_SH = 704
        E = 8
        TOP_K = 2
        B, S = (1, 256)

        def _silu_and_mul(gu, inter):
            return jax.nn.silu(gu[..., :inter]) * gu[..., inter:]
        key = jax.random.key(seed)
        ks = jax.random.split(key, 7)
        sc = 0.02
        return {'hidden_states': jax.random.normal(ks[0], (B, S, H), jnp.float32), 'W_router': jax.random.normal(ks[1], (E, H), jnp.float32) * sc, 'W_sgate': jax.random.normal(ks[2], (1, H), jnp.float32) * sc, 'Ws_gate_up': jax.random.normal(ks[3], (H, 2 * I_SH), jnp.float32) * sc, 'Ws_down': jax.random.normal(ks[4], (I_SH, H), jnp.float32) * sc, 'We_gate_up': jax.random.normal(ks[5], (E, H, 2 * I_MOE), jnp.float32) * sc, 'We_down': jax.random.normal(ks[6], (E, I_MOE, H), jnp.float32) * sc}
    _L0_ffn_in = _L0_ffn_setup()
    _d = {'L0_attn_hidden_states': _L0_attn_in['hidden_states'], 'L0_attn_W_in': _L0_attn_in['W_in'], 'L0_attn_b_in': _L0_attn_in['b_in'], 'L0_attn_conv_w': _L0_attn_in['conv_w'], 'L0_attn_conv_b': _L0_attn_in['conv_b'], 'L0_attn_A_log': _L0_attn_in['A_log'], 'L0_attn_D_param': _L0_attn_in['D_param'], 'L0_attn_dt_bias': _L0_attn_in['dt_bias'], 'L0_attn_norm_w': _L0_attn_in['norm_w'], 'L0_attn_W_out': _L0_attn_in['W_out'], 'L0_attn_b_out': _L0_attn_in['b_out'], 'L0_attn_mup_vector': _L0_attn_in['mup_vector'], 'L0_ffn_W_router': _L0_ffn_in['W_router'], 'L0_ffn_W_sgate': _L0_ffn_in['W_sgate'], 'L0_ffn_Ws_gate_up': _L0_ffn_in['Ws_gate_up'], 'L0_ffn_Ws_down': _L0_ffn_in['Ws_down'], 'L0_ffn_We_gate_up': _L0_ffn_in['We_gate_up'], 'L0_ffn_We_down': _L0_ffn_in['We_down']}
    _x0 = _d['L0_attn_hidden_states']
    _d['L0_attn_hidden_states'] = jax.random.normal(jax.random.fold_in(jax.random.key(seed), 1), (4, 1024, 256), dtype=_x0.dtype)
    del _x0
    return _d

def reference(L0_attn_hidden_states, L0_attn_W_in, L0_attn_b_in, L0_attn_conv_w, L0_attn_conv_b, L0_attn_A_log, L0_attn_D_param, L0_attn_dt_bias, L0_attn_norm_w, L0_attn_W_out, L0_attn_b_out, L0_attn_mup_vector, L0_ffn_W_router, L0_ffn_W_sgate, L0_ffn_Ws_gate_up, L0_ffn_Ws_down, L0_ffn_We_gate_up, L0_ffn_We_down):

    def _L0_attn_ref(hidden_states, W_in, b_in, conv_w, conv_b, A_log, D_param, dt_bias, norm_w, W_out, b_out, mup_vector):
        import jax, jax.numpy as jnp
        from jax import lax
        import numpy as np
        B, L, D_MODEL = (1, 128, 256)
        H, P, G, S = (32, 64, 8, 32)
        D_SSM = H * P
        CONV_DIM = D_SSM + 2 * G * S
        PROJ_DIM = 2 * D_SSM + 2 * G * S + H
        K = 4
        EPS = 1e-05

        def _forward(hidden_states, W_in, b_in, conv_w, conv_b, A_log, D_param, dt_bias, norm_w, W_out, b_out, mup_vector):
            Bb, Ll, _ = hidden_states.shape
            zxbcdt = (hidden_states @ W_in + b_in) * mup_vector
            z = zxbcdt[..., :D_SSM]
            xBC = zxbcdt[..., D_SSM:D_SSM + CONV_DIM]
            dt = zxbcdt[..., D_SSM + CONV_DIM:]
            xBC_t = jnp.transpose(xBC, (0, 2, 1))
            conv = lax.conv_general_dilated(xBC_t, conv_w[:, None, :], (1,), [(K - 1, 0)], dimension_numbers=('NCH', 'OIH', 'NCH'), feature_group_count=CONV_DIM)
            xBC = jnp.transpose(jax.nn.silu(conv + conv_b[None, :, None]), (0, 2, 1))
            x = xBC[..., :D_SSM].reshape(Bb, Ll, H, P)
            Bm = xBC[..., D_SSM:D_SSM + G * S].reshape(Bb, Ll, G, S)
            Cm = xBC[..., D_SSM + G * S:].reshape(Bb, Ll, G, S)
            rep = H // G
            Bh = jnp.repeat(Bm, rep, axis=2)
            Ch = jnp.repeat(Cm, rep, axis=2)
            dt = jax.nn.softplus(dt + dt_bias)
            a = jnp.exp(dt * -jnp.exp(A_log))
            db = dt[..., None, None] * x[..., None] * Bh[:, :, :, None, :]

            def combine(e1, e2):
                a1, s1 = e1
                a2, s2 = e2
                return (a1 * a2, a2[..., None, None] * s1 + s2)
            states = lax.associative_scan(combine, (a, db), axis=1)[1]
            y = jnp.einsum('blhps,blhs->blhp', states, Ch) + D_param[None, None, :, None] * x
            y = y.reshape(Bb, Ll, D_SSM) * jax.nn.silu(z)
            yg = y.reshape(Bb, Ll, G, D_SSM // G)
            var = jnp.mean(yg * yg, axis=-1, keepdims=True)
            y = (yg * lax.rsqrt(var + EPS)).reshape(Bb, Ll, D_SSM) * norm_w
            return y @ W_out + b_out
        return _forward(hidden_states, W_in, b_in, conv_w, conv_b, A_log, D_param, dt_bias, norm_w, W_out, b_out, mup_vector)

    def _L0_ffn_ref(hidden_states, W_router, W_sgate, Ws_gate_up, Ws_down, We_gate_up, We_down):
        import jax, jax.numpy as jnp
        import numpy as np
        H = 256
        I_MOE = 176
        I_SH = 704
        E = 8
        TOP_K = 2
        B, S = (1, 256)

        def _silu_and_mul(gu, inter):
            return jax.nn.silu(gu[..., :inter]) * gu[..., inter:]
        orig_shape = hidden_states.shape
        x = hidden_states.reshape(-1, H)
        T = x.shape[0]
        logits = x @ W_router.T
        probs = jax.nn.softmax(logits.astype(jnp.float32), axis=-1)
        rw, sel = jax.lax.top_k(probs, TOP_K)
        rw = rw.astype(x.dtype)
        combine = jnp.zeros((T, E), x.dtype).at[jnp.arange(T)[:, None], sel].add(rw)
        sh = _silu_and_mul(x @ Ws_gate_up, I_SH) @ Ws_down
        shared_out = sh * jax.nn.sigmoid(x @ W_sgate.T)
        gu = jnp.einsum('th,ehi->eti', x, We_gate_up)
        h = _silu_and_mul(gu, I_MOE)
        eo = jnp.einsum('eti,eih->eth', h, We_down)
        sparse_out = jnp.einsum('eth,te->th', eo, combine)
        return (shared_out + sparse_out).reshape(orig_shape)
    x = L0_attn_hidden_states
    xn = _layernorm(x, axis=-1)
    x = x + _L0_attn_ref(xn, L0_attn_W_in, L0_attn_b_in, L0_attn_conv_w, L0_attn_conv_b, L0_attn_A_log, L0_attn_D_param, L0_attn_dt_bias, L0_attn_norm_w, L0_attn_W_out, L0_attn_b_out, L0_attn_mup_vector) + _L0_ffn_ref(xn, L0_ffn_W_router, L0_ffn_W_sgate, L0_ffn_Ws_gate_up, L0_ffn_Ws_down, L0_ffn_We_gate_up, L0_ffn_We_down)
    return x

_drawn_inputs = setup_inputs


def setup_inputs(seed=0):
    import zlib

    import numpy as np

    out = dict(_drawn_inputs(seed))
    spreads = {'L0_attn_b_out': (0.0, 0.8)}
    factors = {'L0_attn_A_log': 64.0,
     'L0_attn_dt_bias': 22.064,
     'L0_attn_norm_w': 64.0,
     'L0_ffn_W_router': 8.0,
     'L0_ffn_W_sgate': 8.0,
     'L0_ffn_Ws_gate_up': 5.301,
     'L0_ffn_Ws_down': 5.3,
     'L0_ffn_We_gate_up': 8.0,
     'L0_ffn_We_down': 8.0}
    for name, (base, spread) in spreads.items():
        noise = np.random.default_rng([zlib.crc32(name.encode()), seed]).standard_normal(out[name].shape)
        drawn = base * np.exp(spread * noise) if base else spread * noise
        out[name] = jnp.asarray(drawn.astype(out[name].dtype))
    for name, factor in factors.items():
        out[name] = (out[name] * factor).astype(out[name].dtype)
    return out
```

```python
from contextlib import ExitStack

import concourse.bass as bass
from concourse import mybir

ALU = mybir.AluOpType
ACT = mybir.ActivationFunctionType
AX = mybir.AxisListType
F32 = mybir.dt.float32
F16 = mybir.dt.float16
BF16 = mybir.dt.bfloat16
U32 = mybir.dt.uint32
ABSMAX = bass.bass_isa.ReduceOp.absmax

P = 128
D = 256
KC = D // P
TT = 512
Q = TT // P
H, HP, G, S = 32, 64, 8, 32
DS = H * HP
GH = G // 2
NX = DS // P
NB = G * S // P
NCONV = NX + 2 * NB
TAPS = 4
E = 8
I_SH, I_MOE = 704, 176
FI = I_SH + E * I_MOE
NF = -(-FI // P)
TAIL = I_MOE % 32
PARTS = [E] * (I_SH // 32) + [e for e in range(E) for _ in range(I_MOE // 32)] + [E + 1 + i for i in range(E * TAIL // 32)]
EPS = 1e-5
DECAY_FLOOR = -104.0
A_LOG_TOP = 80.0
UP = 256.0
RA = RD = 3

CONV_ORDER = [NX, NX + 1, NX + 2, NX + 3] + list(range(NX))
FFN_LAG = 5
STEPS = NF + FFN_LAG
NY = 3
AHEAD = 2
TILES = 8
V_LINKS = 106


class Signal:

    def __init__(self, sem, names, first=()):
        self.sem, self.n, self.n0 = sem, len(names), len(first)
        self.pos = {name: i for i, name in enumerate(names)}
        self.first = {name: i for i, name in enumerate(first)}
        assert len(self.pos) == len(names)

    def at(self, t, name):
        if t is None:
            return self.first[name] + 1
        return self.n0 + t * self.n + self.pos[name] + 1

    def before(self, t, name, k):
        i = self.pos[name]
        return self.n0 + t * self.n + (i - k + 1 if self.n % k == 0 else max(0, i - k + 1))


def ring_a():
    out = []
    for n in range(AHEAD, STEPS):
        if n < NCONV:
            out.append(("u", n))
        if n >= FFN_LAG:
            out.append(("gate", n - FFN_LAG))
    out += [("E", 0, 0), ("diff", 0), ("diff", 1)]
    for s in range(Q * G):
        q, g = divmod(s, G)
        if s + 2 < Q * G:
            out.append(("diff", s + 2))
        else:
            out.append(("z", s + 2 - Q * G))
        if g == 1:
            out.append(("E", q, 1))
        if q + 1 < Q and g == 5:
            out.append(("E", q + 1, 0))
    return out + [("z", n) for n in range(2, NX)] + [("u", n) for n in range(AHEAD)]


def ring_d():
    out = ["comb", "cum", "suffix"]
    for n in range(NF):
        out += [("up", n), ("bc", n)]
        out += {NF - 2: [("xt", 0, 0), ("xt", 0, 1), ("bt", 0)], NF - 1: [("xt", 0, 2), ("xt", 0, 3)]}.get(n, [])
    for s in range(Q * G):
        q, g = divmod(s, G)
        out.append(("y", s))
        if g == 2:
            out.append(("st", q))
        if q + 1 < Q:
            out += {2: [("xt", q + 1, 0)], 4: [("xt", q + 1, 1)], 5: [("bt", q + 1)], 6: [("xt", q + 1, 2)],
                    7: [("xt", q + 1, 3)]}.get(g, [])
    return out + ["rt0", "xn0", "xn1", ("rb", 0), "small", ("rb", 1), "rt1"] + [("rb", g) for g in range(2, G)] + ["ot0", "ot1"]


def layer_program(nc, x, w_in, w_small, w_gu, w_out, w_down, par, rows, constf, constb, c_rows, out):
    ctx = ExitStack()
    with ctx:
        def sb(name, shape, dt):
            return ctx.enter_context(nc.sbuf_tensor(name, shape, dt))

        def sem(name):
            return ctx.enter_context(nc.semaphore(name))

        win_h = sb("win_h", [P, KC, 2 * DS + 2 * G * S], F16)
        win_l = sb("win_l", [P, KC, 2 * DS + 2 * G * S], F16)
        gu_h = sb("gu_h", [P, KC, 2, FI], F16)
        gu_l = sb("gu_l", [P, KC, 2, FI], F16)
        wo_h = sb("wo_h", [P, NX, D], F16)
        wo_l = sb("wo_l", [P, NX, D], F16)
        wd = sb("wd", [P, NF, D], F32)
        wsm = sb("wsm", [P, KC, H + E + 1], F32)
        NIN = 2 * NX + 2 * NB
        parm = sb("parm", [P, par.shape[1]], F32)
        o = 0
        views = []
        for n in (NIN, NIN, NCONV * TAPS, NCONV, NX, NX, KC):
            views.append(parm[:, o:o + n])
            o += n
        mup, b_in, conv_w, conv_b, d_par, norm_w, b_out = views
        row = sb("row", [P, 4, H], F32)
        cf = sb("cf", [P, constf.shape[1]], F32)
        ident, tri_u, tri_s = cf[:, 0:P], cf[:, P:2 * P], cf[:, 2 * P:3 * P]
        o = 3 * P
        ownrow = cf[:, o:o + 4]
        lower = cf[:, o + 4:o + 4 + E * E].rearrange("p (a b) -> p a b", b=E)
        cb = sb("cb", [P, constb.shape[1]], BF16)
        identb, maskneg = cb[:, 0:P], cb[:, P:2 * P]
        sel, negsel = cb[:, 2 * P:2 * P + H], cb[:, 2 * P + H:2 * P + 2 * H]
        seltail = cb[:, 2 * P + 2 * H:3 * P + 2 * H]
        ev_scale = sb("ev_scale", [P, NIN], F32)
        ev_bias = sb("ev_bias", [P, NIN], F32)
        carrier = sb("carrier", [P, 1], F32)
        one = sb("one", [P, 1], F32)
        amax = sb("amax", [P, 3], F32)
        gmax = sb("gmax", [P, 3], F32)
        pow2 = sb("pow2", [P, 3], F32)
        up_s = sb("up_s", [P, 3], F32)
        down_s = sb("down_s", [P, 3], F32)
        neg_a = sb("neg_a", [P, H], F32)
        half = sb("half", [P, 1], F32)
        gv = sb("gv", [P, Q * GH], F32)
        keep_v = sb("keep_v", [P, 1], F32)
        keep_p = sb("keep_p", [P, 1], F32)

        xbc = sb("xbc", [P, NCONV, TT], F32)
        xh = sb("xh", [P, KC, TT], F16)
        xl = sb("xl", [P, KC, TT], F16)
        out_t = sb("out_t", [P, KC, TT], F32)
        hist = sb("hist", [P, NCONV, TAPS - 1], F32)
        sc = sb("sc", [P, G, HP], F32)
        v_dt = sb("v_dt", [P, Q, H], F32)
        ex = sb("ex", [P, Q, H + E + 1], F32)
        exi = sb("exi", [P, Q, H + E + 1], F32)
        dt = sb("dt", [P, Q, H], F32)
        da = sb("da", [P, Q, H], F32)
        tmp = sb("tmp", [P, Q, H], F32)
        w_end = sb("w_end", [P, Q, H], F32)
        tmp2 = w_end
        probs = sb("probs", [P, Q, E], F32)
        rank = sb("rank", [P, Q, E], F32)
        cmb = sb("cmb", [P, Q, E + 1], F32)
        cmbb = sb("cmbb", [96, TT], BF16)
        cumb = sb("cumb", [96, TT], BF16)
        stat = sb("stat", [P, Q, 6], F32)
        mv = sb("mv", [P, Q, 2], F32)
        rstd = sb("rstd", [P, Q], F32)
        veps = sb("veps", [P, Q], F32)
        lmax = sb("lmax", [P, Q], F32)
        lsum = sb("lsum", [P, Q], F32)
        UW = TT + TAPS - 1
        ARENA = G * 4 * HP + 3 * (UW + 1) + 8 * TT + 2 * DS - DS // 2
        arena = sb("arena", [P, ARENA], F32)
        sbd = arena[:, 0:G * 4 * HP].rearrange("p (g c) -> p g c", g=G)
        at = [G * 4 * HP]

        def carve(n):
            at[0] += n
            assert at[0] <= ARENA
            return arena[:, at[0] - n:at[0]]

        u = [carve(UW + 1)[:, 0:UW] for _ in range(3)]
        acc = [carve(TT) for _ in range(3)]
        top = at[0]
        gact = [carve(TT) for _ in range(2)]
        low_hin = at[0]
        hin = [carve(TT) for _ in range(3)]
        high = at[0]
        at[0] = low_hin
        sp_r = carve(TT)[0:32, :]
        sp_b = carve(TT // 2)[0:32, :].bitcast(BF16)
        big = [carve(Q * E * E).rearrange("p (q a b) -> p q a b", q=Q, a=E) for _ in range(2)]
        assert at[0] <= high
        at[0] = G * 4 * HP
        cm = carve(G * P).rearrange("p (g i) -> p g i", g=G)
        eb = carve(G * P).rearrange("p (g i) -> p g i", g=G)
        crep = carve(G * P).rearrange("p (g i) -> p g i", g=G)
        at[0] = top
        lb = [carve(4 * P) for _ in range(2)]
        mb = [carve(4 * P) for _ in range(2)]
        at[0] = high
        bp = carve(G * 4 * S).rearrange("p (g h s) -> p g h s", g=G, h=4)
        xd = carve(DS)
        at[0] = G * 4 * HP
        sz = [carve(TT) for _ in range(2)]
        sq = [carve(TT) for _ in range(2)]
        xld = carve(Q * D).rearrange("p (q d) -> p q d", q=Q)
        at[0] = top
        x32 = carve(KC * TT).rearrange("p (c t) -> p c t", c=KC)
        at[0] = high
        xres = carve(Q * D).rearrange("p (q d) -> p q d", q=Q)
        yh = [carve(TT // 2).bitcast(F16) for _ in range(NY)]
        yl = [carve(TT // 2).bitcast(F16) for _ in range(NY)]
        sq_odd = carve(TT)
        raw_in = xbc[:, :, :].rearrange("p n t -> p (n t)")[:, 0:KC * (2 * DS + 2 * G * S)]
        raw_gu = arena[:, 0:KC * 2 * FI]
        raw_out = xbc[:, :, :].rearrange("p n t -> p (n t)")[:, 0:NX * D]

        bank = [ctx.enter_context(nc.psum_tensor(f"bank{i}", [P, TT], F32)) for i in range(8)]
        rstdb = [cmbb, cumb]
        acc_bank, a_bank, d_bank = bank[0:2], bank[2:5], bank[5:8]

        RAW, RDW = ring_a(), ring_d()
        PREP = ["xn0", "xn1", "small"]
        assert len(RAW) % RA == 0
        s_const = sem("s_const")
        s_raw = [sem(f"s_raw{i}") for i in range(3)]
        s_mag = sem("s_mag")
        s_gmax = sem("s_gmax")
        s_up = sem("s_up")
        s_hi = sem("s_hi")
        s_lo = sem("s_lo")
        s_zero = sem("s_zero")
        s_alog = sem("s_alog")
        a_full = Signal(sem("a_full"), RAW, RAW[-AHEAD:])
        a_done = Signal(sem("a_done"), RAW, ["a_log"] + RAW[-AHEAD:])
        d_full = Signal(sem("d_full"), RDW, PREP)
        d_done = Signal(sem("d_done"), RDW, PREP)
        s_chain = sem("s_chain")
        s_u = Signal(sem("s_u"), [("pad", n) for n in range(NCONV)])
        s_hist = Signal(sem("s_hist"), [("hist", n) for n in range(NCONV)], ["zero"])
        s_conv = Signal(sem("s_conv"), list(range(NCONV)))
        s_silu = Signal(sem("s_silu"), list(range(NCONV)))
        s_route = sem("s_route")
        s_da = sem("s_da")
        s_split = Signal(sem("s_split"), ["cmbb", "cumb"])
        s_down = Signal(sem("s_down"), list(range(NF)))
        s_ffn = sem("s_ffn")
        s_wend = sem("s_wend")
        s_crow = sem("s_crow")
        s_crep = [sem(f"s_crep{b}") for b in range(2)]
        s_cm = Signal(sem("s_cm"), [(q, b) for q in range(Q) for b in range(2)])
        s_cs = Signal(sem("s_cs"), [(q, b) for q in range(Q) for b in range(2)])
        s_g = Signal(sem("s_g"), [(q, b) for q in range(Q) for b in range(2)])
        s_m = Signal(sem("s_m"), list(range(Q * G)))
        s_carry = sem("s_carry")
        s_sbd = Signal(sem("s_sbd"), [(q, b) for q in range(Q) for b in range(2)], ["zero"])
        s_y = Signal(sem("s_y"), list(range(NX)))
        s_sq = Signal(sem("s_sq"), list(range(NX)))
        s_pair = Signal(sem("s_pair"), list(range(G)))
        s_gs = Signal(sem("s_gs"), list(range(G)))
        s_gv = Signal(sem("s_gv"), [0, 1])
        s_x = sem("s_x")
        s_xres = sem("s_xres")
        s_var = sem("s_var")
        s_pow = Signal(sem("s_pow"), ["ln", "g0", "g1"], ["ln"])
        s_xn = sem("s_xn")
        s_xh = Signal(sem("s_xh"), [0, 1], [0, 1])
        s_xl = Signal(sem("s_xl"), [0, 1], [0, 1])
        s_exi = sem("s_exi")
        s_ex = sem("s_ex")
        s_rp = Signal(sem("s_rp"), [0, 1])
        s_yn = Signal(sem("s_yn"), list(range(0, NX, 2)))
        s_yh = Signal(sem("s_yh"), list(range(NX)))
        s_yl = Signal(sem("s_yl"), list(range(NX)))
        s_wo = Signal(sem("s_wo"), list(range(NX)))
        s_out_t = Signal(sem("s_out_t"), ["out"], ["none"])
        s_out = sem("s_out")

        block = ctx.enter_context(nc.Block())

        def rows_of(n):
            return P if n < NF - 1 else FI - (NF - 1) * P

        def made_in(t, n):
            return t - 1 if n < AHEAD else t

        def span(q):
            return slice(q * P, (q + 1) * P)

        def carry_vector():
            nc.vector.tensor_copy(carrier[:, :], keep_v[:, :])

        @block.sync
        def _(sp):
            sp.dma_start(parm[:, :], par).then_inc(s_const, 16)
            sp.dma_start(row[:, :, :], rows).then_inc(s_const, 16)
            n_in = raw_in.shape[1] // 4
            for i in range(4):
                sp.dma_start(raw_in[:, i * n_in:(i + 1) * n_in], w_in[:, i * n_in:(i + 1) * n_in]).then_inc(s_raw[0], 16)
            n_gu = raw_gu.shape[1] // 4
            for i in range(4):
                sp.dma_start(raw_gu[:, i * n_gu:(i + 1) * n_gu], w_gu[:, i * n_gu:(i + 1) * n_gu]).then_inc(s_raw[1], 16)
            sp.dma_start(cf[:, :], constf).then_inc(s_const, 16)
            sp.dma_start(cb[:, :], constb.bitcast(BF16)).then_inc(s_const, 16)
            sp.dma_start(wsm[:, :, :], w_small).then_inc(s_const, 16)
            sp.dma_start(wd[:, :, :], w_down).then_inc(s_const, 16)
            sp.wait_ge(s_lo, 4)
            sp.wait_ge(s_hi, 4)
            sp.dma_start(raw_out, w_out).then_inc(s_raw[2], 16)
            sp.wait_ge(s_lo, 8)
            sp.wait_ge(s_hi, 8)
            sp.dma_start(xld, x[0]).then_inc(s_x, 16)
            with sp.Fori(0, TILES) as t:
                sp.wait_ge(s_silu.sem, s_silu.at(t, 2 * NB - 1))
                sp.dma_start(c_rows.rearrange("b p t -> p b t"), xbc[:, NX + NB:NX + 2 * NB, :]).then_inc(s_crow, 16)
                sp.wait_ge(s_silu.sem, s_silu.at(t, NCONV - 1))
                for q in range(Q):
                    for b in range(2):
                        if q:
                            sp.wait_ge(d_full.sem, d_full.at(t, ("y", G * (q - 1) + 4 * b + 3)))
                        for h in range(4):
                            sp.dma_start(crep[S * h:S * (h + 1), 4 * b:4 * b + 4, :],
                                         c_rows[b].rearrange("(r s) t -> s r t", s=S)[:, :, span(q)]).then_inc(s_crep[b], 16)
                sp.wait_ge(d_full.sem, d_full.at(t, ("y", Q * G - 1)))
                sp.dma_start(xld, x[t + 1]).then_inc(s_x, 16)
                sp.wait_ge(s_out, 16 * (t + 1))
                sp.dma_start(xres, x[t]).then_inc(s_xres, 16)
                sp.wait_ge(d_done.sem, d_done.at(t, "ot1"))
                sp.dma_start(out[t], xres).then_inc(s_out, 16)
            sp.wait_ge(s_out, 16 * (TILES + 1))

        @block.tensor
        def _(pe):
            mm = nc.tensor.matmul

            def a_slot(t, item):
                if t is not None:
                    pe.wait_ge(a_done.sem, a_done.before(t, item, RA))
                return a_bank[a_done.pos[item] % RA]

            def d_slot(t, item):
                if t is None:
                    return d_bank[d_done.first[item]]
                pe.wait_ge(d_done.sem, d_done.before(t, item, RD))
                return d_bank[d_done.pos[item] % RD]

            def pairs(o, wh, wl, rh, rl, start=True, stop=True):
                mm(o, wh, rh, start=start, stop=False)
                mm(o, wh, rl, start=False, stop=False)
                return mm(o, wl, rh, start=False, stop=stop)

            def project(o, wh, wl):
                for c in range(KC):
                    last = pairs(o, wh[c], wl[c], xh[:, c, :], xl[:, c, :], start=c == 0, stop=c == KC - 1)
                return last

            def in_block(t, item, k):
                cols = slice(k * P, (k + 1) * P)
                b = a_slot(t, item)
                project(b[:, :], [win_h[:, c, cols] for c in range(KC)],
                        [win_l[:, c, cols] for c in range(KC)]).then_inc(a_full.sem, 1)

            def ffn_block(t, n):
                m = rows_of(n)
                cols = slice(n * P, n * P + m)
                for j, slot, item, full in ((0, a_slot, ("gate", n), a_full), (1, d_slot, ("up", n), d_full)):
                    b = slot(t, item)
                    project(b[0:m, :], [gu_h[:, c, j, cols] for c in range(KC)],
                            [gu_l[:, c, j, cols] for c in range(KC)]).then_inc(full.sem, 1)
                b = d_slot(t, ("bc", n))
                if n == 0:
                    pe.wait_ge(s_split.sem, s_split.at(t, "cmbb"))
                parts = PARTS[4 * n:4 * n + 4]
                wide = len(set(parts)) == 1
                for j, part in enumerate(parts[:1] if wide else parts):
                    if part > E:
                        pick = seltail[0:96, 32 * (part - E - 1):32 * (part - E)]
                    else:
                        pick = sel[0:96, part:part + 1].broadcast_to([96, P if wide else 32])
                    last = mm(b[:, :] if wide else b[32 * j:32 * j + 32, :], pick, cmbb[:, :], start=True, stop=True,
                              skip_group_check=True)
                last.then_inc(d_full.sem, 1)

            def ffn_down(t, n):
                m = rows_of(n)
                pe.wait_ge(d_done.sem, d_done.at(t, ("bc", n)))
                if n == 0:
                    pe.wait_ge(s_out_t.sem, t + s_out_t.n0)
                for c in range(KC):
                    last = mm(acc_bank[c][:, :], wd[0:m, n, c * P:(c + 1) * P], hin[n % 3][0:m, :],
                              start=n == 0, stop=n == NF - 1)
                last.then_inc(s_down.sem, 1)

            def prep_tokens(t, k):
                pe.wait_ge(s_xn, k + 1)
                for c in range(KC):
                    b = d_slot(t, f"xn{c}")
                    for q in range(Q):
                        last = nc.tensor.transpose(b[:, span(q)], xld[:, q, c * P:(c + 1) * P], ident)
                    last.then_inc(d_full.sem, 1)

            def prep_small(t):
                pe.wait_ge(d_done.sem, d_done.at(t, "xn1"))
                b = d_slot(t, "small")
                w = H + E + 1
                for q in range(Q):
                    for c in range(KC):
                        last = mm(b[:, q * w:(q + 1) * w], x32[:, c, span(q)], wsm[:, c, :],
                                  start=c == 0, stop=c == KC - 1)
                last.then_inc(d_full.sem, 1)

            def chunk_decay(t, q, b):
                eo = a_slot(t, ("E", q, b))
                if q == 0 and b == 0:
                    pe.wait_ge(s_split.sem, s_split.at(t, "cumb"))
                for r in range(4):
                    g = 4 * b + r
                    for h in range(4):
                        e = mm(eo[S * h:S * (h + 1), span(r)], sel[0:96, 4 * g + h:4 * g + h + 1].broadcast_to([96, S]),
                               cumb[:, span(q)], start=True, stop=True, skip_group_check=True)
                e.then_inc(a_full.sem, 1)

            def c_times_b(t, q, b):
                if q == 0:
                    pe.wait_ge(s_ffn, t + 1)
                else:
                    pe.wait_ge(s_m.sem, s_m.at(t, G * (q - 1) + 4 * b + 3))
                pe.wait_ge(s_cm.sem, s_cm.at(t, (q, b)))
                for r in range(4):
                    c = mm(acc_bank[b][:, span(r)], xbc[:, NX + b, span(q)], cm[:, 4 * b + r, :], start=True, stop=True)
                c.then_inc(s_g.sem, 1)

            def diff(t, s):
                q, g = divmod(s, G)
                b = a_slot(t, ("diff", s))
                mm(b[:, :], cumb[:, span(q)], negsel[0:96, 4 * g:4 * g + 4].unsqueeze(2).broadcast_to([96, 4, P]),
                   start=True, stop=False)
                for h in range(4):
                    mm(b[:, span(h)], sel[0:96, 4 * g + h:4 * g + h + 1].broadcast_to([96, P]),
                              cumb[:, span(q)], start=False, stop=False, skip_group_check=True)
                mm(b[:, :], identb, maskneg.unsqueeze(1).broadcast_to([P, 4, P]), start=False,
                   stop=True).then_inc(a_full.sem, 1)

            def x_tokens(t, q, r):
                b = d_slot(t, ("xt", q, r))
                if q == 0:
                    pe.wait_ge(s_silu.sem, s_silu.at(t, 2 * NB + 4 * r + 3))
                for k in range(4):
                    last = nc.tensor.transpose(b[:, span(k)], xbc[:, 4 * r + k, span(q)], ident)
                last.then_inc(d_full.sem, 1)

            def b_tokens(t, q):
                b = d_slot(t, ("bt", q))
                for k in range(NB):
                    last = nc.tensor.transpose(b[:, span(k)], xbc[:, NX + k, span(q)], ident)
                last.then_inc(d_full.sem, 1)

            def states(t, q):
                b = d_slot(t, ("st", q))
                pe.wait_ge(d_done.sem, d_done.at(t, ("xt", q, 3)))
                for g in range(G):
                    for h in range(4):
                        last = mm(b[S * h:S * (h + 1), g * HP:(g + 1) * HP], bp[:, g, h, :],
                                  xd[:, (4 * g + h) * HP:(4 * g + h + 1) * HP], start=True, stop=True,
                                  skip_group_check=True)
                last.then_inc(d_full.sem, 1)

            def mix(t, s):
                q, g = divmod(s, G)
                b = d_slot(t, ("y", s))
                pe.wait_ge(s_m.sem, s_m.at(t, s))
                if g % 4 == 0:
                    pe.wait_ge(s_cs.sem, s_cs.at(t, (q, g // 4)))
                    if q:
                        pe.wait_ge(s_sbd.sem, s_sbd.at(t, (q - 1, g // 4)))
                    else:
                        pe.wait_ge(s_sbd.sem, s_sbd.n0 + t * s_sbd.n)
                for pr in range(2):
                    for e in range(2):
                        h = 2 * pr + e
                        mm(b[HP * e:HP * (e + 1), span(pr)], xd[:, (4 * g + h) * HP:(4 * g + h + 1) * HP],
                           mb[s % 2][:, span(h)], start=True, stop=False, skip_group_check=True)
                    last = mm(b[:, span(pr)], sbd[:, g, pr * P:(pr + 1) * P], crep[:, g, :],
                              start=False, stop=True, skip_group_check=True)
                last.then_inc(d_full.sem, 1)

            def blocks_ahead(t):
                pe.wait_ge(s_xh.sem, s_xh.at(t, KC - 1))
                pe.wait_ge(s_xl.sem, s_xl.at(t, KC - 1))
                for n in range(AHEAD):
                    in_block(t, ("u", n), NX + CONV_ORDER[n])

            pe.wait_ge(s_const, 6 * 16)
            prep_tokens(None, 0)
            prep_small(None)
            blocks_ahead(None)
            with pe.Fori(0, TILES) as t:
                for n in range(AHEAD, STEPS):
                    if n < NCONV:
                        in_block(t, ("u", n), NX + CONV_ORDER[n])
                    if n == 2:
                        pe.wait_ge(s_route, t + 1)
                        b = d_slot(t, "comb")
                        for q in range(Q):
                            last = nc.tensor.transpose(b[0:E + 1, span(q)], cmb[:, q, :], ident)
                        last.then_inc(d_full.sem, 1)
                    if n == 3:
                        pe.wait_ge(s_da, t + 1)
                        b = d_slot(t, "cum")
                        for q in range(Q):
                            last = mm(b[0:H, span(q)], da[:, q, :], tri_u, start=True, stop=True)
                        last.then_inc(d_full.sem, 1)
                        b = d_slot(t, "suffix")
                        mm(b[:, 0:Q * H], tri_s, da[:, :, :], start=True, stop=True).then_inc(d_full.sem, 1)
                    if n >= FFN_LAG:
                        ffn_block(t, n - FFN_LAG)
                    if n > FFN_LAG:
                        ffn_down(t, n - FFN_LAG - 1)
                    if n == STEPS - 2:
                        x_tokens(t, 0, 0)
                        x_tokens(t, 0, 1)
                        b_tokens(t, 0)
                    if n == STEPS - 1:
                        x_tokens(t, 0, 2)
                        x_tokens(t, 0, 3)
                        chunk_decay(t, 0, 0)
                        diff(t, 0)
                        diff(t, 1)
                ffn_down(t, NF - 1)
                c_times_b(t, 0, 0)
                for s in range(Q * G):
                    q, g = divmod(s, G)
                    if s + 2 < Q * G:
                        diff(t, s + 2)
                    else:
                        in_block(t, ("z", s + 2 - Q * G), s + 2 - Q * G)
                    mix(t, s)
                    if g == 1:
                        chunk_decay(t, q, 1)
                        c_times_b(t, q, 1)
                    if g == 2:
                        states(t, q)
                    if q + 1 < Q:
                        if g in (2, 4, 6):
                            x_tokens(t, q + 1, g // 2 - 1)
                        if g == 5:
                            b_tokens(t, q + 1)
                            chunk_decay(t, q + 1, 0)
                            c_times_b(t, q + 1, 0)
                        if g == 7:
                            x_tokens(t, q + 1, 3)

                def square_sum(g):
                    pe.wait_ge(s_pair.sem, s_pair.at(t, g))
                    if g % GH == 0:
                        pe.wait_ge(s_m.sem, s_m.at(t, Q * G - 1))
                    for q in range(Q):
                        k = q * GH + g % GH
                        last = mm(acc_bank[g // GH][:, k:k + 1], sq[g % 2][:, span(q)], one[:, 0:1], start=True, stop=True,
                                  skip_group_check=True)
                    last.then_inc(s_gs.sem, 1)

                def turn_roots(k):
                    pe.wait_ge(s_pow.sem, s_pow.at(t, f"g{k}"))
                    b = d_slot(t, f"rt{k}")
                    for q in range(Q):
                        last = nc.tensor.transpose(b[0:GH, span(q)], gv[:, q * GH:(q + 1) * GH], ident)
                    last.then_inc(d_full.sem, 1)

                def spread_norm(g):
                    if g % GH == 0:
                        pe.wait_ge(s_rp.sem, s_rp.at(t, g // GH))
                    b = d_slot(t, ("rb", g))
                    mm(b[:, :], sel[0:96, g % GH:g % GH + 1].broadcast_to([96, P]), rstdb[g // GH][:, :], start=True,
                       stop=True).then_inc(d_full.sem, 1)

                for n in range(2, NX):
                    in_block(t, ("z", n), n)
                    if n % 2 == 1:
                        square_sum((n - 3) // 2)
                turn_roots(0)
                prep_tokens(t, t + 1)
                spread_norm(0)
                square_sum(G - 1)
                prep_small(t)
                spread_norm(1)
                pe.wait_ge(s_gv.sem, s_gv.at(t, 1))
                for n in range(NX):
                    pe.wait_ge(s_yh.sem, s_yh.at(t, n))
                    pe.wait_ge(s_yl.sem, s_yl.at(t, n))
                    for c in range(KC):
                        cols = slice(c * P, (c + 1) * P)
                        last = pairs(acc_bank[c][:, :], wo_h[:, n, cols], wo_l[:, n, cols], yh[n % NY], yl[n % NY],
                                     start=n == 0, stop=n == NX - 1)
                    last.then_inc(s_wo.sem, 1)
                    if n == 1:
                        turn_roots(1)
                    if n % 2 == 1 and n // 2 + 2 < G:
                        spread_norm(n // 2 + 2)
                blocks_ahead(t)
                pe.wait_ge(s_out_t.sem, s_out_t.at(t, "out"))
                for j in range(2):
                    b = d_slot(t, f"ot{j}")
                    for k in range(2):
                        for c in range(KC):
                            last = nc.tensor.transpose(b[:, k * D + c * P:k * D + (c + 1) * P],
                                                       out_t[:, c, span(2 * j + k)], ident)
                    last.then_inc(d_full.sem, 1)

        @block.scalar
        def _(act):
            fn = nc.scalar.activation
            for j, raw, hi in ((0, raw_in, win_h[:, :, :].rearrange("p c n -> p (c n)")),
                               (1, raw_gu, gu_h[:, :, :, :].rearrange("p c j n -> p (c j n)")),
                               (2, raw_out, wo_h[:, :, :].rearrange("p n d -> p (n d)"))):
                act.wait_ge(s_up, j + 1)
                n = raw.shape[1] // 4
                for i in range(4):
                    fn(hi[:, i * n:(i + 1) * n], raw[:, i * n:(i + 1) * n], ACT.Copy,
                       scale=up_s[:, j:j + 1]).then_inc(s_hi, 1)
                if j == 0:
                    act.wait_ge(s_alog, 1)
                    fn(neg_a[:, :], row[:, 3, :], ACT.Exp).then_inc(a_done.sem, 1)

            def prep_high(t):
                for c in range(KC):
                    act.wait_ge(d_done.sem, d_done.at(t, f"xn{c}"))
                    fn(xh[:, c, :], x32[:, c, :], ACT.Copy).then_inc(s_xh.sem, 1)

            def prep(k):
                act.wait_ge(s_exi, k + 1)
                fn(ex[:, :, :], exi[:, :, :], ACT.Exp).then_inc(s_ex, 1)

            prep_high(None)
            prep(0)
            with act.Fori(0, TILES) as t:
                def conv_silu(n):
                    if n == NCONV - 1:
                        act.wait_ge(s_crow, 16 * (t + 1))
                    act.wait_ge(s_conv.sem, s_conv.at(t, n))
                    fn(xbc[:, CONV_ORDER[n], :], acc[n % 3], ACT.Silu).then_inc(s_silu.sem, 1)

                for n in range(STEPS):
                    if n < NCONV:
                        k = NX + CONV_ORDER[n]
                        act.wait_ge(a_full.sem, a_full.at(made_in(t, n), ("u", n)))
                        if n >= 3:
                            act.wait_ge(s_conv.sem, s_conv.at(t, n - 3))
                            act.wait_ge(s_hist.sem, s_hist.at(t, ("hist", n - 3)))
                        fn(u[n % 3][:, TAPS - 1:UW], a_bank[a_full.pos[("u", n)] % RA][:, :], ACT.Identity,
                           bias=ev_bias[:, k:k + 1], scale=ev_scale[:, k:k + 1]).then_inc(a_done.sem, 1)
                    if n >= 2:
                        conv_silu(n - 2)
                    if n == 7:
                        act.wait_ge(d_done.sem, d_done.at(t, "suffix"))
                        fn(w_end[:, :, :], tmp[:, :, :], ACT.Exp).then_inc(s_wend, 1)
                    if n >= FFN_LAG:
                        f = n - FFN_LAG
                        m = rows_of(f)
                        act.wait_ge(a_full.sem, a_full.at(t, ("gate", f)))
                        if f >= 2:
                            act.wait_ge(d_done.sem, d_done.at(t, ("up", f - 2)))
                        fn(gact[f % 2][0:m, :], a_bank[a_full.pos[("gate", f)] % RA][0:m, :], ACT.Silu,
                           scale=down_s[0:m, 1:2]).then_inc(a_done.sem, 1)
                assert STEPS == NCONV + 2
                def decay(q, b):
                    act.wait_ge(a_full.sem, a_full.at(t, ("E", q, b)))
                    if q == 0 and b == 0:
                        act.wait_ge(s_hist.sem, s_hist.at(t, ("hist", NCONV - 1)))
                    if q:
                        act.wait_ge(s_cs.sem, s_cs.at(t, (q - 1, b)))
                        act.wait_ge(d_done.sem, d_done.at(t, ("st", q - 1)))
                    fn(eb[:, 4 * b:4 * b + 4, :], a_bank[a_full.pos[("E", q, b)] % RA][:, :], ACT.Exp).then_inc(a_done.sem, 1)

                def decays(s):
                    act.wait_ge(a_full.sem, a_full.at(t, ("diff", s)))
                    if s >= 2:
                        act.wait_ge(s_m.sem, s_m.at(t, s - 2))
                    elif s == 0:
                        act.wait_ge(d_done.sem, d_done.at(t, ("up", NF - 1)))
                    fn(lb[s % 2], a_bank[a_full.pos[("diff", s)] % RA][:, :], ACT.Exp).then_inc(a_done.sem, 1)

                def gate(n):
                    act.wait_ge(a_full.sem, a_full.at(t, ("z", n)))
                    if n >= 2:
                        act.wait_ge(s_y.sem, s_y.at(t, n - 2))
                    fn(sz[n % 2], a_bank[a_full.pos[("z", n)] % RA][:, :], ACT.Silu, bias=ev_bias[:, n:n + 1],
                       scale=ev_scale[:, n:n + 1]).then_inc(a_done.sem, 1)

                decay(0, 0)
                decays(0)
                decays(1)
                for s in range(Q * G):
                    q, g = divmod(s, G)
                    if s + 2 < Q * G:
                        decays(s + 2)
                    else:
                        gate(s + 2 - Q * G)
                    if g == 1:
                        decay(q, 1)
                    if q + 1 < Q and g == 5:
                        decay(q + 1, 0)
                def square(n):
                    act.wait_ge(s_y.sem, s_y.at(t, n))
                    if n % 2 == 0:
                        if n >= 4:
                            act.wait_ge(s_gs.sem, s_gs.at(t, n // 2 - 2))
                    elif n >= 3:
                        act.wait_ge(s_pair.sem, s_pair.at(t, n // 2 - 1))
                    fn(sq_odd if n % 2 else sq[n // 2 % 2], xbc[:, n, :], ACT.Square).then_inc(s_sq.sem, 1)

                act.wait_ge(s_cs.sem, s_cs.at(t, (Q - 1, 1)))
                square(0)
                for n in range(2, NX):
                    gate(n)
                    square(n - 1)
                square(NX - 1)
                for n in range(NX):
                    if n == 2:
                        prep_high(t)
                        prep(t + 1)
                    if n % 2 == 0:
                        act.wait_ge(s_yn.sem, s_yn.at(t, n))
                    else:
                        act.wait_ge(d_done.sem, d_done.at(t, ("rb", n // 2)))
                    if n >= NY:
                        act.wait_ge(s_wo.sem, s_wo.at(t, n - NY))
                    fn(yh[n % NY], xbc[:, n, :], ACT.Copy).then_inc(s_yh.sem, 1)

        @block.gpsimd
        def _(pool):
            gp = nc.gpsimd
            gp.memset(half[:, :], -0.5)
            gp.memset(one[:, :], 1.0)
            gp.memset(keep_p[:, :], 0.0)
            gp.memset(hist[:, :, :], 0.0).then_inc(s_hist.sem, 1)
            gp.memset(sc[:, :, :], 0.0)
            for split in (cmbb, cumb):
                gp.memset(split[:, :], 0.0)
            gp.memset(w_end[:, :, :], 0.0).then_inc(s_zero, 1)
            for j in range(3):
                pool.wait_ge(s_mag, j + 1)
                gp.partition_all_reduce(gmax[:, j:j + 1], amax[:, j:j + 1], P, ABSMAX).then_inc(s_gmax, 1)
            pool.wait_ge(s_lo, 8)
            pool.wait_ge(s_hi, 8)
            gp.memset(sbd, 0.0).then_inc(s_sbd.sem, 1)

            def prep(t, k):
                pool.wait_ge(s_var, k + 1)
                gp.tensor_tensor(rstd[:, :], veps[:, :], half[:, 0:1].broadcast_to([P, Q]), ALU.pow).then_inc(s_pow.sem, 1)

            def prep_low(t):
                for c in range(KC):
                    pool.wait_ge(s_xh.sem, s_xh.at(t, c))
                    gp.tensor_tensor(xl[:, c, :], x32[:, c, :], xh[:, c, :], ALU.subtract).then_inc(s_xl.sem, 1)

            prep(None, 0)
            prep_low(None)
            with pool.Fori(0, TILES) as t:
                for n in range(NCONV + 1):
                    if n < NCONV:
                        if n >= 3:
                            pool.wait_ge(s_conv.sem, s_conv.at(t, n - 3))
                        elif n == 0:
                            pool.wait_ge(s_hist.sem, s_hist.n0 + s_hist.n * t)
                            pool.wait_ge(s_zero, t + 1)
                        gp.tensor_tensor(u[n % 3][:, 0:TAPS - 1], hist[:, CONV_ORDER[n], :],
                                         keep_p[:, 0:1].broadcast_to([P, TAPS - 1]), ALU.mult).then_inc(s_u.sem, 1)
                    if n:
                        k = n - 1
                        pool.wait_ge(a_done.sem, a_done.at(made_in(t, k), ("u", k)))
                        pool.wait_ge(s_u.sem, s_u.at(t, ("pad", k)))
                        gp.tensor_tensor(hist[:, CONV_ORDER[k], :], u[k % 3][:, TT:UW],
                                         one[:, 0:1].broadcast_to([P, TAPS - 1]), ALU.mult).then_inc(s_hist.sem, 1)
                pool.wait_ge(s_u.sem, s_u.at(t, ("pad", NCONV - 1)))
                gp.tensor_tensor(keep_p[:, :], one[:, :], keep_p[:, :], ALU.subtract).then_inc(s_zero, 1)

                pool.wait_ge(s_silu.sem, s_silu.at(t, NCONV - 1))
                pool.wait_ge(s_hist.sem, s_hist.at(t, ("hist", NCONV - 1)))

                def own_rows(q, b):
                    if q:
                        pool.wait_ge(s_g.sem, s_g.at(t, (q - 1, b)))
                    gp.tensor_tensor(cm[:, 4 * b:4 * b + 4, :], xbc[:, NX + NB + b, span(q)].unsqueeze(1).broadcast_to([P, 4, P]),
                                     ownrow.unsqueeze(2).broadcast_to([P, 4, P]), ALU.mult).then_inc(s_cm.sem, 1)

                def scale_c(q, b):
                    pool.wait_ge(s_crep[b], 4 * 16 * (t * Q + q + 1))
                    pool.wait_ge(a_done.sem, a_done.at(t, ("E", q, b)))
                    v = crep[:, 4 * b:4 * b + 4, :]
                    gp.tensor_tensor(v, v, eb[:, 4 * b:4 * b + 4, :], ALU.mult).then_inc(s_cs.sem, 1)
                    pool.wait_ge(s_cs.sem, s_cs.at(t, (q, b)))

                def spread(q, b):
                    if q + 1 < Q:
                        pool.wait_ge(d_done.sem, d_done.at(t, ("st", q)))
                    else:
                        pool.wait_ge(s_carry, t + 1)
                    pool.wait_ge(d_full.sem, d_full.at(t, ("y", G * q + 4 * b + 3)))
                    gp.tensor_tensor(sbd[:, 4 * b:4 * b + 4, :].rearrange("p g (h w) -> p g h w", h=4),
                                     sc[:, 4 * b:4 * b + 4, :].unsqueeze(2).broadcast_to([P, 4, 4, HP]),
                                     ownrow.unsqueeze(1).unsqueeze(3).broadcast_to([P, 4, 4, HP]),
                                     ALU.mult).then_inc(s_sbd.sem, 1)

                own_rows(0, 0)
                own_rows(0, 1)
                scale_c(0, 0)
                scale_c(0, 1)
                for q in range(Q):
                    if q + 1 < Q:
                        own_rows(q + 1, 0)
                    spread(q, 0)
                    if q + 1 < Q:
                        scale_c(q + 1, 0)
                        own_rows(q + 1, 1)
                    spread(q, 1)
                    if q + 1 < Q:
                        scale_c(q + 1, 1)

                def add_pair(g):
                    pool.wait_ge(s_sq.sem, s_sq.at(t, 2 * g + 1))
                    gp.tensor_tensor(sq[g % 2], sq[g % 2], sq_odd, ALU.add).then_inc(s_pair.sem, 1)

                def group_roots(k):
                    pool.wait_ge(s_gv.sem, s_gv.at(t, k))
                    gp.tensor_tensor(gv[:, :], gv[:, :], half[:, 0:1].broadcast_to([P, Q * GH]), ALU.pow).then_inc(s_pow.sem, 1)

                def y_low(n):
                    pool.wait_ge(s_yh.sem, s_yh.at(t, n))
                    gp.tensor_tensor(yl[n % NY], xbc[:, n, :], yh[n % NY], ALU.subtract).then_inc(s_yl.sem, 1)

                for g in range(G):
                    add_pair(g)
                    if g == 2:
                        prep(t, t + 1)
                    if g == 5:
                        group_roots(0)
                y_low(0)
                y_low(1)
                group_roots(1)
                prep_low(t)
                for n in range(2, NX):
                    y_low(n)

        @block.vector
        def _(dve):
            v = nc.vector
            links = [0]
            base = [0]

            def link(ins):
                links[0] += 1
                ins.then_inc(s_chain, 1)
                dve.wait_ge(s_chain, base[0] + links[0])

            def magnitude(j, raw):
                v.tensor_reduce(amax[:, j:j + 1], raw, AX.X, ALU.max, apply_absolute_value=True).then_inc(s_mag, 1)

            def scale(j):
                dve.wait_ge(s_gmax, j + 1)
                g, p2, up = gmax[:, j:j + 1], pow2[:, j:j + 1], up_s[:, j:j + 1]
                link(v.tensor_scalar(g, g, 1e-30, 1e36, ALU.max, ALU.min))
                link(v.tensor_scalar(p2.bitcast(U32), g.bitcast(U32), 0x7F800000, None, ALU.bitwise_and))
                link(v.reciprocal(up, p2))
                link(v.tensor_scalar(down_s[:, j:j + 1], p2, 1.0 / UP, None, ALU.mult))
                v.tensor_scalar(up, up, UP, None, ALU.mult).then_inc(s_up, 1)

            def low(j, raw, hi, lo):
                n = raw.shape[1] // 4
                dve.wait_ge(s_up, j + 1)
                for i in range(4):
                    dve.wait_ge(s_hi, 4 * j + i + 1)
                    c = slice(i * n, (i + 1) * n)
                    v.scalar_tensor_tensor(lo[:, c], raw[:, c], up_s[:, j:j + 1], hi[:, c],
                                           ALU.mult, ALU.subtract).then_inc(s_lo, 1)

            dve.wait_ge(s_const, 6 * 16)
            v.tensor_scalar(row[:, 3, :], row[:, 3, :], A_LOG_TOP, None, ALU.min).then_inc(s_alog, 1)
            v.memset(keep_v[:, :], 1.0).then_inc(s_out_t.sem, 1)
            v.memset(carrier[:, :], 0.0).then_inc(s_out, 16)
            dve.wait_ge(s_raw[0], 4 * 16)
            magnitude(0, raw_in)
            scale(0)
            link(v.tensor_scalar(ev_scale[:, :], mup, down_s[:, 0:1], None, ALU.mult))
            link(v.tensor_tensor(ev_bias[:, :], mup, b_in, ALU.mult))
            low(0, raw_in, win_h[:, :, :].rearrange("p c n -> p (c n)"), win_l[:, :, :].rearrange("p c n -> p (c n)"))
            dve.wait_ge(a_done.sem, a_done.at(None, "a_log"))
            link(v.tensor_scalar(neg_a[:, :], neg_a[:, :], -1.0, None, ALU.mult))
            dve.wait_ge(s_raw[1], 4 * 16)
            magnitude(1, raw_gu)
            scale(1)
            low(1, raw_gu, gu_h[:, :, :, :].rearrange("p c j n -> p (c j n)"),
                gu_l[:, :, :, :].rearrange("p c j n -> p (c j n)"))
            dve.wait_ge(s_raw[2], 16)
            for n in range(NX):
                c = slice(n * D, (n + 1) * D)
                ins = v.tensor_scalar(raw_out[:, c], raw_out[:, c], norm_w[:, n:n + 1], None, ALU.mult)
            link(ins)
            magnitude(2, raw_out)
            scale(2)
            low(2, raw_out, wo_h[:, :, :].rearrange("p n d -> p (n d)"), wo_l[:, :, :].rearrange("p n d -> p (n d)"))

            def taken(t, item):
                dve.wait_ge(d_full.sem, d_full.at(t, item))
                return d_bank[d_full.first[item] if t is None else d_full.pos[item] % RD]

            def split3(src, n, dst, done):
                link(v.tensor_copy(dst[0:n, :], src))
                ins = v.tensor_tensor(sp_r[0:n, :], src, dst[0:n, :], ALU.subtract)
                ins.then_inc(d_done.sem, 1)
                dve.wait_ge(d_done.sem, done)
                link(v.tensor_copy(sp_b[0:n, :], sp_r[0:n, :]))
                link(v.tensor_tensor(sp_r[0:n, :], sp_r[0:n, :], sp_b[0:n, :], ALU.subtract))
                v.tensor_copy(dst[32:32 + n, :], sp_b[0:n, :])
                return v.tensor_copy(dst[64:64 + n, :], sp_r[0:n, :])

            def prep_stats(k):
                dve.wait_ge(s_x, 16 * (k + 1))
                for q in range(Q):
                    ins = v.bn_stats(stat[:, q, :], xld[:, q, :])
                link(ins)
                carry_vector()
                for q in range(Q):
                    ins = v.bn_aggr(mv[:, q, :], stat[:, q, :])
                link(ins)
                v.tensor_scalar(veps[:, :], mv[:, :, 1], EPS, None, ALU.add).then_inc(s_var, 1)

            def prep_norm(t):
                dve.wait_ge(s_pow.sem, s_pow.at(t, "ln"))
                for q in range(Q):
                    ins = v.tensor_scalar(xld[:, q, :], xld[:, q, :], mv[:, q, 0:1], rstd[:, q:q + 1],
                                          ALU.subtract, ALU.mult)
                ins.then_inc(s_xn, 1)

            def prep_turned(t):
                for c in range(KC):
                    b = taken(t, f"xn{c}")
                    v.tensor_copy(x32[:, c, :], b[:, :]).then_inc(d_done.sem, 1)

            def prep_exp(t):
                w = H + E + 1
                b = taken(t, "small")[:, 0:Q * w].rearrange("p (q w) -> p q w", q=Q)
                link(v.tensor_reduce(lmax[:, :], b[:, :, H:H + E], AX.X, ALU.max))
                v.tensor_tensor(exi[:, :, H:H + E], b[:, :, H:H + E], lmax[:, :].unsqueeze(2).broadcast_to([P, Q, E]),
                                ALU.subtract)
                v.tensor_scalar(exi[:, :, w - 1], b[:, :, w - 1], -1.0, None, ALU.mult)

                def on_heads(k):
                    return row[:, k, :].unsqueeze(1).broadcast_to([P, Q, H])

                v.tensor_tensor(v_dt[:, :, :], b[:, :, 0:H], on_heads(0), ALU.add).then_inc(d_done.sem, 1)
                dve.wait_ge(d_done.sem, d_done.at(t, "small"))
                link(v.tensor_tensor(v_dt[:, :, :], v_dt[:, :, :], on_heads(1), ALU.mult))
                link(v.tensor_tensor(v_dt[:, :, :], v_dt[:, :, :], on_heads(2), ALU.add))
                v.scalar_tensor_tensor(exi[:, :, 0:H], v_dt[:, :, :], -1.0, v_dt[:, :, :], ALU.mult,
                                       ALU.min).then_inc(s_exi, 1)

            def route():
                link(v.tensor_reduce(lsum[:, :], ex[:, :, H:H + E], AX.X, ALU.add))
                link(v.reciprocal(lsum[:, :], lsum[:, :]))
                link(v.tensor_tensor(probs[:, :, :], ex[:, :, H:H + E], lsum[:, :].unsqueeze(2).broadcast_to([P, Q, E]),
                                     ALU.mult))
                other = probs[:, :, :].unsqueeze(2).broadcast_to([P, Q, E, E])
                own = probs[:, :, :].unsqueeze(3).broadcast_to([P, Q, E, E])
                link(v.tensor_tensor(big[0], other, own, ALU.is_equal))
                link(v.tensor_tensor(big[0], big[0], lower.unsqueeze(1).broadcast_to([P, Q, E, E]), ALU.mult))
                link(v.tensor_tensor(big[1], other, own, ALU.is_gt))
                link(v.tensor_tensor(big[1], big[1], big[0], ALU.add))
                link(v.tensor_reduce(rank[:, :, :], big[1], AX.X, ALU.add))
                v.scalar_tensor_tensor(cmb[:, :, 0:E], rank[:, :, :], 1.5, probs[:, :, :], ALU.is_lt, ALU.mult)
                link(v.tensor_scalar(lmax[:, :], ex[:, :, H + E], 1.0, None, ALU.add))
                v.reciprocal(cmb[:, :, E], lmax[:, :]).then_inc(s_route, 1)

            def steps():
                e = ex[:, :, 0:H]
                link(v.tensor_scalar(tmp[:, :, :], e, 2.0, None, ALU.add))
                link(v.reciprocal(tmp[:, :, :], tmp[:, :, :]))
                link(v.tensor_tensor(tmp[:, :, :], tmp[:, :, :], e, ALU.mult))
                link(v.tensor_tensor(tmp2[:, :, :], tmp[:, :, :], tmp[:, :, :], ALU.mult))
                link(v.tensor_scalar(da[:, :, :], tmp2[:, :, :], 1.0 / 15, None, ALU.mult))
                for k in (13, 11, 9, 7, 5, 3):
                    link(v.scalar_tensor_tensor(da[:, :, :], da[:, :, :], 1.0 / k, tmp2[:, :, :], ALU.add, ALU.mult))
                link(v.scalar_tensor_tensor(da[:, :, :], da[:, :, :], 1.0, tmp[:, :, :], ALU.add, ALU.mult))
                link(v.tensor_scalar(dt[:, :, :], v_dt[:, :, :], 0.0, None, ALU.max))
                link(v.scalar_tensor_tensor(dt[:, :, :], da[:, :, :], 2.0, dt[:, :, :], ALU.mult, ALU.add))
                link(v.tensor_tensor(da[:, :, :], dt[:, :, :], neg_a[:, :].unsqueeze(1).broadcast_to([P, Q, H]),
                                     ALU.mult))
                v.tensor_scalar(da[:, :, :], da[:, :, :], DECAY_FLOOR, None, ALU.max).then_inc(s_da, 1)

            prep_stats(0)
            prep_norm(None)
            prep_turned(None)
            prep_exp(None)
            dve.wait_ge(s_ex, 1)
            route()
            steps()
            dve.wait_ge(s_zero, 1)
            before = links[0]
            with dve.Fori(0, TILES) as t:
                links[0] = 0
                base[0] = before + t * V_LINKS

                def conv(n):
                    k = CONV_ORDER[n]
                    uu, a = u[n % 3], acc[n % 3]
                    w = conv_w[:, TAPS * k:TAPS * (k + 1)]
                    dve.wait_ge(a_done.sem, a_done.at(made_in(t, n), ("u", n)))
                    dve.wait_ge(s_u.sem, s_u.at(t, ("pad", n)))
                    if n >= 3:
                        dve.wait_ge(s_silu.sem, s_silu.at(t, n - 3))
                    link(v.tensor_scalar(a, uu[:, TAPS - 1:UW], w[:, TAPS - 1:TAPS], conv_b[:, k:k + 1],
                                         ALU.mult, ALU.add))
                    for j in range(TAPS - 1):
                        ins = v.scalar_tensor_tensor(a, uu[:, j:j + TT], w[:, j:j + 1], a, ALU.mult, ALU.add)
                        if j < TAPS - 2:
                            link(ins)
                    ins.then_inc(s_conv.sem, 1)

                def inner(n):
                    m = rows_of(n)
                    h = hin[n % 3][0:m, :]
                    b = taken(t, ("up", n))
                    dve.wait_ge(a_done.sem, a_done.at(t, ("gate", n)))
                    if n >= 3:
                        dve.wait_ge(s_down.sem, s_down.at(t, n - 3))
                    v.scalar_tensor_tensor(h, b[0:m, :], down_s[0:m, 1:2], gact[n % 2][0:m, :], ALU.mult,
                                           ALU.mult).then_inc(d_done.sem, 1)
                    b = taken(t, ("bc", n))
                    dve.wait_ge(d_done.sem, d_done.at(t, ("up", n)))
                    v.tensor_tensor(h, h, b[0:m, :], ALU.mult).then_inc(d_done.sem, 1)

                def steps_x(q, r):
                    b = taken(t, ("xt", q, r))
                    v.tensor_tensor(xd[:, r * TT:(r + 1) * TT].rearrange("p (h w) -> p h w", h=8),
                                    b[:, :].rearrange("p (h w) -> p h w", h=8),
                                    dt[:, q, 8 * r:8 * r + 8].unsqueeze(2).broadcast_to([P, 8, HP]),
                                    ALU.mult).then_inc(d_done.sem, 1)

                def decayed_b(q):
                    b = taken(t, ("bt", q))
                    if q == 0:
                        dve.wait_ge(s_wend, t + 1)
                    v.tensor_tensor(bp, b[:, 0:G * S].rearrange("p (g s) -> p g s", g=G).unsqueeze(2).broadcast_to([P, G, 4, S]),
                                    w_end[:, q, :].rearrange("p (g h) -> p g h", g=G).unsqueeze(3).broadcast_to([P, G, 4, S]),
                                    ALU.mult).then_inc(d_done.sem, 1)

                for n in range(STEPS):
                    if n < NCONV:
                        conv(n)
                    if n == 3:
                        split3(taken(t, "comb")[0:E + 1, :], E + 1, cmbb, d_done.at(t, "comb")).then_inc(s_split.sem, 1)
                    if n == 4:
                        split3(taken(t, "cum")[0:H, :], H, cumb, d_done.at(t, "cum")).then_inc(s_split.sem, 1)
                        b = taken(t, "suffix")
                        v.tensor_copy(tmp[:, :, :], b[:, 0:Q * H]).then_inc(d_done.sem, 1)
                    if n >= FFN_LAG:
                        inner(n - FFN_LAG)
                    if n == STEPS - 2:
                        dve.wait_ge(s_out, 16 * (t + 1))
                        steps_x(0, 0)
                        steps_x(0, 1)
                        decayed_b(0)
                    if n == STEPS - 1:
                        steps_x(0, 2)
                        steps_x(0, 3)
                dve.wait_ge(s_down.sem, s_down.at(t, NF - 1))
                for c in range(KC):
                    ins = v.tensor_scalar(out_t[:, c, :], acc_bank[c][:, :], b_out[:, c:c + 1], None, ALU.add)
                ins.then_inc(s_ffn, 1)

                def new_states(q):
                    dve.wait_ge(a_done.sem, a_done.at(t, ("E", q, 1)))
                    if q:
                        dve.wait_ge(s_sbd.sem, s_sbd.at(t, (q - 1, 1)))
                    else:
                        dve.wait_ge(s_sbd.sem, s_sbd.n0 + t * s_sbd.n)
                    link(v.tensor_tensor(sc[:, :, :], sc[:, :, :], eb[:, :, P - 1:P].broadcast_to([P, G, HP]), ALU.mult))
                    b = taken(t, ("st", q))
                    v.tensor_tensor(sc[:, :, :], sc[:, :, :], b[:, :].rearrange("p (g w) -> p g w", g=G),
                                    ALU.add).then_inc(d_done.sem, 1)
                    if q == Q - 1:
                        dve.wait_ge(d_done.sem, d_done.at(t, ("st", q)))
                        v.tensor_scalar(sc[:, :, :], sc[:, :, :], keep_v[:, 0:1], None, ALU.mult).then_inc(s_carry, 1)
                        dve.wait_ge(s_carry, t + 1)
                        link(v.tensor_scalar(keep_v[:, :], keep_v[:, :], -1.0, 1.0, ALU.mult, ALU.add))

                def weigh(s):
                    q, g = divmod(s, G)
                    dve.wait_ge(a_done.sem, a_done.at(t, ("diff", s)))
                    dve.wait_ge(s_g.sem, s_g.at(t, (q, g // 4)))
                    if s >= 2:
                        dve.wait_ge(d_full.sem, d_full.at(t, ("y", s - 2)))
                    k = g % 4
                    v.tensor_tensor(mb[s % 2].rearrange("p (h i) -> p h i", h=4),
                                    lb[s % 2].rearrange("p (h i) -> p h i", h=4),
                                    acc_bank[g // 4][:, span(k)].unsqueeze(1).broadcast_to([P, 4, P]),
                                    ALU.mult).then_inc(s_m.sem, 1)

                def take_y(s):
                    q, g = divmod(s, G)
                    b = taken(t, ("y", s))
                    for k in range(2):
                        xx = xbc[:, 2 * g + k, span(q)]
                        ins = v.scalar_tensor_tensor(xx, xx, d_par[:, 2 * g + k:2 * g + k + 1], b[:, span(k)],
                                                     ALU.mult, ALU.add)
                    ins.then_inc(d_done.sem, 1)

                weigh(0)
                weigh(1)
                for s in range(Q * G):
                    q, g = divmod(s, G)
                    take_y(s)
                    if s + 2 < Q * G:
                        weigh(s + 2)
                    if g == 2:
                        new_states(q)
                    if q + 1 < Q:
                        if g in (2, 4, 6):
                            steps_x(q + 1, g // 2 - 1)
                        if g == 5:
                            decayed_b(q + 1)
                        if g == 7:
                            steps_x(q + 1, 3)

                def group_squares(k):
                    dve.wait_ge(s_gs.sem, s_gs.at(t, GH * k + GH - 1))
                    v.tensor_scalar(gv[:, :], acc_bank[k][:, 0:Q * GH], float(G) / DS, EPS, ALU.mult, ALU.add).then_inc(s_gv.sem, 1)

                def split_roots(k):
                    item = f"rt{k}"
                    split3(taken(t, item)[0:GH, :], GH, rstdb[k], d_done.at(t, item)).then_inc(s_rp.sem, 1)

                def normalise(n):
                    b = taken(t, ("rb", n // 2))
                    ins = v.tensor_tensor(xbc[:, n, :], xbc[:, n, :], b[:, :], ALU.mult)
                    ins.then_inc(s_yn.sem if n % 2 == 0 else d_done.sem, 1)

                dve.wait_ge(d_done.sem, d_done.at(t, ("y", Q * G - 1)))
                for n in range(NX):
                    dve.wait_ge(a_done.sem, a_done.at(t, ("z", n)))
                    v.tensor_tensor(xbc[:, n, :], xbc[:, n, :], sz[n % 2], ALU.mult).then_inc(s_y.sem, 1)
                    if n == 4:
                        prep_stats(t + 1)
                    if n == 8:
                        prep_norm(t)
                    if n == 11:
                        group_squares(0)
                split_roots(0)
                prep_turned(t)
                for n in range(NX):
                    normalise(n)
                    if n == 1:
                        group_squares(1)
                        prep_exp(t)
                    if n == 3:
                        split_roots(1)
                    if n == 5:
                        dve.wait_ge(s_ex, t + 2)
                        route()
                    if n == 9:
                        steps()
                dve.wait_ge(s_wo.sem, s_wo.at(t, NX - 1))
                for c in range(KC):
                    ins = v.scalar_tensor_tensor(out_t[:, c, :], acc_bank[c][:, :], down_s[:, 2:3], out_t[:, c, :],
                                                 ALU.mult, ALU.add)
                ins.then_inc(s_out_t.sem, 1)
                dve.wait_ge(s_xres, 16 * (t + 1))
                for j in range(2):
                    b = taken(t, f"ot{j}")
                    res = xres[:, 2 * j:2 * j + 2, :]
                    v.tensor_tensor(res, res, b[:, :].rearrange("p (q d) -> p q d", q=2), ALU.add).then_inc(d_done.sem, 1)
                assert links[0] == V_LINKS, links[0]


def kernel(L0_attn_hidden_states, L0_attn_W_in, L0_attn_b_in, L0_attn_conv_w, L0_attn_conv_b, L0_attn_A_log,
           L0_attn_D_param, L0_attn_dt_bias, L0_attn_norm_w, L0_attn_W_out, L0_attn_b_out, L0_attn_mup_vector,
           L0_ffn_W_router, L0_ffn_W_sgate, L0_ffn_Ws_gate_up, L0_ffn_Ws_down, L0_ffn_We_gate_up, L0_ffn_We_down):
    import numpy as np
    import concourse.bacc as bacc
    from concourse.bass_utils import run_bass_kernel_spmd

    f = np.float32

    def on_p(a):
        a = np.asarray(a)
        return a.reshape((-1, P) + a.shape[1:]).swapaxes(0, 1)

    def flat(a):
        return np.ascontiguousarray(a.reshape(P, -1))

    x = np.asarray(L0_attn_hidden_states)
    shape = x.shape
    x = x.reshape(TILES, Q, P, D).transpose(0, 2, 1, 3)
    x = np.ascontiguousarray(np.concatenate([x, x[:1]]))
    w_in = np.asarray(L0_attn_W_in)
    wide = 2 * DS + 2 * G * S
    mup, b_in = np.asarray(L0_attn_mup_vector), np.asarray(L0_attn_b_in)
    w_small = np.concatenate([w_in[:, wide:], np.asarray(L0_ffn_W_router).T, np.asarray(L0_ffn_W_sgate).T], axis=1)
    gu_s, gu_e = np.asarray(L0_ffn_Ws_gate_up), np.asarray(L0_ffn_We_gate_up)

    main = I_MOE - TAIL

    def inner(k):
        experts = [gu_e[e][:, k * I_MOE:(k + 1) * I_MOE] for e in range(E)]
        return np.concatenate([gu_s[:, k * I_SH:(k + 1) * I_SH]] + [w[:, :main] for w in experts]
                              + [w[:, main:] for w in experts], axis=1)

    w_gu = np.stack([inner(0), inner(1)], axis=1)
    down_e = np.asarray(L0_ffn_We_down)
    down = np.concatenate([np.asarray(L0_ffn_Ws_down), down_e[:, :main].reshape(-1, D), down_e[:, main:].reshape(-1, D),
                           np.zeros((NF * P - FI, D), f)])
    par = np.concatenate([flat(on_p(mup[:wide])), flat(on_p(b_in[:wide])), flat(on_p(L0_attn_conv_w)),
                          flat(on_p(L0_attn_conv_b)), flat(on_p(np.repeat(np.asarray(L0_attn_D_param), HP))),
                          flat(on_p(L0_attn_norm_w)), flat(on_p(L0_attn_b_out))], axis=1)
    rows = np.stack([b_in[wide:], mup[wide:], np.asarray(L0_attn_dt_bias), np.asarray(L0_attn_A_log)])
    rows = np.ascontiguousarray(np.broadcast_to(rows, (P,) + rows.shape))

    i = np.arange(P)
    lower = np.broadcast_to(np.tril(np.ones((E, E)), -1), (P, E, E)).reshape(P, -1)
    constf = np.concatenate([np.eye(P), i[:, None] <= i, i[:, None] > i, i[:, None] // S == np.arange(4), lower], axis=1).astype(f)
    sel = (i[:, None] % H == np.arange(H)) & (i[:, None] < 3 * H)
    tail = (i[:, None] % 32 == i // TAIL) & (i[:, None] < 96)
    constb = np.concatenate([np.eye(P), np.where(i[:, None] > i, -32768.0, 0.0), sel, -1.0 * sel, tail], axis=1)
    constb = np.ascontiguousarray(constb.astype(f).view(np.uint32) >> 16).astype(np.uint16)

    arrays = {"x": x, "w_in": flat(on_p(w_in[:, :wide])), "w_small": np.ascontiguousarray(on_p(w_small)),
              "w_gu": flat(on_p(w_gu)), "w_out": flat(on_p(L0_attn_W_out)), "w_down": np.ascontiguousarray(on_p(down)),
              "par": np.ascontiguousarray(par), "rows": rows, "constf": constf, "constb": constb}
    nc = bacc.Bacc("TRN2", target_bir_lowering=False, num_devices=1)
    args = [nc.dram_tensor(k, a.shape, mybir.dt.from_np(a.dtype), kind="ExternalInput").ap() for k, a in arrays.items()]
    out = nc.dram_tensor("out", (TILES, P, Q, D), F32, kind="ExternalOutput").ap()
    c_rows = nc.dram_tensor("c_rows", (NB, P, TT), F32, kind="Internal").ap()
    layer_program(nc, *args, c_rows, out)
    r = run_bass_kernel_spmd(nc, [arrays], core_ids=[0])
    return r.results[0]["out"].transpose(0, 2, 1, 3).reshape(shape)
```

```python
from contextlib import ExitStack

import concourse.bass as bass
from concourse import mybir

ALU = mybir.AluOpType
ACT = mybir.ActivationFunctionType
AX = mybir.AxisListType
F32 = mybir.dt.float32
F16 = mybir.dt.float16
BF16 = mybir.dt.bfloat16
U32 = mybir.dt.uint32
ABSMAX = bass.bass_isa.ReduceOp.absmax

P = 128
D = 256
KC = D // P
TT = 512
Q = TT // P
H, HP, G, S = 32, 64, 8, 32
DS = H * HP
GH = G // 2
NX = DS // P
NB = G * S // P
NCONV = NX + 2 * NB
TAPS = 4
E = 8
I_SH, I_MOE = 704, 176
FI = I_SH + E * I_MOE
NF = -(-FI // P)
TAIL = I_MOE % 32
PARTS = [E] * (I_SH // 32) + [e for e in range(E) for _ in range(I_MOE // 32)] + [E + 1 + i for i in range(E * TAIL // 32)]
EPS = 1e-5
DECAY_FLOOR = -104.0
A_LOG_TOP = 80.0
UP = 256.0
RA = RD = 3

CONV_ORDER = [NX, NX + 1, NX + 2, NX + 3] + list(range(NX))
NY = 3
AHEAD = 2
SUM_AFTER = {6: 0, 7: 1, 8: 2, 9: 3, 13: 4}
STATS_AT, NORM_AT, TURN_AT, SMALL_AT, ROUTE_AT, STEPS_AT = 4, 9, 11, 14, 17, 28
ROUTE_CHUNK_AT = {19: 0, 24: 1, 25: 2, 27: 3}
TILES = 8
V_LINKS = 125


class Signal:

    def __init__(self, sem, names, first=()):
        self.sem, self.n, self.n0 = sem, len(names), len(first)
        self.pos = {name: i for i, name in enumerate(names)}
        self.first = {name: i for i, name in enumerate(first)}
        assert len(self.pos) == len(names)

    def at(self, t, name):
        if t is None:
            return self.first[name] + 1
        return self.n0 + t * self.n + self.pos[name] + 1

    def before(self, t, name, k):
        i = self.pos[name]
        return self.n0 + t * self.n + i - k + 1


def conv_blocks(k):
    def upto(k):
        return min(NCONV, AHEAD + 1 + -(-k * (NCONV - AHEAD - 1) // (NF - 3)))
    return range(upto(k - 1) if k else 0, upto(k))


def ring_a():
    out = []
    for k in range(NF):
        out += [("u", n) for n in conv_blocks(k) if n >= AHEAD] + [("gate", k)]
    out += [("E", 0, 0), ("diff", 0), ("diff", 1)]
    for s in range(Q * G):
        q, g = divmod(s, G)
        if s + 2 < Q * G:
            out.append(("diff", s + 2))
        else:
            out.append(("z", s + 2 - Q * G))
        if g == 1:
            out.append(("E", q, 1))
        if q + 1 < Q and g == 5:
            out.append(("E", q + 1, 0))
    return out + [("z", n) for n in range(2, NX)] + [("u", n) for n in range(AHEAD)]


def ring_d():
    out = []
    for n in range(NF):
        out += [("up", n), ("bc", n)]
        out += {NF - 2: [("xt", 0, 0), ("xt", 0, 1), ("bt", 0)], NF - 1: [("xt", 0, 2), ("xt", 0, 3)]}.get(n, [])
    for s in range(Q * G):
        q, g = divmod(s, G)
        out.append(("y", s))
        if g == 2:
            out.append(("st", q))
        if q + 1 < Q:
            out += {2: [("xt", q + 1, 0)], 4: [("xt", q + 1, 1)], 5: [("bt", q + 1)], 6: [("xt", q + 1, 2)],
                    7: [("xt", q + 1, 3)]}.get(g, [])
        out += {TURN_AT: ["xn0", "xn1"], SMALL_AT: ["small"]}.get(s, [])
    return (out + ["rt0"] + [("rb", g) for g in range(GH)] + ["rt1"] + [("rb", g) for g in range(GH, G)]
            + ["comb", "cum", "suffix", "ot0", "ot1"])


def layer_program(nc, x, w_in, w_small, w_gu, w_out, w_down, par, rows, constf, constb, c_rows, out):
    ctx = ExitStack()
    with ctx:
        def sb(name, shape, dt):
            return ctx.enter_context(nc.sbuf_tensor(name, shape, dt))

        def sem(name):
            return ctx.enter_context(nc.semaphore(name))

        win_h = sb("win_h", [P, KC, 2 * DS + 2 * G * S], F16)
        win_l = sb("win_l", [P, KC, 2 * DS + 2 * G * S], F16)
        gu_h = sb("gu_h", [P, KC, 2, FI], F16)
        gu_l = sb("gu_l", [P, KC, 2, FI], F16)
        wo_h = sb("wo_h", [P, NX, D], F16)
        wo_l = sb("wo_l", [P, NX, D], F16)
        wd = sb("wd", [P, NF, D], F32)
        wsm = sb("wsm", [P, KC, H + E + 1], F32)
        NIN = 2 * NX + 2 * NB
        parm = sb("parm", [P, par.shape[1]], F32)
        o = 0
        views = []
        for n in (NIN, NIN, NCONV * TAPS, NCONV, NX, NX, KC):
            views.append(parm[:, o:o + n])
            o += n
        mup, b_in, conv_w, conv_b, d_par, norm_w, b_out = views
        row = sb("row", [P, 4, H], F32)
        cf = sb("cf", [P, constf.shape[1]], F32)
        ident, tri_u, tri_s = cf[:, 0:P], cf[:, P:2 * P], cf[:, 2 * P:3 * P]
        o = 3 * P
        ownrow = cf[:, o:o + 4]
        lower = cf[:, o + 4:o + 4 + E * E].rearrange("p (a b) -> p a b", b=E)
        cb = sb("cb", [P, constb.shape[1]], BF16)
        identb, maskneg = cb[:, 0:P], cb[:, P:2 * P]
        sel, seltail = cb[:, 2 * P:2 * P + H], cb[:, 2 * P + H:3 * P + H]
        ev_scale = sb("ev_scale", [P, NIN], F32)
        ev_bias = sb("ev_bias", [P, NIN], F32)
        carrier = sb("carrier", [P, 1], F32)
        one = sb("one", [P, 1], F32)
        amax = sb("amax", [P, 3], F32)
        amax_q = sb("amax_q", [P, 4], F32)
        gmax = sb("gmax", [P, 3], F32)
        pow2 = sb("pow2", [P, 3], F32)
        up_s = sb("up_s", [P, 3], F32)
        down_s = sb("down_s", [P, 3], F32)
        neg_a = sb("neg_a", [P, H], F32)
        half = sb("half", [P, 1], F32)
        gv = sb("gv", [P, Q * GH], F32)
        keep_v = sb("keep_v", [P, 1], F32)
        keep_p = sb("keep_p", [P, 1], F32)

        xbc = sb("xbc", [P, NCONV, TT], F32)
        xh = sb("xh", [P, KC, TT], F16)
        xl = sb("xl", [P, KC, TT], F16)
        out_t = sb("out_t", [P, KC, TT], F32)
        hist = sb("hist", [P, NCONV, TAPS - 1], F32)
        sc = sb("sc", [P, G, HP], F32)
        v_dt = sb("v_dt", [P, Q, H], F32)
        ex = sb("ex", [P, Q, H + E + 1], F32)
        exi = sb("exi", [P, Q, H + E + 1], F32)
        exi_flat = exi[:, :, :].rearrange("p q w -> p (q w)")
        big = [exi_flat[:, k * E * E:(k + 1) * E * E].rearrange("p (a b) -> p a b", a=E) for k in range(2)]
        rank = exi_flat[:, 2 * E * E:2 * E * E + E]
        dt = sb("dt", [P, Q, H], F32)
        da = sb("da", [P, Q, H], F32)
        tmp = sb("tmp", [P, Q, H], F32)
        w_end = sb("w_end", [P, Q, H], F32)
        probs = sb("probs", [P, Q, E], F32)
        cmb = sb("cmb", [P, Q, E + 1], F32)
        cmbb = sb("cmbb", [96, TT], BF16)
        cumb = sb("cumb", [96, TT], BF16)
        stat = sb("stat", [P, Q, 6], F32)
        mv = sb("mv", [P, Q, 2], F32)
        rstd = sb("rstd", [P, Q], F32)
        veps = sb("veps", [P, Q], F32)
        lmax = sb("lmax", [P, Q], F32)
        lsum = sb("lsum", [P, Q], F32)
        UW = TT + TAPS - 1
        ARENA = G * 4 * HP + 3 * (UW + 1) + 9 * TT + 2 * DS - DS // 2
        arena = sb("arena", [P, ARENA], F32)
        sbd = arena[:, 0:G * 4 * HP].rearrange("p (g c) -> p g c", g=G)
        at = [G * 4 * HP]

        def carve(n):
            at[0] += n
            assert at[0] <= ARENA
            return arena[:, at[0] - n:at[0]]

        u = [carve(UW + 1)[:, 0:UW] for _ in range(3)]
        acc = [carve(TT) for _ in range(3)]
        top = at[0]
        gact = [carve(TT) for _ in range(2)]
        low_hin = at[0]
        hin = [carve(TT) for _ in range(3)]
        at[0] = low_hin + 2 * TT
        xld_flat = carve(Q * D)
        xld = xld_flat.rearrange("p (q d) -> p q d", q=Q)
        x32 = xld_flat.rearrange("p (c t) -> p c t", c=KC)
        high = at[0]
        at[0] = low_hin
        sp_r = carve(TT)[0:32, :]
        sp_b = carve(TT // 2)[0:32, :].bitcast(BF16)
        at[0] = G * 4 * HP
        cm = carve(G * P).rearrange("p (g i) -> p g i", g=G)
        eb = carve(G * P).rearrange("p (g i) -> p g i", g=G)
        crep = carve(G * P).rearrange("p (g i) -> p g i", g=G)
        at[0] = top
        lb = [carve(4 * P) for _ in range(2)]
        mb = [carve(4 * P) for _ in range(2)]
        at[0] = high
        bp = carve(G * 4 * S).rearrange("p (g h s) -> p g h s", g=G, h=4)
        xd = carve(DS)
        at[0] = G * 4 * HP
        sz = [carve(TT) for _ in range(2)]
        sq = [carve(TT) for _ in range(3)]
        sq_odd = [carve(TT)]
        at[0] = high
        xres = carve(Q * D).rearrange("p (q d) -> p q d", q=Q)
        yh = [carve(TT // 2).bitcast(F16) for _ in range(NY)]
        yl = [carve(TT // 2).bitcast(F16) for _ in range(NY)]
        sq_odd.append(carve(TT))
        raw_in = xbc[:, :, :].rearrange("p n t -> p (n t)")[:, 0:KC * (2 * DS + 2 * G * S)]
        raw_gu = arena[:, 0:KC * 2 * FI]
        raw_out = xbc[:, :, :].rearrange("p n t -> p (n t)")[:, 0:NX * D]

        bank = [ctx.enter_context(nc.psum_tensor(f"bank{i}", [P, TT], F32)) for i in range(8)]
        rstdb = [cmbb, cumb]
        acc_bank, a_bank, d_bank = bank[0:2], bank[2:5], bank[5:8]

        RAW, RDW = ring_a(), ring_d()
        PREP = ["xn0", "xn1", "small", "comb", "cum", "suffix"]
        assert len(RAW) % RA == 0 and len(RDW) % RD == 0 and len(PREP) % RD == 0
        s_par = sem("s_par")
        s_const = sem("s_const")
        s_quarter = [sem(f"s_quarter{i}") for i in range(4)]
        s_raw_gu = sem("s_raw_gu")
        s_raw_out = sem("s_raw_out")
        s_mag = sem("s_mag")
        s_gmax = sem("s_gmax")
        s_up = sem("s_up")
        s_hi = sem("s_hi")
        s_lo = sem("s_lo")
        s_scaled = sem("s_scaled")
        s_lo_out = sem("s_lo_out")
        s_zero = sem("s_zero")
        s_alog = sem("s_alog")
        a_full = Signal(sem("a_full"), RAW, RAW[-AHEAD:])
        a_done = Signal(sem("a_done"), RAW, ["a_log"] + RAW[-AHEAD:])
        d_full = Signal(sem("d_full"), RDW, PREP)
        d_done = Signal(sem("d_done"), RDW, PREP)
        s_chain = sem("s_chain")
        s_u = Signal(sem("s_u"), [("pad", n) for n in range(NCONV)])
        s_hist = Signal(sem("s_hist"), [("hist", n) for n in range(NCONV)], ["zero"])
        s_conv = Signal(sem("s_conv"), list(range(NCONV)))
        s_silu = Signal(sem("s_silu"), list(range(NCONV)))
        s_route = sem("s_route")
        s_da = sem("s_da")
        SPLIT = ["cmbb", "cumb", "tmp"]
        s_split = Signal(sem("s_split"), SPLIT, SPLIT)
        s_down = Signal(sem("s_down"), list(range(NF)))
        s_ffn = sem("s_ffn")
        s_wend = sem("s_wend")
        s_crow = sem("s_crow")
        s_crep = [sem(f"s_crep{b}") for b in range(2)]
        s_cm = Signal(sem("s_cm"), [(q, b) for q in range(Q) for b in range(2)])
        s_cs = Signal(sem("s_cs"), [(q, b) for q in range(Q) for b in range(2)])
        s_g = Signal(sem("s_g"), [(q, b) for q in range(Q) for b in range(2)])
        s_m = Signal(sem("s_m"), list(range(Q * G)))
        s_carry = sem("s_carry")
        s_sbd = Signal(sem("s_sbd"), [(q, b) for q in range(Q) for b in range(2)], ["zero"])
        s_y = Signal(sem("s_y"), list(range(NX)))
        SQUARED = [n for n in range(NX) if n % 2 == 0 or n > NX // 2]
        s_sq = Signal(sem("s_sq"), SQUARED)
        s_odd = Signal(sem("s_odd"), list(range(GH)))
        s_pair = Signal(sem("s_pair"), list(range(G - 1)))
        s_gs = Signal(sem("s_gs"), list(range(G)))
        s_gv = Signal(sem("s_gv"), [0, 1])
        s_x = sem("s_x")
        s_xres = sem("s_xres")
        s_var = sem("s_var")
        s_pow = Signal(sem("s_pow"), ["ln", "g0", "g1"], ["ln"])
        s_xn = sem("s_xn")
        s_xh = Signal(sem("s_xh"), [0, 1], [0, 1])
        s_xl = Signal(sem("s_xl"), [0, 1], [0, 1])
        s_exi = sem("s_exi")
        s_ex = sem("s_ex")
        s_rp = Signal(sem("s_rp"), [0, 1])
        s_yn = Signal(sem("s_yn"), list(range(0, NX, 2)))
        s_yh = Signal(sem("s_yh"), list(range(NX)))
        s_yl = Signal(sem("s_yl"), list(range(NX)))
        s_wo = Signal(sem("s_wo"), list(range(NX)))
        s_out_t = Signal(sem("s_out_t"), ["out"], ["none"])
        s_out = sem("s_out")

        block = ctx.enter_context(nc.Block())

        def rows_of(n):
            return P if n < NF - 1 else FI - (NF - 1) * P

        def made_in(t, n):
            return t - 1 if n < AHEAD else t

        def span(q):
            return slice(q * P, (q + 1) * P)

        def carry_vector():
            nc.vector.tensor_copy(carrier[:, :], keep_v[:, :])

        @block.sync
        def _(sp):
            n_in = raw_in.shape[1] // 4
            for i in range(4):
                sp.dma_start(raw_in[:, i * n_in:(i + 1) * n_in], w_in[:, i * n_in:(i + 1) * n_in]).then_inc(s_quarter[i], 16)
            sp.dma_start(parm[:, :], par).then_inc(s_par, 16)
            sp.dma_start(row[:, :, :], rows).then_inc(s_par, 16)
            n_gu = raw_gu.shape[1] // 4
            for i in range(4):
                sp.dma_start(raw_gu[:, i * n_gu:(i + 1) * n_gu], w_gu[:, i * n_gu:(i + 1) * n_gu]).then_inc(s_raw_gu, 16)
            sp.dma_start(cf[:, :], constf).then_inc(s_const, 16)
            sp.dma_start(cb[:, :], constb.bitcast(BF16)).then_inc(s_const, 16)
            sp.dma_start(wsm[:, :, :], w_small).then_inc(s_const, 16)
            sp.dma_start(wd[:, :, :], w_down).then_inc(s_const, 16)
            sp.wait_ge(s_lo, 4)
            sp.wait_ge(s_hi, 4)
            sp.dma_start(raw_out, w_out).then_inc(s_raw_out, 16)
            sp.wait_ge(s_lo, 8)
            sp.wait_ge(s_hi, 8)
            sp.dma_start(xld, x[0]).then_inc(s_x, 16)
            with sp.Fori(0, TILES) as t:
                sp.wait_ge(s_silu.sem, s_silu.at(t, 2 * NB - 1))
                sp.dma_start(c_rows.rearrange("b p t -> p b t"), xbc[:, NX + NB:NX + 2 * NB, :]).then_inc(s_crow, 16)
                sp.wait_ge(s_silu.sem, s_silu.at(t, NCONV - 1))
                for q in range(Q):
                    if q == 1:
                        sp.wait_ge(s_ffn, t + 1)
                        sp.dma_start(xld, x[t + 1]).then_inc(s_x, 16)
                    for b in range(2):
                        if q:
                            sp.wait_ge(d_full.sem, d_full.at(t, ("y", G * (q - 1) + 4 * b + 3)))
                        for h in range(4):
                            sp.dma_start(crep[S * h:S * (h + 1), 4 * b:4 * b + 4, :],
                                         c_rows[b].rearrange("(r s) t -> s r t", s=S)[:, :, span(q)]).then_inc(s_crep[b], 16)
                sp.wait_ge(d_full.sem, d_full.at(t, ("y", Q * G - 1)))
                sp.dma_start(xres, x[t]).then_inc(s_xres, 16)
                sp.wait_ge(d_done.sem, d_done.at(t, "ot1"))
                sp.dma_start(out[t], xres).then_inc(s_out, 16)
            sp.wait_ge(s_out, 16 * (TILES + 1))

        @block.tensor
        def _(pe):
            mm = nc.tensor.matmul

            def a_slot(t, item):
                if t is not None:
                    pe.wait_ge(a_done.sem, a_done.before(t, item, RA))
                return a_bank[a_done.pos[item] % RA]

            def d_slot(t, item):
                if t is None:
                    return d_bank[d_done.first[item] % RD]
                pe.wait_ge(d_done.sem, d_done.before(t, item, RD))
                return d_bank[d_done.pos[item] % RD]

            def pairs(o, wh, wl, rh, rl, start=True, stop=True):
                mm(o, wh, rh, start=start, stop=False)
                mm(o, wh, rl, start=False, stop=False)
                return mm(o, wl, rh, start=False, stop=stop)

            def project(o, wh, wl):
                for c in range(KC):
                    last = pairs(o, wh[c], wl[c], xh[:, c, :], xl[:, c, :], start=c == 0, stop=c == KC - 1)
                return last

            def in_block(t, item, k):
                cols = slice(k * P, (k + 1) * P)
                b = a_slot(t, item)
                project(b[:, :], [win_h[:, c, cols] for c in range(KC)],
                        [win_l[:, c, cols] for c in range(KC)]).then_inc(a_full.sem, 1)

            def ffn_block(t, n):
                m = rows_of(n)
                cols = slice(n * P, n * P + m)
                for j, slot, item, full in ((0, a_slot, ("gate", n), a_full), (1, d_slot, ("up", n), d_full)):
                    b = slot(t, item)
                    project(b[0:m, :], [gu_h[:, c, j, cols] for c in range(KC)],
                            [gu_l[:, c, j, cols] for c in range(KC)]).then_inc(full.sem, 1)
                b = d_slot(t, ("bc", n))
                if n == 0:
                    pe.wait_ge(s_split.sem, s_split.at(t - 1, "cmbb"))
                parts = PARTS[4 * n:4 * n + 4]
                wide = len(set(parts)) == 1
                for j, part in enumerate(parts[:1] if wide else parts):
                    if part > E:
                        pick = seltail[0:96, 32 * (part - E - 1):32 * (part - E)]
                    else:
                        pick = sel[0:96, part:part + 1].broadcast_to([96, P if wide else 32])
                    last = mm(b[:, :] if wide else b[32 * j:32 * j + 32, :], pick, cmbb[:, :], start=True, stop=True,
                              skip_group_check=True)
                last.then_inc(d_full.sem, 1)

            def ffn_down(t, n):
                m = rows_of(n)
                pe.wait_ge(d_done.sem, d_done.at(t, ("bc", n)))
                if n == 0:
                    pe.wait_ge(s_out_t.sem, t + s_out_t.n0)
                for c in range(KC):
                    last = mm(acc_bank[c][:, :], wd[0:m, n, c * P:(c + 1) * P], hin[n % 3][0:m, :],
                              start=n == 0, stop=n == NF - 1)
                last.then_inc(s_down.sem, 1)

            def prep_tokens(t, k):
                pe.wait_ge(s_xn, k + 1)
                for c in range(KC):
                    b = d_slot(t, f"xn{c}")
                    for q in range(Q):
                        last = nc.tensor.transpose(b[:, span(q)], xld[:, q, c * P:(c + 1) * P], ident)
                    last.then_inc(d_full.sem, 1)

            def prep_small(t):
                pe.wait_ge(d_done.sem, d_done.at(t, "xn1"))
                b = d_slot(t, "small")
                w = H + E + 1
                for q in range(Q):
                    for c in range(KC):
                        last = mm(b[:, q * w:(q + 1) * w], x32[:, c, span(q)], wsm[:, c, :],
                                  start=c == 0, stop=c == KC - 1)
                last.then_inc(d_full.sem, 1)

            def chunk_decay(t, q, b):
                eo = a_slot(t, ("E", q, b))
                if q == 0 and b == 0:
                    pe.wait_ge(s_split.sem, s_split.at(t - 1, "cumb"))
                for r in range(4):
                    g = 4 * b + r
                    for h in range(4):
                        e = mm(eo[S * h:S * (h + 1), span(r)], sel[0:96, 4 * g + h:4 * g + h + 1].broadcast_to([96, S]),
                               cumb[:, span(q)], start=True, stop=True, skip_group_check=True)
                e.then_inc(a_full.sem, 1)

            def c_times_b(t, q, b):
                if q == 0:
                    pe.wait_ge(s_ffn, t + 1)
                else:
                    pe.wait_ge(s_m.sem, s_m.at(t, G * (q - 1) + 4 * b + 3))
                pe.wait_ge(s_cm.sem, s_cm.at(t, (q, b)))
                for r in range(4):
                    c = mm(acc_bank[b][:, span(r)], xbc[:, NX + b, span(q)], cm[:, 4 * b + r, :], start=True, stop=True)
                c.then_inc(s_g.sem, 1)

            def diff(t, s):
                q, g = divmod(s, G)
                b = a_slot(t, ("diff", s))
                for h in range(4):
                    mm(b[:, span(h)], identb, maskneg, start=True, stop=False, skip_group_check=True)
                    last = mm(b[:, span(h)], sel[0:96, 4 * g + h:4 * g + h + 1].broadcast_to([96, P]), cumb[:, span(q)],
                              start=False, stop=True, skip_group_check=True)
                last.then_inc(a_full.sem, 1)

            def x_tokens(t, q, r):
                b = d_slot(t, ("xt", q, r))
                if q == 0:
                    pe.wait_ge(s_silu.sem, s_silu.at(t, 2 * NB + 4 * r + 3))
                for k in range(4):
                    last = nc.tensor.transpose(b[:, span(k)], xbc[:, 4 * r + k, span(q)], ident)
                last.then_inc(d_full.sem, 1)

            def b_tokens(t, q):
                b = d_slot(t, ("bt", q))
                for k in range(NB):
                    last = nc.tensor.transpose(b[:, span(k)], xbc[:, NX + k, span(q)], ident)
                last.then_inc(d_full.sem, 1)

            def states(t, q):
                b = d_slot(t, ("st", q))
                pe.wait_ge(d_done.sem, d_done.at(t, ("xt", q, 3)))
                for g in range(G):
                    for h in range(4):
                        last = mm(b[S * h:S * (h + 1), g * HP:(g + 1) * HP], bp[:, g, h, :],
                                  xd[:, (4 * g + h) * HP:(4 * g + h + 1) * HP], start=True, stop=True,
                                  skip_group_check=True)
                last.then_inc(d_full.sem, 1)

            def mix(t, s):
                q, g = divmod(s, G)
                b = d_slot(t, ("y", s))
                pe.wait_ge(s_m.sem, s_m.at(t, s))
                if g % 4 == 0:
                    pe.wait_ge(s_cs.sem, s_cs.at(t, (q, g // 4)))
                    if q:
                        pe.wait_ge(s_sbd.sem, s_sbd.at(t, (q - 1, g // 4)))
                    else:
                        pe.wait_ge(s_sbd.sem, s_sbd.n0 + t * s_sbd.n)
                for pr in range(2):
                    for e in range(2):
                        h = 2 * pr + e
                        mm(b[HP * e:HP * (e + 1), span(pr)], xd[:, (4 * g + h) * HP:(4 * g + h + 1) * HP],
                           mb[s % 2][:, span(h)], start=True, stop=False, skip_group_check=True)
                    last = mm(b[:, span(pr)], sbd[:, g, pr * P:(pr + 1) * P], crep[:, g, :],
                              start=False, stop=True, skip_group_check=True)
                last.then_inc(d_full.sem, 1)

            def blocks_ahead(t):
                pe.wait_ge(s_xh.sem, s_xh.at(t, KC - 1))
                pe.wait_ge(s_xl.sem, s_xl.at(t, KC - 1))
                for n in range(AHEAD):
                    in_block(t, ("u", n), NX + CONV_ORDER[n])

            def combination(t, k):
                pe.wait_ge(s_route, k + 1)
                b = d_slot(t, "comb")
                for q in range(Q):
                    last = nc.tensor.transpose(b[0:E + 1, span(q)], cmb[:, q, :], ident)
                last.then_inc(d_full.sem, 1)

            def decay_sums(t, k):
                pe.wait_ge(s_da, k + 1)
                b = d_slot(t, "cum")
                for q in range(Q):
                    last = mm(b[0:H, span(q)], da[:, q, :], tri_u, start=True, stop=True)
                last.then_inc(d_full.sem, 1)
                b = d_slot(t, "suffix")
                mm(b[:, 0:Q * H], tri_s, da[:, :, :], start=True, stop=True)
                mm(b[:, Q * H:2 * Q * H], tri_u, da[:, :, :], start=True, stop=True).then_inc(d_full.sem, 1)

            pe.wait_ge(s_const, 4 * 16)
            prep_tokens(None, 0)
            prep_small(None)
            blocks_ahead(None)
            combination(None, 0)
            decay_sums(None, 0)
            with pe.Fori(0, TILES) as t:
                for k in range(NF):
                    for n in conv_blocks(k):
                        if n >= AHEAD:
                            in_block(t, ("u", n), NX + CONV_ORDER[n])
                    ffn_block(t, k)
                    if k:
                        ffn_down(t, k - 1)
                    if k == NF - 2:
                        x_tokens(t, 0, 0)
                        x_tokens(t, 0, 1)
                        b_tokens(t, 0)
                    if k == NF - 1:
                        x_tokens(t, 0, 2)
                        x_tokens(t, 0, 3)
                        chunk_decay(t, 0, 0)
                        diff(t, 0)
                        diff(t, 1)
                ffn_down(t, NF - 1)
                c_times_b(t, 0, 0)
                for s in range(Q * G):
                    q, g = divmod(s, G)
                    if s + 2 < Q * G:
                        diff(t, s + 2)
                    else:
                        in_block(t, ("z", s + 2 - Q * G), s + 2 - Q * G)
                    mix(t, s)
                    if g == 1:
                        chunk_decay(t, q, 1)
                        c_times_b(t, q, 1)
                    if g == 2:
                        states(t, q)
                    if q + 1 < Q:
                        if g in (2, 4, 6):
                            x_tokens(t, q + 1, g // 2 - 1)
                        if g == 5:
                            b_tokens(t, q + 1)
                            chunk_decay(t, q + 1, 0)
                            c_times_b(t, q + 1, 0)
                        if g == 7:
                            x_tokens(t, q + 1, 3)
                    if s == TURN_AT:
                        prep_tokens(t, t + 1)
                    if s == SMALL_AT:
                        prep_small(t)

                def square_sum(g):
                    squares = [sq[g % 3]]
                    if g < G - 1:
                        pe.wait_ge(s_pair.sem, s_pair.at(t, g))
                    else:
                        pe.wait_ge(s_sq.sem, s_sq.at(t, NX - 1))
                        squares.append(sq_odd[g % 2])
                    if g % GH == 0:
                        pe.wait_ge(s_m.sem, s_m.at(t, Q * G - 1))
                    for q in range(Q):
                        k = q * GH + g % GH
                        for part in squares:
                            last = mm(acc_bank[g // GH][:, k:k + 1], part[:, span(q)], one[:, 0:1], start=part is squares[0],
                                      stop=part is squares[-1], skip_group_check=True)
                    last.then_inc(s_gs.sem, 1)

                def turn_roots(k):
                    pe.wait_ge(s_pow.sem, s_pow.at(t, f"g{k}"))
                    b = d_slot(t, f"rt{k}")
                    for q in range(Q):
                        last = nc.tensor.transpose(b[0:GH, span(q)], gv[:, q * GH:(q + 1) * GH], ident)
                    last.then_inc(d_full.sem, 1)

                def spread_norm(g):
                    if g % GH == 0:
                        pe.wait_ge(s_rp.sem, s_rp.at(t, g // GH))
                    b = d_slot(t, ("rb", g))
                    mm(b[:, :], sel[0:96, g % GH:g % GH + 1].broadcast_to([96, P]), rstdb[g // GH][:, :], start=True,
                       stop=True).then_inc(d_full.sem, 1)

                for n in range(2, NX):
                    in_block(t, ("z", n), n)
                    if n in SUM_AFTER:
                        square_sum(SUM_AFTER[n])
                    if n == 12:
                        turn_roots(0)
                spread_norm(0)
                spread_norm(1)
                square_sum(G - 3)
                square_sum(G - 2)
                square_sum(G - 1)
                pe.wait_ge(s_gv.sem, s_gv.at(t, 1))
                for n in range(NX):
                    pe.wait_ge(s_yh.sem, s_yh.at(t, n))
                    pe.wait_ge(s_yl.sem, s_yl.at(t, n))
                    for c in range(KC):
                        cols = slice(c * P, (c + 1) * P)
                        last = pairs(acc_bank[c][:, :], wo_h[:, n, cols], wo_l[:, n, cols], yh[n % NY], yl[n % NY],
                                     start=n == 0, stop=n == NX - 1)
                    last.then_inc(s_wo.sem, 1)
                    if n % 2 == 1 and n // 2 + 2 < G:
                        spread_norm(n // 2 + 2)
                    if n == 3:
                        turn_roots(1)
                    if n == NX - 3:
                        combination(t, t + 1)
                    if n == NX - 2:
                        decay_sums(t, t + 1)
                blocks_ahead(t)
                pe.wait_ge(s_out_t.sem, s_out_t.at(t, "out"))
                for j in range(2):
                    b = d_slot(t, f"ot{j}")
                    for k in range(2):
                        for c in range(KC):
                            last = nc.tensor.transpose(b[:, k * D + c * P:k * D + (c + 1) * P],
                                                       out_t[:, c, span(2 * j + k)], ident)
                    last.then_inc(d_full.sem, 1)

        @block.scalar
        def _(act):
            fn = nc.scalar.activation
            def high_parts(j, raw, hi):
                act.wait_ge(s_up, j + 1)
                n = raw.shape[1] // 4
                for i in range(4):
                    c = slice(i * n, (i + 1) * n)
                    if j == 2:
                        fn(raw[:, c], raw[:, c], ACT.Copy, scale=up_s[:, j:j + 1]).then_inc(s_scaled, 1)
                        act.wait_ge(s_scaled, i + 1)
                        fn(hi[:, c], raw[:, c], ACT.Copy).then_inc(s_hi, 1)
                    else:
                        fn(hi[:, c], raw[:, c], ACT.Copy, scale=up_s[:, j:j + 1]).then_inc(s_hi, 1)

            high_parts(0, raw_in, win_h[:, :, :].rearrange("p c n -> p (c n)"))
            act.wait_ge(s_alog, 1)
            fn(neg_a[:, :], row[:, 3, :], ACT.Exp).then_inc(a_done.sem, 1)
            high_parts(1, raw_gu, gu_h[:, :, :, :].rearrange("p c j n -> p (c j n)"))

            def prep_high(t):
                act.wait_ge(d_done.sem, d_done.at(t, "xn1"))
                for c in range(KC):
                    fn(xh[:, c, :], x32[:, c, :], ACT.Copy).then_inc(s_xh.sem, 1)

            def prep(k):
                act.wait_ge(s_exi, k + 1)
                fn(ex[:, :, :], exi[:, :, :], ACT.Exp).then_inc(s_ex, 1)

            prep_high(None)
            prep(0)
            high_parts(2, raw_out, wo_h[:, :, :].rearrange("p n d -> p (n d)"))
            with act.Fori(0, TILES) as t:
                def conv_silu(n):
                    if n == NCONV - 1:
                        act.wait_ge(s_crow, 16 * (t + 1))
                    if n == 2 * NB:
                        act.wait_ge(s_lo_out, 4)
                    act.wait_ge(s_conv.sem, s_conv.at(t, n))
                    fn(xbc[:, CONV_ORDER[n], :], acc[n % 3], ACT.Silu).then_inc(s_silu.sem, 1)

                for f in range(NF):
                    for n in conv_blocks(f):
                        k = NX + CONV_ORDER[n]
                        act.wait_ge(a_full.sem, a_full.at(made_in(t, n), ("u", n)))
                        if n >= 3:
                            act.wait_ge(s_conv.sem, s_conv.at(t, n - 3))
                            act.wait_ge(s_hist.sem, s_hist.at(t, ("hist", n - 3)))
                        fn(u[n % 3][:, TAPS - 1:UW], a_bank[a_full.pos[("u", n)] % RA][:, :], ACT.Identity,
                           bias=ev_bias[:, k:k + 1], scale=ev_scale[:, k:k + 1]).then_inc(a_done.sem, 1)
                        if n >= 2:
                            conv_silu(n - 2)
                    if f == NF - 2:
                        conv_silu(NCONV - 2)
                    if f == NF - 1:
                        conv_silu(NCONV - 1)
                    if f == 2:
                        act.wait_ge(s_split.sem, s_split.at(t - 1, "tmp"))
                        fn(w_end[:, :, :], tmp[:, :, :], ACT.Exp).then_inc(s_wend, 1)
                    m = rows_of(f)
                    act.wait_ge(a_full.sem, a_full.at(t, ("gate", f)))
                    if f >= 2:
                        act.wait_ge(d_done.sem, d_done.at(t, ("up", f - 2)))
                    fn(gact[f % 2][0:m, :], a_bank[a_full.pos[("gate", f)] % RA][0:m, :], ACT.Silu,
                       scale=down_s[0:m, 1:2]).then_inc(a_done.sem, 1)
                def decay(q, b):
                    act.wait_ge(a_full.sem, a_full.at(t, ("E", q, b)))
                    if q == 0 and b == 0:
                        act.wait_ge(s_hist.sem, s_hist.at(t, ("hist", NCONV - 1)))
                    if q:
                        act.wait_ge(s_cs.sem, s_cs.at(t, (q - 1, b)))
                        act.wait_ge(d_done.sem, d_done.at(t, ("st", q - 1)))
                    fn(eb[:, 4 * b:4 * b + 4, :], a_bank[a_full.pos[("E", q, b)] % RA][:, :], ACT.Exp).then_inc(a_done.sem, 1)

                def decays(s):
                    act.wait_ge(a_full.sem, a_full.at(t, ("diff", s)))
                    if s >= 2:
                        act.wait_ge(s_m.sem, s_m.at(t, s - 2))
                    elif s == 0:
                        act.wait_ge(d_done.sem, d_done.at(t, ("up", NF - 1)))
                    q, g = divmod(s, G)
                    b = a_bank[a_full.pos[("diff", s)] % RA]
                    for h in range(4):
                        ins = fn(lb[s % 2][:, span(h)], b[:, span(h)], ACT.Exp, bias=da[:, q, 4 * g + h:4 * g + h + 1])
                    ins.then_inc(a_done.sem, 1)

                def gate(n):
                    act.wait_ge(a_full.sem, a_full.at(t, ("z", n)))
                    if n >= 2:
                        act.wait_ge(s_y.sem, s_y.at(t, n - 2))
                    fn(sz[n % 2], a_bank[a_full.pos[("z", n)] % RA][:, :], ACT.Silu, bias=ev_bias[:, n:n + 1],
                       scale=ev_scale[:, n:n + 1]).then_inc(a_done.sem, 1)

                decay(0, 0)
                decays(0)
                decays(1)
                for s in range(Q * G):
                    q, g = divmod(s, G)
                    if s + 2 < Q * G:
                        decays(s + 2)
                    else:
                        gate(s + 2 - Q * G)
                    if g == 1:
                        decay(q, 1)
                    if q + 1 < Q and g == 5:
                        decay(q + 1, 0)
                    if s == SMALL_AT + 1:
                        prep(t + 1)
                def square(n):
                    act.wait_ge(s_y.sem, s_y.at(t, n))
                    if n % 2:
                        act.wait_ge(s_pair.sem, s_pair.at(t, n // 2 - 2))
                    elif n >= 6:
                        act.wait_ge(s_gs.sem, s_gs.at(t, n // 2 - 3))
                    fn(sq_odd[n // 2 % 2] if n % 2 else sq[n // 2 % 3], xbc[:, n, :], ACT.Square).then_inc(s_sq.sem, 1)

                act.wait_ge(s_cs.sem, s_cs.at(t, (Q - 1, 1)))
                square(0)
                for n in range(2, NX):
                    gate(n)
                    if n - 1 in SQUARED:
                        square(n - 1)
                square(NX - 1)
                for n in range(NX):
                    if n == 6:
                        prep_high(t)
                    if n % 2 == 0:
                        act.wait_ge(s_yn.sem, s_yn.at(t, n))
                    else:
                        act.wait_ge(d_done.sem, d_done.at(t, ("rb", n // 2)))
                    if n >= NY:
                        act.wait_ge(s_wo.sem, s_wo.at(t, n - NY))
                    fn(yh[n % NY], xbc[:, n, :], ACT.Copy).then_inc(s_yh.sem, 1)

        @block.gpsimd
        def _(pool):
            gp = nc.gpsimd
            gp.memset(half[:, :], -0.5)
            gp.memset(one[:, :], 1.0)
            gp.memset(keep_p[:, :], 0.0)
            gp.memset(hist[:, :, :], 0.0).then_inc(s_hist.sem, 1)
            gp.memset(sc[:, :, :], 0.0)
            for split in (cmbb, cumb):
                gp.memset(split[:, :], 0.0)
            gp.memset(w_end[:, :, :], 0.0).then_inc(s_zero, 1)

            def largest(j):
                pool.wait_ge(s_mag, j + 1)
                gp.partition_all_reduce(gmax[:, j:j + 1], amax[:, j:j + 1], P, ABSMAX).then_inc(s_gmax, 1)

            largest(0)
            largest(1)
            pool.wait_ge(s_lo, 8)
            pool.wait_ge(s_hi, 8)
            gp.memset(sbd, 0.0).then_inc(s_sbd.sem, 1)

            def prep(t, k):
                pool.wait_ge(s_var, k + 1)
                gp.tensor_tensor(rstd[:, :], veps[:, :], half[:, 0:1].broadcast_to([P, Q]), ALU.pow).then_inc(s_pow.sem, 1)

            def prep_low(t):
                for c in range(KC):
                    pool.wait_ge(s_xh.sem, s_xh.at(t, c))
                    gp.tensor_tensor(xl[:, c, :], x32[:, c, :], xh[:, c, :], ALU.subtract).then_inc(s_xl.sem, 1)

            largest(2)
            prep(None, 0)
            prep_low(None)
            n_out = raw_out.shape[1] // 4
            for i in range(4):
                c = slice(i * n_out, (i + 1) * n_out)
                pool.wait_ge(s_hi, 8 + i + 1)
                gp.tensor_tensor(wo_l[:, :, :].rearrange("p n d -> p (n d)")[:, c], raw_out[:, c],
                                 wo_h[:, :, :].rearrange("p n d -> p (n d)")[:, c], ALU.subtract).then_inc(s_lo_out, 1)
            with pool.Fori(0, TILES) as t:
                for n in range(NCONV + 1):
                    if n < NCONV:
                        if n >= 3:
                            pool.wait_ge(s_conv.sem, s_conv.at(t, n - 3))
                        elif n == 0:
                            pool.wait_ge(s_hist.sem, s_hist.n0 + s_hist.n * t)
                            pool.wait_ge(s_zero, t + 1)
                        gp.tensor_tensor(u[n % 3][:, 0:TAPS - 1], hist[:, CONV_ORDER[n], :],
                                         keep_p[:, 0:1].broadcast_to([P, TAPS - 1]), ALU.mult).then_inc(s_u.sem, 1)
                    if n:
                        k = n - 1
                        pool.wait_ge(a_done.sem, a_done.at(made_in(t, k), ("u", k)))
                        pool.wait_ge(s_u.sem, s_u.at(t, ("pad", k)))
                        gp.tensor_tensor(hist[:, CONV_ORDER[k], :], u[k % 3][:, TT:UW],
                                         one[:, 0:1].broadcast_to([P, TAPS - 1]), ALU.mult).then_inc(s_hist.sem, 1)
                pool.wait_ge(s_u.sem, s_u.at(t, ("pad", NCONV - 1)))
                gp.tensor_tensor(keep_p[:, :], one[:, :], keep_p[:, :], ALU.subtract).then_inc(s_zero, 1)

                pool.wait_ge(s_silu.sem, s_silu.at(t, NCONV - 1))
                pool.wait_ge(s_hist.sem, s_hist.at(t, ("hist", NCONV - 1)))

                def own_rows(q, b):
                    if q:
                        pool.wait_ge(s_g.sem, s_g.at(t, (q - 1, b)))
                    gp.tensor_tensor(cm[:, 4 * b:4 * b + 4, :], xbc[:, NX + NB + b, span(q)].unsqueeze(1).broadcast_to([P, 4, P]),
                                     ownrow.unsqueeze(2).broadcast_to([P, 4, P]), ALU.mult).then_inc(s_cm.sem, 1)

                def scale_c(q, b):
                    pool.wait_ge(s_crep[b], 4 * 16 * (t * Q + q + 1))
                    pool.wait_ge(a_done.sem, a_done.at(t, ("E", q, b)))
                    v = crep[:, 4 * b:4 * b + 4, :]
                    gp.tensor_tensor(v, v, eb[:, 4 * b:4 * b + 4, :], ALU.mult).then_inc(s_cs.sem, 1)
                    pool.wait_ge(s_cs.sem, s_cs.at(t, (q, b)))

                def spread(q, b):
                    if q + 1 < Q:
                        pool.wait_ge(d_done.sem, d_done.at(t, ("st", q)))
                    else:
                        pool.wait_ge(s_carry, t + 1)
                    pool.wait_ge(d_full.sem, d_full.at(t, ("y", G * q + 4 * b + 3)))
                    gp.tensor_tensor(sbd[:, 4 * b:4 * b + 4, :].rearrange("p g (h w) -> p g h w", h=4),
                                     sc[:, 4 * b:4 * b + 4, :].unsqueeze(2).broadcast_to([P, 4, 4, HP]),
                                     ownrow.unsqueeze(1).unsqueeze(3).broadcast_to([P, 4, 4, HP]),
                                     ALU.mult).then_inc(s_sbd.sem, 1)

                own_rows(0, 0)
                own_rows(0, 1)
                scale_c(0, 0)
                scale_c(0, 1)
                for q in range(Q):
                    if q + 1 < Q:
                        own_rows(q + 1, 0)
                    spread(q, 0)
                    if q == 0:
                        prep(t, t + 1)
                    if q + 1 < Q:
                        scale_c(q + 1, 0)
                        own_rows(q + 1, 1)
                    spread(q, 1)
                    if q + 1 < Q:
                        scale_c(q + 1, 1)

                def add_pair(g):
                    if g < GH:
                        pool.wait_ge(s_odd.sem, s_odd.at(t, g))
                        pool.wait_ge(s_sq.sem, s_sq.at(t, 2 * g))
                    else:
                        pool.wait_ge(s_sq.sem, s_sq.at(t, 2 * g + 1))
                    gp.tensor_tensor(sq[g % 3], sq[g % 3], sq_odd[g % 2], ALU.add).then_inc(s_pair.sem, 1)

                def group_roots(k):
                    pool.wait_ge(s_gv.sem, s_gv.at(t, k))
                    gp.tensor_tensor(gv[:, :], gv[:, :], half[:, 0:1].broadcast_to([P, Q * GH]), ALU.pow).then_inc(s_pow.sem, 1)

                def y_low(n):
                    pool.wait_ge(s_yh.sem, s_yh.at(t, n))
                    gp.tensor_tensor(yl[n % NY], xbc[:, n, :], yh[n % NY], ALU.subtract).then_inc(s_yl.sem, 1)

                for g in range(G - 1):
                    add_pair(g)
                    if g == GH - 1:
                        group_roots(0)
                y_low(0)
                y_low(1)
                group_roots(1)
                for n in range(2, NX):
                    y_low(n)
                    if n == 7:
                        prep_low(t)

        @block.vector
        def _(dve):
            v = nc.vector
            links = [0]
            base = [0]

            def link(ins):
                links[0] += 1
                ins.then_inc(s_chain, 1)
                dve.wait_ge(s_chain, base[0] + links[0])

            def magnitude(j, raw):
                v.tensor_reduce(amax[:, j:j + 1], raw, AX.X, ALU.max, apply_absolute_value=True).then_inc(s_mag, 1)

            def scale(j):
                dve.wait_ge(s_gmax, j + 1)
                g, p2, up = gmax[:, j:j + 1], pow2[:, j:j + 1], up_s[:, j:j + 1]
                link(v.tensor_scalar(g, g, 1e-30, 1e36, ALU.max, ALU.min))
                link(v.tensor_scalar(p2.bitcast(U32), g.bitcast(U32), 0x7F800000, None, ALU.bitwise_and))
                link(v.reciprocal(up, p2))
                link(v.tensor_scalar(down_s[:, j:j + 1], p2, 1.0 / UP, None, ALU.mult))
                v.tensor_scalar(up, up, UP, None, ALU.mult).then_inc(s_up, 1)

            def low(j, raw, hi, lo):
                n = raw.shape[1] // 4
                dve.wait_ge(s_up, j + 1)
                for i in range(4):
                    dve.wait_ge(s_hi, 4 * j + i + 1)
                    c = slice(i * n, (i + 1) * n)
                    v.scalar_tensor_tensor(lo[:, c], raw[:, c], up_s[:, j:j + 1], hi[:, c],
                                           ALU.mult, ALU.subtract).then_inc(s_lo, 1)

            v.memset(keep_v[:, :], 1.0).then_inc(s_out_t.sem, 1)
            v.memset(carrier[:, :], 0.0).then_inc(s_out, 16)
            n_in = raw_in.shape[1] // 4
            for i in range(4):
                dve.wait_ge(s_quarter[i], 16)
                ins = v.tensor_reduce(amax_q[:, i:i + 1], raw_in[:, i * n_in:(i + 1) * n_in], AX.X, ALU.max,
                                      apply_absolute_value=True)
            link(ins)
            magnitude(0, amax_q[:, :])
            dve.wait_ge(s_par, 2 * 16)
            v.tensor_scalar(row[:, 3, :], row[:, 3, :], A_LOG_TOP, None, ALU.min).then_inc(s_alog, 1)
            scale(0)
            link(v.tensor_scalar(ev_scale[:, :], mup, down_s[:, 0:1], None, ALU.mult))
            link(v.tensor_tensor(ev_bias[:, :], mup, b_in, ALU.mult))
            low(0, raw_in, win_h[:, :, :].rearrange("p c n -> p (c n)"), win_l[:, :, :].rearrange("p c n -> p (c n)"))
            dve.wait_ge(s_raw_gu, 4 * 16)
            magnitude(1, raw_gu)
            dve.wait_ge(a_done.sem, a_done.at(None, "a_log"))
            link(v.tensor_scalar(neg_a[:, :], neg_a[:, :], -1.0, None, ALU.mult))
            dve.wait_ge(s_raw_out, 16)
            for n in range(NX):
                c = slice(n * D, (n + 1) * D)
                ins = v.tensor_scalar(raw_out[:, c], raw_out[:, c], norm_w[:, n:n + 1], None, ALU.mult)
            link(ins)
            scale(1)
            low(1, raw_gu, gu_h[:, :, :, :].rearrange("p c j n -> p (c j n)"),
                gu_l[:, :, :, :].rearrange("p c j n -> p (c j n)"))
            magnitude(2, raw_out)
            scale(2)

            def taken(t, item):
                dve.wait_ge(d_full.sem, d_full.at(t, item))
                return d_bank[(d_full.first[item] if t is None else d_full.pos[item]) % RD]

            def split3(src, n, dst, done):
                link(v.tensor_copy(dst[0:n, :], src))
                ins = v.tensor_tensor(sp_r[0:n, :], src, dst[0:n, :], ALU.subtract)
                ins.then_inc(d_done.sem, 1)
                dve.wait_ge(d_done.sem, done)
                link(v.tensor_copy(sp_b[0:n, :], sp_r[0:n, :]))
                link(v.tensor_tensor(sp_r[0:n, :], sp_r[0:n, :], sp_b[0:n, :], ALU.subtract))
                v.tensor_copy(dst[32:32 + n, :], sp_b[0:n, :])
                return v.tensor_copy(dst[64:64 + n, :], sp_r[0:n, :])

            def prep_stats(k):
                dve.wait_ge(s_x, 16 * (k + 1))
                for q in range(Q):
                    ins = v.bn_stats(stat[:, q, :], xld[:, q, :])
                link(ins)
                carry_vector()
                for q in range(Q):
                    ins = v.bn_aggr(mv[:, q, :], stat[:, q, :])
                link(ins)
                v.tensor_scalar(veps[:, :], mv[:, :, 1], EPS, None, ALU.add).then_inc(s_var, 1)

            def prep_norm(t):
                dve.wait_ge(s_pow.sem, s_pow.at(t, "ln"))
                for q in range(Q):
                    ins = v.tensor_scalar(xld[:, q, :], xld[:, q, :], mv[:, q, 0:1], rstd[:, q:q + 1],
                                          ALU.subtract, ALU.mult)
                ins.then_inc(s_xn, 1)

            def prep_turned(t):
                taken(t, "xn1")
                for c in range(KC):
                    b = taken(t, f"xn{c}")
                    v.tensor_copy(x32[:, c, :], b[:, :]).then_inc(d_done.sem, 1)

            def prep_exp(t):
                w = H + E + 1
                b = taken(t, "small")[:, 0:Q * w].rearrange("p (q w) -> p q w", q=Q)
                link(v.tensor_reduce(lmax[:, :], b[:, :, H:H + E], AX.X, ALU.max))
                v.tensor_tensor(exi[:, :, H:H + E], b[:, :, H:H + E], lmax[:, :].unsqueeze(2).broadcast_to([P, Q, E]),
                                ALU.subtract)
                v.tensor_scalar(exi[:, :, w - 1], b[:, :, w - 1], -1.0, None, ALU.mult)

                def on_heads(k):
                    return row[:, k, :].unsqueeze(1).broadcast_to([P, Q, H])

                v.tensor_tensor(v_dt[:, :, :], b[:, :, 0:H], on_heads(0), ALU.add).then_inc(d_done.sem, 1)
                dve.wait_ge(d_done.sem, d_done.at(t, "small"))
                link(v.tensor_tensor(v_dt[:, :, :], v_dt[:, :, :], on_heads(1), ALU.mult))
                link(v.tensor_tensor(v_dt[:, :, :], v_dt[:, :, :], on_heads(2), ALU.add))
                v.scalar_tensor_tensor(exi[:, :, 0:H], v_dt[:, :, :], -1.0, v_dt[:, :, :], ALU.mult,
                                       ALU.min).then_inc(s_exi, 1)

            def route():
                link(v.tensor_reduce(lsum[:, :], ex[:, :, H:H + E], AX.X, ALU.add))
                link(v.reciprocal(lsum[:, :], lsum[:, :]))
                link(v.tensor_tensor(probs[:, :, :], ex[:, :, H:H + E], lsum[:, :].unsqueeze(2).broadcast_to([P, Q, E]),
                                     ALU.mult))

            def route_chunk(q):
                other = probs[:, q, :].unsqueeze(1).broadcast_to([P, E, E])
                own = probs[:, q, :].unsqueeze(2).broadcast_to([P, E, E])
                link(v.tensor_tensor(big[0], other, own, ALU.is_equal))
                link(v.tensor_tensor(big[0], big[0], lower, ALU.mult))
                link(v.tensor_tensor(big[1], other, own, ALU.is_gt))
                link(v.tensor_tensor(big[1], big[1], big[0], ALU.add))
                link(v.tensor_reduce(rank, big[1], AX.X, ALU.add))
                link(v.scalar_tensor_tensor(cmb[:, q, 0:E], rank, 1.5, probs[:, q, :], ALU.is_lt, ALU.mult))
                if q == Q - 1:
                    link(v.tensor_scalar(lmax[:, :], ex[:, :, H + E], 1.0, None, ALU.add))
                    v.reciprocal(cmb[:, :, E], lmax[:, :]).then_inc(s_route, 1)

            e, series = ex[:, :, 0:H], exi[:, :, 0:H]

            def steps_ratio():
                link(v.tensor_scalar(tmp[:, :, :], e, 2.0, None, ALU.add))
                link(v.reciprocal(tmp[:, :, :], tmp[:, :, :]))
                link(v.tensor_tensor(tmp[:, :, :], tmp[:, :, :], e, ALU.mult))
                link(v.tensor_tensor(e, tmp[:, :, :], tmp[:, :, :], ALU.mult))
                link(v.tensor_scalar(series, e, 1.0 / 15, None, ALU.mult))

            def steps_series():
                for k in (13, 11, 9, 7, 5, 3):
                    link(v.scalar_tensor_tensor(series, series, 1.0 / k, e, ALU.add, ALU.mult))

            def steps_softplus():
                link(v.scalar_tensor_tensor(series, series, 1.0, tmp[:, :, :], ALU.add, ALU.mult))
                link(v.tensor_scalar(v_dt[:, :, :], v_dt[:, :, :], 0.0, None, ALU.max))
                link(v.scalar_tensor_tensor(v_dt[:, :, :], series, 2.0, v_dt[:, :, :], ALU.mult, ALU.add))

            def steps():
                v.tensor_copy(dt[:, :, :], v_dt[:, :, :])
                link(v.tensor_tensor(da[:, :, :], v_dt[:, :, :], neg_a[:, :].unsqueeze(1).broadcast_to([P, Q, H]),
                                     ALU.mult))
                v.tensor_scalar(da[:, :, :], da[:, :, :], DECAY_FLOOR, None, ALU.max).then_inc(s_da, 1)

            def split_sums(t):
                split3(taken(t, "comb")[0:E + 1, :], E + 1, cmbb, d_done.at(t, "comb")).then_inc(s_split.sem, 1)
                split3(taken(t, "cum")[0:H, :], H, cumb, d_done.at(t, "cum")).then_inc(s_split.sem, 1)
                b = taken(t, "suffix")
                v.tensor_copy(tmp[:, :, :], b[:, 0:Q * H]).then_inc(s_split.sem, 1)
                v.tensor_scalar(da[:, :, :], b[:, Q * H:2 * Q * H].rearrange("p (q h) -> p q h", q=Q), -1.0, None,
                                ALU.mult).then_inc(d_done.sem, 1)

            prep_stats(0)
            prep_norm(None)
            prep_turned(None)
            prep_exp(None)
            dve.wait_ge(s_ex, 1)
            route()
            for q in range(Q):
                route_chunk(q)
            steps_ratio()
            steps_series()
            steps_softplus()
            steps()
            dve.wait_ge(s_zero, 1)
            split_sums(None)
            before = links[0]
            with dve.Fori(0, TILES) as t:
                links[0] = 0
                base[0] = before + t * V_LINKS

                def conv(n):
                    k = CONV_ORDER[n]
                    uu, a = u[n % 3], acc[n % 3]
                    w = conv_w[:, TAPS * k:TAPS * (k + 1)]
                    dve.wait_ge(a_done.sem, a_done.at(made_in(t, n), ("u", n)))
                    dve.wait_ge(s_u.sem, s_u.at(t, ("pad", n)))
                    if n >= 3:
                        dve.wait_ge(s_silu.sem, s_silu.at(t, n - 3))
                    link(v.tensor_scalar(a, uu[:, TAPS - 1:UW], w[:, TAPS - 1:TAPS], conv_b[:, k:k + 1],
                                         ALU.mult, ALU.add))
                    for j in range(TAPS - 1):
                        ins = v.scalar_tensor_tensor(a, uu[:, j:j + TT], w[:, j:j + 1], a, ALU.mult, ALU.add)
                        if j < TAPS - 2:
                            link(ins)
                    ins.then_inc(s_conv.sem, 1)

                def inner(n):
                    m = rows_of(n)
                    h = hin[n % 3][0:m, :]
                    b = taken(t, ("up", n))
                    dve.wait_ge(a_done.sem, a_done.at(t, ("gate", n)))
                    if n >= 3:
                        dve.wait_ge(s_down.sem, s_down.at(t, n - 3))
                    v.scalar_tensor_tensor(h, b[0:m, :], down_s[0:m, 1:2], gact[n % 2][0:m, :], ALU.mult,
                                           ALU.mult).then_inc(d_done.sem, 1)
                    b = taken(t, ("bc", n))
                    dve.wait_ge(d_done.sem, d_done.at(t, ("up", n)))
                    v.tensor_tensor(h, h, b[0:m, :], ALU.mult).then_inc(d_done.sem, 1)

                def steps_x(q, r):
                    b = taken(t, ("xt", q, r))
                    v.tensor_tensor(xd[:, r * TT:(r + 1) * TT].rearrange("p (h w) -> p h w", h=8),
                                    b[:, :].rearrange("p (h w) -> p h w", h=8),
                                    dt[:, q, 8 * r:8 * r + 8].unsqueeze(2).broadcast_to([P, 8, HP]),
                                    ALU.mult).then_inc(d_done.sem, 1)

                def decayed_b(q):
                    b = taken(t, ("bt", q))
                    if q == 0:
                        dve.wait_ge(s_wend, t + 1)
                    v.tensor_tensor(bp, b[:, 0:G * S].rearrange("p (g s) -> p g s", g=G).unsqueeze(2).broadcast_to([P, G, 4, S]),
                                    w_end[:, q, :].rearrange("p (g h) -> p g h", g=G).unsqueeze(3).broadcast_to([P, G, 4, S]),
                                    ALU.mult).then_inc(d_done.sem, 1)

                for k in range(NF):
                    for n in conv_blocks(k):
                        conv(n)
                    inner(k)
                    if k == NF - 2:
                        dve.wait_ge(s_out, 16 * (t + 1))
                        steps_x(0, 0)
                        steps_x(0, 1)
                        decayed_b(0)
                    if k == NF - 1:
                        steps_x(0, 2)
                        steps_x(0, 3)
                dve.wait_ge(s_down.sem, s_down.at(t, NF - 1))
                for c in range(KC):
                    ins = v.tensor_scalar(out_t[:, c, :], acc_bank[c][:, :], b_out[:, c:c + 1], None, ALU.add)
                ins.then_inc(s_ffn, 1)

                def new_states(q):
                    dve.wait_ge(a_done.sem, a_done.at(t, ("E", q, 1)))
                    if q:
                        dve.wait_ge(s_sbd.sem, s_sbd.at(t, (q - 1, 1)))
                    else:
                        dve.wait_ge(s_sbd.sem, s_sbd.n0 + t * s_sbd.n)
                    link(v.tensor_tensor(sc[:, :, :], sc[:, :, :], eb[:, :, P - 1:P].broadcast_to([P, G, HP]), ALU.mult))
                    b = taken(t, ("st", q))
                    v.tensor_tensor(sc[:, :, :], sc[:, :, :], b[:, :].rearrange("p (g w) -> p g w", g=G),
                                    ALU.add).then_inc(d_done.sem, 1)
                    if q == Q - 1:
                        dve.wait_ge(d_done.sem, d_done.at(t, ("st", q)))
                        v.tensor_scalar(sc[:, :, :], sc[:, :, :], keep_v[:, 0:1], None, ALU.mult).then_inc(s_carry, 1)
                        dve.wait_ge(s_carry, t + 1)
                        link(v.tensor_scalar(keep_v[:, :], keep_v[:, :], -1.0, 1.0, ALU.mult, ALU.add))

                def weigh(s):
                    q, g = divmod(s, G)
                    dve.wait_ge(a_done.sem, a_done.at(t, ("diff", s)))
                    dve.wait_ge(s_g.sem, s_g.at(t, (q, g // 4)))
                    if s >= 2:
                        dve.wait_ge(d_full.sem, d_full.at(t, ("y", s - 2)))
                    k = g % 4
                    v.tensor_tensor(mb[s % 2].rearrange("p (h i) -> p h i", h=4),
                                    lb[s % 2].rearrange("p (h i) -> p h i", h=4),
                                    acc_bank[g // 4][:, span(k)].unsqueeze(1).broadcast_to([P, 4, P]),
                                    ALU.mult).then_inc(s_m.sem, 1)

                def take_y(s):
                    q, g = divmod(s, G)
                    b = taken(t, ("y", s))
                    for k in range(2):
                        xx = xbc[:, 2 * g + k, span(q)]
                        ins = v.scalar_tensor_tensor(xx, xx, d_par[:, 2 * g + k:2 * g + k + 1], b[:, span(k)],
                                                     ALU.mult, ALU.add)
                    ins.then_inc(d_done.sem, 1)

                weigh(0)
                weigh(1)
                for s in range(Q * G):
                    q, g = divmod(s, G)
                    take_y(s)
                    if s + 2 < Q * G:
                        weigh(s + 2)
                    if g == 2:
                        new_states(q)
                    if q + 1 < Q:
                        if g in (2, 4, 6):
                            steps_x(q + 1, g // 2 - 1)
                        if g == 5:
                            decayed_b(q + 1)
                        if g == 7:
                            steps_x(q + 1, 3)
                    if s == STATS_AT:
                        prep_stats(t + 1)
                    if s == NORM_AT:
                        prep_norm(t)
                    if s == TURN_AT:
                        prep_turned(t)
                    if s == SMALL_AT:
                        prep_exp(t)
                    if s == ROUTE_AT:
                        dve.wait_ge(s_ex, t + 2)
                        route()
                    if s in ROUTE_CHUNK_AT:
                        route_chunk(ROUTE_CHUNK_AT[s])
                    if s == STEPS_AT:
                        steps_ratio()
                    if s == STEPS_AT + 1:
                        steps_series()
                    if s == STEPS_AT + 2:
                        steps_softplus()

                def group_squares(k):
                    dve.wait_ge(s_gs.sem, s_gs.at(t, GH * k + GH - 1))
                    v.tensor_scalar(gv[:, :], acc_bank[k][:, 0:Q * GH], float(G) / DS, EPS, ALU.mult, ALU.add).then_inc(s_gv.sem, 1)

                def split_roots(k):
                    item = f"rt{k}"
                    split3(taken(t, item)[0:GH, :], GH, rstdb[k], d_done.at(t, item)).then_inc(s_rp.sem, 1)

                def normalise(n):
                    b = taken(t, ("rb", n // 2))
                    ins = v.tensor_tensor(xbc[:, n, :], xbc[:, n, :], b[:, :], ALU.mult)
                    ins.then_inc(s_yn.sem if n % 2 == 0 else d_done.sem, 1)

                dve.wait_ge(d_done.sem, d_done.at(t, ("y", Q * G - 1)))
                for n in range(NX):
                    dve.wait_ge(a_done.sem, a_done.at(t, ("z", n)))
                    v.tensor_tensor(xbc[:, n, :], xbc[:, n, :], sz[n % 2], ALU.mult).then_inc(s_y.sem, 1)
                    if n % 2 and n < NX // 2:
                        g = n // 2
                        dve.wait_ge(s_y.sem, s_y.at(t, n))
                        if g >= 2:
                            dve.wait_ge(s_pair.sem, s_pair.at(t, g - 2))
                        v.tensor_tensor(sq_odd[g % 2], xbc[:, n, :], xbc[:, n, :], ALU.mult).then_inc(s_odd.sem, 1)
                    if n == 9:
                        group_squares(0)
                    if n == 12:
                        split_roots(0)
                for n in range(NX):
                    normalise(n)
                    if n == 1:
                        group_squares(1)
                    if n == NX // 2 - 1:
                        split_roots(1)
                    if n == NX // 2 + 1:
                        steps()
                split_sums(t)
                dve.wait_ge(s_wo.sem, s_wo.at(t, NX - 1))
                for c in range(KC):
                    ins = v.scalar_tensor_tensor(out_t[:, c, :], acc_bank[c][:, :], down_s[:, 2:3], out_t[:, c, :],
                                                 ALU.mult, ALU.add)
                ins.then_inc(s_out_t.sem, 1)
                dve.wait_ge(s_xres, 16 * (t + 1))
                for j in range(2):
                    b = taken(t, f"ot{j}")
                    res = xres[:, 2 * j:2 * j + 2, :]
                    v.tensor_tensor(res, res, b[:, :].rearrange("p (q d) -> p q d", q=2), ALU.add).then_inc(d_done.sem, 1)
                assert links[0] == V_LINKS, links[0]


def kernel(L0_attn_hidden_states, L0_attn_W_in, L0_attn_b_in, L0_attn_conv_w, L0_attn_conv_b, L0_attn_A_log,
           L0_attn_D_param, L0_attn_dt_bias, L0_attn_norm_w, L0_attn_W_out, L0_attn_b_out, L0_attn_mup_vector,
           L0_ffn_W_router, L0_ffn_W_sgate, L0_ffn_Ws_gate_up, L0_ffn_Ws_down, L0_ffn_We_gate_up, L0_ffn_We_down):
    import numpy as np
    import concourse.bacc as bacc
    from concourse.bass_utils import run_bass_kernel_spmd

    f = np.float32

    def on_p(a):
        a = np.asarray(a)
        return a.reshape((-1, P) + a.shape[1:]).swapaxes(0, 1)

    def flat(a):
        return np.ascontiguousarray(a.reshape(P, -1))

    x = np.asarray(L0_attn_hidden_states)
    shape = x.shape
    x = x.reshape(TILES, Q, P, D).transpose(0, 2, 1, 3)
    x = np.ascontiguousarray(np.concatenate([x, x[:1]]))
    w_in = np.asarray(L0_attn_W_in)
    wide = 2 * DS + 2 * G * S
    mup, b_in = np.asarray(L0_attn_mup_vector), np.asarray(L0_attn_b_in)
    w_small = np.concatenate([w_in[:, wide:], np.asarray(L0_ffn_W_router).T, np.asarray(L0_ffn_W_sgate).T], axis=1)
    gu_s, gu_e = np.asarray(L0_ffn_Ws_gate_up), np.asarray(L0_ffn_We_gate_up)

    main = I_MOE - TAIL

    def inner(k):
        experts = [gu_e[e][:, k * I_MOE:(k + 1) * I_MOE] for e in range(E)]
        return np.concatenate([gu_s[:, k * I_SH:(k + 1) * I_SH]] + [w[:, :main] for w in experts]
                              + [w[:, main:] for w in experts], axis=1)

    w_gu = np.stack([inner(0), inner(1)], axis=1)
    down_e = np.asarray(L0_ffn_We_down)
    down = np.concatenate([np.asarray(L0_ffn_Ws_down), down_e[:, :main].reshape(-1, D), down_e[:, main:].reshape(-1, D),
                           np.zeros((NF * P - FI, D), f)])
    par = np.concatenate([flat(on_p(mup[:wide])), flat(on_p(b_in[:wide])), flat(on_p(L0_attn_conv_w)),
                          flat(on_p(L0_attn_conv_b)), flat(on_p(np.repeat(np.asarray(L0_attn_D_param), HP))),
                          flat(on_p(L0_attn_norm_w)), flat(on_p(L0_attn_b_out))], axis=1)
    rows = np.stack([b_in[wide:], mup[wide:], np.asarray(L0_attn_dt_bias), np.asarray(L0_attn_A_log)])
    rows = np.ascontiguousarray(np.broadcast_to(rows, (P,) + rows.shape))

    i = np.arange(P)
    lower = np.broadcast_to(np.tril(np.ones((E, E)), -1), (P, E, E)).reshape(P, -1)
    constf = np.concatenate([np.eye(P), i[:, None] <= i, i[:, None] > i, i[:, None] // S == np.arange(4), lower], axis=1).astype(f)
    sel = (i[:, None] % H == np.arange(H)) & (i[:, None] < 3 * H)
    tail = (i[:, None] % 32 == i // TAIL) & (i[:, None] < 96)
    constb = np.concatenate([np.eye(P), np.where(i[:, None] > i, -32768.0, 0.0), sel, tail], axis=1)
    constb = np.ascontiguousarray(constb.astype(f).view(np.uint32) >> 16).astype(np.uint16)

    arrays = {"x": x, "w_in": flat(on_p(w_in[:, :wide])), "w_small": np.ascontiguousarray(on_p(w_small)),
              "w_gu": flat(on_p(w_gu)), "w_out": flat(on_p(L0_attn_W_out)), "w_down": np.ascontiguousarray(on_p(down)),
              "par": np.ascontiguousarray(par), "rows": rows, "constf": constf, "constb": constb}
    nc = bacc.Bacc("TRN2", target_bir_lowering=False, num_devices=1)
    args = [nc.dram_tensor(k, a.shape, mybir.dt.from_np(a.dtype), kind="ExternalInput").ap() for k, a in arrays.items()]
    out = nc.dram_tensor("out", (TILES, P, Q, D), F32, kind="ExternalOutput").ap()
    c_rows = nc.dram_tensor("c_rows", (NB, P, TT), F32, kind="Internal").ap()
    layer_program(nc, *args, c_rows, out)
    r = run_bass_kernel_spmd(nc, [arrays], core_ids=[0])
    return r.results[0]["out"].transpose(0, 2, 1, 3).reshape(shape)
```

```python
from contextlib import ExitStack

import concourse.bass as bass
from concourse import mybir

ALU = mybir.AluOpType
ACT = mybir.ActivationFunctionType
AX = mybir.AxisListType
F32 = mybir.dt.float32
F16 = mybir.dt.float16
BF16 = mybir.dt.bfloat16
U32 = mybir.dt.uint32
ABSMAX = bass.bass_isa.ReduceOp.absmax

P = 128
D = 256
KC = D // P
TT = 512
Q = TT // P
H, HP, G, S = 32, 64, 8, 32
DS = H * HP
GH = G // 2
NX = DS // P
NB = G * S // P
NCONV = NX + 2 * NB
TAPS = 4
E = 8
I_SH, I_MOE = 704, 176
FI = I_SH + E * I_MOE
NF = -(-FI // P)
TAIL = I_MOE % 32
PARTS = [E] * (I_SH // 32) + [e for e in range(E) for _ in range(I_MOE // 32)] + [E + 1 + i for i in range(E * TAIL // 32)]
EPS = 1e-5
DECAY_FLOOR = -104.0
A_LOG_TOP = 80.0
UP = 256.0
RA = RD = 3

CONV_ORDER = [NX, NX + 1, NX + 2, NX + 3] + list(range(NX))
NY = 3
AHEAD = 1
SUM_AFTER = {6: 0, 7: 1, 8: 2, 9: 3, 13: 4}
STATS_AT, NORM_AT, TURN_AT, SMALL_AT, ROUTE_AT, STEPS_AT = 4, 9, 11, 12, 14, 27
ROUTE_CHUNK_AT = {16: 0, 19: 1, 22: 2, 24: 3}
TILES = 8
V_LINKS = 125


class Signal:

    def __init__(self, sem, names, first=()):
        self.sem, self.n, self.n0 = sem, len(names), len(first)
        self.pos = {name: i for i, name in enumerate(names)}
        self.first = {name: i for i, name in enumerate(first)}
        assert len(self.pos) == len(names)

    def at(self, t, name):
        if t is None:
            return self.first[name] + 1
        return self.n0 + t * self.n + self.pos[name] + 1

    def before(self, t, name, k):
        i = self.pos[name]
        assert self.n0 + i - k + 1 > 0
        return self.n0 + t * self.n + i - k + 1


def conv_blocks(k):
    def upto(k):
        return min(NCONV, AHEAD + -(-k * (NCONV - AHEAD) // (NF - 3)))
    return range(upto(k - 1) if k else 0, upto(k))


def ring_a():
    out = []
    for k in range(NF):
        out += [("u", n) for n in conv_blocks(k) if n >= AHEAD] + [("gate", k)]
    out += [("E", 0, 0), ("diff", 0), ("diff", 1)]
    for s in range(Q * G):
        q, g = divmod(s, G)
        if s + 2 < Q * G:
            out.append(("diff", s + 2))
        else:
            out.append(("z", s + 2 - Q * G))
        if g == 1:
            out.append(("E", q, 1))
        if q + 1 < Q and g == 5:
            out.append(("E", q + 1, 0))
    return out + [("z", n) for n in range(2, NX)] + [("u", n) for n in range(AHEAD)]


def ring_d():
    out = []
    for n in range(NF):
        out += [("up", n), ("bc", n)]
        out += {NF - 2: [("xt", 0, 0), ("xt", 0, 1), ("bt", 0)], NF - 1: [("xt", 0, 2), ("xt", 0, 3)]}.get(n, [])
    for s in range(Q * G):
        q, g = divmod(s, G)
        out.append(("y", s))
        if g == 2:
            out.append(("st", q))
        if q + 1 < Q:
            out += {2: [("xt", q + 1, 0)], 4: [("xt", q + 1, 1)], 5: [("bt", q + 1)], 6: [("xt", q + 1, 2)],
                    7: [("xt", q + 1, 3)]}.get(g, [])
        out += {TURN_AT: ["xn0", "xn1"], SMALL_AT: ["small"]}.get(s, [])
    return (out + ["rt0"] + [("rb", g) for g in range(GH)] + ["rt1"] + [("rb", g) for g in range(GH, G)]
            + ["comb", "sums", "cum", "ot0", "ot1"])


def layer_program(nc, x, w_in, w_small, w_gu, w_out, w_down, par, rows, constf, constb, c_rows, out):
    ctx = ExitStack()
    with ctx:
        def sb(name, shape, dt):
            return ctx.enter_context(nc.sbuf_tensor(name, shape, dt))

        def sem(name):
            return ctx.enter_context(nc.semaphore(name))

        win_h = sb("win_h", [P, KC, 2 * DS + 2 * G * S], F16)
        win_l = sb("win_l", [P, KC, 2 * DS + 2 * G * S], F16)
        gu_h = sb("gu_h", [P, KC, 2, FI], F16)
        gu_l = sb("gu_l", [P, KC, 2, FI], F16)
        wo_h = sb("wo_h", [P, NX, D], F16)
        wo_l = sb("wo_l", [P, NX, D], F16)
        wd_h = sb("wd_h", [P, NF, D], F16)
        wd_l = sb("wd_l", [P, NF, D], F16)
        wsm = sb("wsm", [P, KC, H + E + 1], F32)
        NIN = 2 * NX + 2 * NB
        parm = sb("parm", [P, par.shape[1]], F32)
        o = 0
        views = []
        for n in (NIN, NIN, NCONV * TAPS, NCONV, NX, NX, KC):
            views.append(parm[:, o:o + n])
            o += n
        mup, b_in, conv_w, conv_b, d_par, norm_w, b_out = views
        row = sb("row", [P, 4, H], F32)
        cf = sb("cf", [P, constf.shape[1]], F32)
        ident, tri_u, tri_s = cf[:, 0:P], cf[:, P:2 * P], cf[:, 2 * P:3 * P]
        o = 3 * P
        ownrow = cf[:, o:o + 4]
        lower = cf[:, o + 4:o + 4 + E * E].rearrange("p (a b) -> p a b", b=E)
        cb = sb("cb", [P, constb.shape[1]], BF16)
        identb, maskneg = cb[:, 0:P], cb[:, P:2 * P]
        o = 2 * P
        sel = {}
        for n in (H, E + 1, GH):
            sel[n] = cb[0:3 * n, o:o + n]
            o += n
        seltail = cb[0:3 * (E + 1), o:o + P]
        ev_scale = sb("ev_scale", [P, NIN], F32)
        ev_bias = sb("ev_bias", [P, NIN], F32)
        carrier = sb("carrier", [P, 1], F32)
        one = sb("one", [P, 1], F32)
        amax = sb("amax", [P, 4], F32)
        amax_q = sb("amax_q", [P, 4], F32)
        gmax = sb("gmax", [P, 4], F32)
        pow2 = sb("pow2", [P, 4], F32)
        up_s = sb("up_s", [P, 4], F32)
        down_s = sb("down_s", [P, 4], F32)
        assert (2 * D) ** 2 / 8 < 65504
        in_scale = sb("in_scale", [P, 1], F32)
        out_scale = sb("out_scale", [P, 1], F32)
        neg_a = sb("neg_a", [P, H], F32)
        half = sb("half", [P, 1], F32)
        gv = sb("gv", [P, Q * GH], F32)
        keep_v = sb("keep_v", [P, 1], F32)
        keep_p = sb("keep_p", [P, 1], F32)

        xbc = sb("xbc", [P, NCONV, TT], F32)
        xh = sb("xh", [P, KC, TT], F16)
        xl = sb("xl", [P, KC, TT], F16)
        out_t = sb("out_t", [P, KC, TT], F32)
        hist = sb("hist", [P, NCONV, TAPS - 1], F32)
        sc = sb("sc", [P, G, HP], F32)
        v_dt = sb("v_dt", [P, Q, H], F32)
        ex = sb("ex", [P, Q, H + E + 1], F32)
        exi = sb("exi", [P, Q, H + E + 1], F32)
        exi_flat = exi[:, :, :].rearrange("p q w -> p (q w)")
        big = [exi_flat[:, k * E * E:(k + 1) * E * E].rearrange("p (a b) -> p a b", a=E) for k in range(2)]
        rank = exi_flat[:, 2 * E * E:2 * E * E + E]
        dt = sb("dt", [P, Q, H], F32)
        da = sb("da", [P, Q, H], F32)
        tmp = sb("tmp", [P, Q, H], F32)
        w_end = sb("w_end", [P, Q, H], F32)
        probs = sb("probs", [P, Q, E], F32)
        cmb = sb("cmb", [P, Q, E + 1], F32)
        cmbb = sb("cmbb", [96, TT], BF16)
        cumb = sb("cumb", [96, TT], BF16)
        stat = sb("stat", [P, Q, 6], F32)
        mv = sb("mv", [P, Q, 2], F32)
        rstd = sb("rstd", [P, Q], F32)
        veps = sb("veps", [P, Q], F32)
        lmax = sb("lmax", [P, Q], F32)
        lsum = sb("lsum", [P, Q], F32)
        UW = TT + TAPS - 1
        ARENA = G * 4 * HP + 3 * (UW + 1) + 9 * TT + 2 * DS - DS // 2
        arena = sb("arena", [P, ARENA], F32)
        sbd = arena[:, 0:G * 4 * HP].rearrange("p (g c) -> p g c", g=G)
        at = [G * 4 * HP]

        def carve(n):
            at[0] += n
            assert at[0] <= ARENA
            return arena[:, at[0] - n:at[0]]

        u = [carve(UW + 1)[:, 0:UW] for _ in range(3)]
        acc = [carve(TT) for _ in range(3)]
        top = at[0]
        gact = [carve(TT) for _ in range(2)]
        low_hin = at[0]
        hin = [carve(TT) for _ in range(2)]
        hh = [carve(TT // 2).bitcast(F16) for _ in range(2)]
        hl = [carve(TT // 2).bitcast(F16) for _ in range(2)]
        at[0] = low_hin + 2 * TT
        xld_flat = carve(Q * D)
        xld = xld_flat.rearrange("p (q d) -> p q d", q=Q)
        x32 = xld_flat.rearrange("p (c t) -> p c t", c=KC)
        high = at[0]
        at[0] = low_hin
        parts_of = {n: carve(Q * 3 * n // 2).bitcast(BF16).rearrange("p (q k n) -> p q k n", q=Q, k=3) for n in (H, E + 1, GH)}
        left_of = {n: carve(Q * n).rearrange("p (q n) -> p q n", q=Q) for n in (H, E + 1, GH)}
        assert at[0] <= low_hin + 2 * TT
        at[0] = G * 4 * HP
        cm = carve(G * P).rearrange("p (g i) -> p g i", g=G)
        eb = carve(G * P).rearrange("p (g i) -> p g i", g=G)
        crep = carve(G * P).rearrange("p (g i) -> p g i", g=G)
        at[0] = top
        lb = [carve(4 * P) for _ in range(2)]
        mb = [carve(4 * P) for _ in range(2)]
        at[0] = high
        bp = carve(G * 4 * S).rearrange("p (g h s) -> p g h s", g=G, h=4)
        xd = carve(DS)
        at[0] = G * 4 * HP
        sz = [carve(TT) for _ in range(2)]
        sq = [carve(TT) for _ in range(3)]
        sq_odd = [carve(TT)]
        at[0] = high
        xres = carve(Q * D).rearrange("p (q d) -> p q d", q=Q)
        yh = [carve(TT // 2).bitcast(F16) for _ in range(NY)]
        yl = [carve(TT // 2).bitcast(F16) for _ in range(NY)]
        sq_odd.append(carve(TT))
        raw_in = xbc[:, :, :].rearrange("p n t -> p (n t)")[:, 0:KC * (2 * DS + 2 * G * S)]
        raw_gu = arena[:, 0:KC * 2 * FI]
        raw_out = xbc[:, :, :].rearrange("p n t -> p (n t)")[:, 0:NX * D]
        raw_down = xbc[:, :, :].rearrange("p n t -> p (n t)")[:, NX * D:(NX + NF) * D]

        bank = [ctx.enter_context(nc.psum_tensor(f"bank{i}", [P, TT], F32)) for i in range(8)]
        rstdb = [cmbb, cumb]
        acc_bank, a_bank, d_bank = bank[0:2], bank[2:5], bank[5:8]

        RAW, RDW = ring_a(), ring_d()
        PREP = ["xn0", "xn1", "small", "comb", "sums", "cum"]
        assert len(RAW) % RA == 0 and len(RDW) % RD == 0 and len(PREP) % RD == 0
        s_par = sem("s_par")
        s_const = sem("s_const")
        s_quarter = [sem(f"s_quarter{i}") for i in range(4)]
        s_raw_gu = sem("s_raw_gu")
        s_raw_out = sem("s_raw_out")
        s_raw_down = sem("s_raw_down")
        s_mag = sem("s_mag")
        s_gmax = sem("s_gmax")
        s_up = sem("s_up")
        s_hi = sem("s_hi")
        s_lo = sem("s_lo")
        s_lo_last = sem("s_lo_last")
        s_scaled = sem("s_scaled")
        s_lo_out = sem("s_lo_out")
        s_zero = sem("s_zero")
        s_alog = sem("s_alog")
        a_full = Signal(sem("a_full"), RAW, RAW[-AHEAD:])
        a_done = Signal(sem("a_done"), RAW, ["a_log", "normed"] + RAW[-AHEAD:])
        d_full = Signal(sem("d_full"), RDW, PREP)
        d_done = Signal(sem("d_done"), RDW, PREP)
        s_chain = sem("s_chain")
        s_u = Signal(sem("s_u"), [("pad", n) for n in range(NCONV)])
        s_hist = Signal(sem("s_hist"), [("hist", n) for n in range(NCONV)], ["zero"])
        s_conv = Signal(sem("s_conv"), list(range(NCONV)))
        s_silu = Signal(sem("s_silu"), list(range(NCONV)))
        s_route = sem("s_route")
        s_da = sem("s_da")
        s_parts = {"cmb": sem("s_parts_cmb"), "cum": sem("s_parts_cum")}
        s_tmp = sem("s_tmp")
        DOWN = list(range(NF - 1)) + [(NF - 1, c) for c in range(KC)]
        s_down = Signal(sem("s_down"), DOWN)
        s_hh = Signal(sem("s_hh"), list(range(NF)))
        s_hl = Signal(sem("s_hl"), list(range(NF)))
        s_ffn = Signal(sem("s_ffn"), list(range(KC)))
        s_wend = sem("s_wend")
        s_crow = sem("s_crow")
        s_crep = [sem(f"s_crep{b}") for b in range(2)]
        s_cm = Signal(sem("s_cm"), [(q, b) for q in range(Q) for b in range(2)])
        s_cs = Signal(sem("s_cs"), [(q, b) for q in range(Q) for b in range(2)])
        s_g = Signal(sem("s_g"), [(q, b) for q in range(Q) for b in range(2)])
        s_m = Signal(sem("s_m"), list(range(Q * G)))
        s_carry = sem("s_carry")
        s_sbd = Signal(sem("s_sbd"), [(q, b) for q in range(Q) for b in range(2)], ["zero"])
        s_y = Signal(sem("s_y"), list(range(NX)))
        SQUARED = [n for n in range(NX) if n % 2 == 0 or n > NX // 2]
        s_sq = Signal(sem("s_sq"), SQUARED)
        s_odd = Signal(sem("s_odd"), list(range(GH)))
        s_pair = Signal(sem("s_pair"), list(range(G - 1)))
        s_gs = Signal(sem("s_gs"), list(range(G)))
        s_gv = Signal(sem("s_gv"), [0, 1])
        s_x = sem("s_x")
        s_xres = sem("s_xres")
        s_var = sem("s_var")
        s_pow = Signal(sem("s_pow"), ["ln", "g0", "g1"], ["ln"])
        s_xn = sem("s_xn")
        s_xh = Signal(sem("s_xh"), [0, 1], [0, 1])
        s_xl = Signal(sem("s_xl"), [0, 1], [0, 1])
        s_exi = sem("s_exi")
        s_ex = sem("s_ex")
        s_rp = Signal(sem("s_rp"), [0, 1])
        s_yn = Signal(sem("s_yn"), list(range(0, NX, 2)))
        s_yh = Signal(sem("s_yh"), list(range(NX)))
        s_yl = Signal(sem("s_yl"), list(range(NX)))
        s_wo = Signal(sem("s_wo"), list(range(NX)))
        s_out_t = Signal(sem("s_out_t"), ["out"], ["none"])
        s_out = sem("s_out")

        block = ctx.enter_context(nc.Block())

        def rows_of(n):
            return P if n < NF - 1 else FI - (NF - 1) * P

        def made_in(t, n):
            return t - 1 if n < AHEAD else t

        def span(q):
            return slice(q * P, (q + 1) * P)

        def carry_vector():
            nc.vector.tensor_copy(carrier[:, :], keep_v[:, :])

        @block.sync
        def _(sp):
            n_in = raw_in.shape[1] // 4
            for i in range(4):
                sp.dma_start(raw_in[:, i * n_in:(i + 1) * n_in], w_in[:, i * n_in:(i + 1) * n_in]).then_inc(s_quarter[i], 16)
            sp.dma_start(parm[:, :], par).then_inc(s_par, 16)
            sp.dma_start(row[:, :, :], rows).then_inc(s_par, 16)
            n_gu = raw_gu.shape[1] // 4
            for i in range(4):
                sp.dma_start(raw_gu[:, i * n_gu:(i + 1) * n_gu], w_gu[:, i * n_gu:(i + 1) * n_gu]).then_inc(s_raw_gu, 16)
            sp.dma_start(cf[:, :], constf).then_inc(s_const, 16)
            sp.dma_start(cb[:, :], constb.bitcast(BF16)).then_inc(s_const, 16)
            sp.dma_start(wsm[:, :, :], w_small).then_inc(s_const, 16)
            sp.wait_ge(s_lo, 2)
            sp.dma_start(raw_out, w_out).then_inc(s_raw_out, 16)
            sp.wait_ge(s_lo, 3)
            sp.wait_ge(s_lo_last, 1)
            sp.dma_start(raw_down, w_down.rearrange("p n d -> p (n d)")).then_inc(s_raw_down, 16)
            sp.wait_ge(s_lo, 6)
            sp.wait_ge(s_lo_last, 2)
            sp.dma_start(xld, x[0]).then_inc(s_x, 16)
            with sp.Fori(0, TILES) as t:
                sp.wait_ge(s_silu.sem, s_silu.at(t, 2 * NB - 1))
                sp.dma_start(c_rows.rearrange("b p t -> p b t"), xbc[:, NX + NB:NX + 2 * NB, :]).then_inc(s_crow, 16)
                sp.wait_ge(s_silu.sem, s_silu.at(t, NCONV - 1))
                for q in range(Q):
                    if q == 1:
                        sp.wait_ge(s_ffn.sem, s_ffn.at(t, KC - 1))
                        sp.dma_start(xld, x[t + 1]).then_inc(s_x, 16)
                    for b in range(2):
                        if q:
                            sp.wait_ge(d_full.sem, d_full.at(t, ("y", G * (q - 1) + 4 * b + 3)))
                        for h in range(4):
                            sp.dma_start(crep[S * h:S * (h + 1), 4 * b:4 * b + 4, :],
                                         c_rows[b].rearrange("(r s) t -> s r t", s=S)[:, :, span(q)]).then_inc(s_crep[b], 16)
                sp.wait_ge(d_full.sem, d_full.at(t, ("y", Q * G - 1)))
                sp.dma_start(xres, x[t]).then_inc(s_xres, 16)
                sp.wait_ge(d_done.sem, d_done.at(t, "ot1"))
                sp.dma_start(out[t], xres).then_inc(s_out, 16)
            sp.wait_ge(s_out, 16 * (TILES + 1))

        @block.tensor
        def _(pe):
            mm = nc.tensor.matmul

            def a_slot(t, item):
                if t is not None:
                    pe.wait_ge(a_done.sem, a_done.before(t, item, RA))
                return a_bank[a_done.pos[item] % RA]

            def d_slot(t, item):
                if t is None:
                    return d_bank[d_done.first[item] % RD]
                pe.wait_ge(d_done.sem, d_done.before(t, item, RD))
                return d_bank[d_done.pos[item] % RD]

            def pairs(o, wh, wl, rh, rl, start=True, stop=True):
                mm(o, wh, rh, start=start, stop=False)
                mm(o, wh, rl, start=False, stop=False)
                return mm(o, wl, rh, start=False, stop=stop)

            def project(o, wh, wl):
                for c in range(KC):
                    last = pairs(o, wh[c], wl[c], xh[:, c, :], xl[:, c, :], start=c == 0, stop=c == KC - 1)
                return last

            def in_block(t, item, k):
                cols = slice(k * P, (k + 1) * P)
                b = a_slot(t, item)
                project(b[:, :], [win_h[:, c, cols] for c in range(KC)],
                        [win_l[:, c, cols] for c in range(KC)]).then_inc(a_full.sem, 1)

            def ffn_block(t, n):
                m = rows_of(n)
                cols = slice(n * P, n * P + m)
                for j, slot, item, full in ((0, a_slot, ("gate", n), a_full), (1, d_slot, ("up", n), d_full)):
                    b = slot(t, item)
                    project(b[0:m, :], [gu_h[:, c, j, cols] for c in range(KC)],
                            [gu_l[:, c, j, cols] for c in range(KC)]).then_inc(full.sem, 1)
                b = d_slot(t, ("bc", n))
                def weights_onto(rows, pick):
                    return mm(b[rows, :], pick, cmbb[0:3 * (E + 1), :], start=True, stop=True, skip_group_check=True)

                parts = PARTS[4 * n:4 * n + 4]
                if parts[0] > E:
                    o = 32 * (parts[0] - E - 1)
                    last = weights_onto(slice(0, m), seltail[:, o:o + m])
                else:
                    last = weights_onto(slice(0, P), sel[E + 1][:, parts[0]:parts[0] + 1].broadcast_to([3 * (E + 1), P]))
                    for j, part in enumerate(parts):
                        if part == parts[0]:
                            continue
                        if part > E:
                            pick = seltail[:, 32 * (part - E - 1):32 * (part - E)]
                        else:
                            pick = sel[E + 1][:, part:part + 1].broadcast_to([3 * (E + 1), 32])
                        last = weights_onto(slice(32 * j, 32 * j + 32), pick)
                last.then_inc(d_full.sem, 1)

            def ffn_down(t, n):
                m = rows_of(n)
                pe.wait_ge(s_hl.sem, s_hl.at(t, n))
                if n == 0:
                    pe.wait_ge(s_out_t.sem, t + s_out_t.n0)
                for c in range(KC):
                    cols = slice(c * P, (c + 1) * P)
                    last = pairs(acc_bank[c][:, :], wd_h[0:m, n, cols], wd_l[0:m, n, cols], hh[n % 2][0:m, :],
                                 hl[n % 2][0:m, :], start=n == 0, stop=n == NF - 1)
                    if n == NF - 1:
                        last.then_inc(s_down.sem, 1)
                if n < NF - 1:
                    last.then_inc(s_down.sem, 1)

            def prep_tokens(t, k):
                pe.wait_ge(s_xn, k + 1)
                for c in range(KC):
                    b = d_slot(t, f"xn{c}")
                    for q in range(Q):
                        last = nc.tensor.transpose(b[:, span(q)], xld[:, q, c * P:(c + 1) * P], ident)
                    last.then_inc(d_full.sem, 1)

            def prep_small(t):
                pe.wait_ge(d_done.sem, d_done.at(t, "xn1"))
                b = d_slot(t, "small")
                w = H + E + 1
                for q in range(Q):
                    for c in range(KC):
                        last = mm(b[:, q * w:(q + 1) * w], x32[:, c, span(q)], wsm[:, c, :],
                                  start=c == 0, stop=c == KC - 1)
                last.then_inc(d_full.sem, 1)

            def chunk_decay(t, q, b):
                eo = a_slot(t, ("E", q, b))
                for r in range(4):
                    g = 4 * b + r
                    for h in range(4):
                        e = mm(eo[S * h:S * (h + 1), span(r)], sel[H][:, 4 * g + h:4 * g + h + 1].broadcast_to([96, S]),
                               cumb[:, span(q)], start=True, stop=True, skip_group_check=True)
                e.then_inc(a_full.sem, 1)

            def c_times_b(t, q, b):
                if q == 0:
                    pe.wait_ge(s_ffn.sem, s_ffn.at(t, b))
                else:
                    pe.wait_ge(s_m.sem, s_m.at(t, G * (q - 1) + 4 * b + 3))
                pe.wait_ge(s_cm.sem, s_cm.at(t, (q, b)))
                for r in range(4):
                    c = mm(acc_bank[b][:, span(r)], xbc[:, NX + b, span(q)], cm[:, 4 * b + r, :], start=True, stop=True)
                c.then_inc(s_g.sem, 1)

            def diff(t, s):
                q, g = divmod(s, G)
                b = a_slot(t, ("diff", s))
                for h in range(4):
                    mm(b[:, span(h)], identb, maskneg, start=True, stop=False, skip_group_check=True)
                    last = mm(b[:, span(h)], sel[H][:, 4 * g + h:4 * g + h + 1].broadcast_to([96, P]), cumb[:, span(q)],
                              start=False, stop=True, skip_group_check=True)
                last.then_inc(a_full.sem, 1)

            def x_tokens(t, q, r):
                b = d_slot(t, ("xt", q, r))
                if q == 0:
                    pe.wait_ge(s_silu.sem, s_silu.at(t, 2 * NB + 4 * r + 3))
                for k in range(4):
                    last = nc.tensor.transpose(b[:, span(k)], xbc[:, 4 * r + k, span(q)], ident)
                last.then_inc(d_full.sem, 1)

            def b_tokens(t, q):
                b = d_slot(t, ("bt", q))
                for k in range(NB):
                    last = nc.tensor.transpose(b[:, span(k)], xbc[:, NX + k, span(q)], ident)
                last.then_inc(d_full.sem, 1)

            def states(t, q):
                b = d_slot(t, ("st", q))
                pe.wait_ge(d_done.sem, d_done.at(t, ("xt", q, 3)))
                for g in range(G):
                    for h in range(4):
                        last = mm(b[S * h:S * (h + 1), g * HP:(g + 1) * HP], bp[:, g, h, :],
                                  xd[:, (4 * g + h) * HP:(4 * g + h + 1) * HP], start=True, stop=True,
                                  skip_group_check=True)
                last.then_inc(d_full.sem, 1)

            def mix(t, s):
                q, g = divmod(s, G)
                b = d_slot(t, ("y", s))
                if g % 4 == 0:
                    pe.wait_ge(s_cs.sem, s_cs.at(t, (q, g // 4)))
                    if q:
                        pe.wait_ge(s_sbd.sem, s_sbd.at(t, (q - 1, g // 4)))
                    else:
                        pe.wait_ge(s_sbd.sem, s_sbd.n0 + t * s_sbd.n)
                for pr in range(2):
                    mm(b[:, span(pr)], sbd[:, g, pr * P:(pr + 1) * P], crep[:, g, :], start=pr == 0, stop=False,
                       skip_group_check=True)
                pe.wait_ge(s_m.sem, s_m.at(t, s))
                for pr in range(2):
                    for e in range(2):
                        h = 2 * pr + e
                        last = mm(b[HP * e:HP * (e + 1), span(pr)], xd[:, (4 * g + h) * HP:(4 * g + h + 1) * HP],
                                  mb[s % 2][:, span(h)], start=False, stop=True, skip_group_check=True)
                last.then_inc(d_full.sem, 1)

            def blocks_ahead(t):
                pe.wait_ge(s_xh.sem, s_xh.at(t, KC - 1))
                pe.wait_ge(s_xl.sem, s_xl.at(t, KC - 1))
                for n in range(AHEAD):
                    in_block(t, ("u", n), NX + CONV_ORDER[n])

            def turn_parts(t, item, n, ready, value):
                pe.wait_ge(ready, value)
                b = d_slot(t, item)
                for q in range(Q):
                    last = mm(b[0:3 * n, span(q)], parts_of[n][:, q, :, :].rearrange("p k n -> p (k n)"), identb,
                              start=True, stop=True)
                last.then_inc(d_full.sem, 1)

            def decay_sums(t, k):
                pe.wait_ge(s_da, k + 1)
                b = d_slot(t, "sums")
                mm(b[:, 0:Q * H], tri_s, da[:, :, :], start=True, stop=True)
                mm(b[:, Q * H:2 * Q * H], tri_u, da[:, :, :], start=True, stop=True).then_inc(d_full.sem, 1)

            pe.wait_ge(s_const, 3 * 16)
            prep_tokens(None, 0)
            prep_small(None)
            blocks_ahead(None)
            turn_parts(None, "comb", E + 1, s_parts["cmb"], 1)
            decay_sums(None, 0)
            turn_parts(None, "cum", H, s_parts["cum"], 1)
            with pe.Fori(0, TILES) as t:
                for k in range(NF):
                    for n in conv_blocks(k):
                        if n >= AHEAD:
                            in_block(t, ("u", n), NX + CONV_ORDER[n])
                    ffn_block(t, k)
                    if k >= 2:
                        ffn_down(t, k - 2)
                    if k == NF - 2:
                        x_tokens(t, 0, 0)
                        x_tokens(t, 0, 1)
                        b_tokens(t, 0)
                    if k == NF - 1:
                        x_tokens(t, 0, 2)
                        x_tokens(t, 0, 3)
                        ffn_down(t, NF - 2)
                        chunk_decay(t, 0, 0)
                        diff(t, 0)
                        diff(t, 1)
                ffn_down(t, NF - 1)
                c_times_b(t, 0, 0)
                for s in range(Q * G):
                    q, g = divmod(s, G)
                    if s + 2 < Q * G:
                        diff(t, s + 2)
                    else:
                        in_block(t, ("z", s + 2 - Q * G), s + 2 - Q * G)
                    mix(t, s)
                    if g == 1:
                        chunk_decay(t, q, 1)
                        c_times_b(t, q, 1)
                    if g == 2:
                        states(t, q)
                    if q + 1 < Q:
                        if g in (2, 4, 6):
                            x_tokens(t, q + 1, g // 2 - 1)
                        if g == 5:
                            b_tokens(t, q + 1)
                            chunk_decay(t, q + 1, 0)
                            c_times_b(t, q + 1, 0)
                        if g == 7:
                            x_tokens(t, q + 1, 3)
                    if s == TURN_AT:
                        prep_tokens(t, t + 1)
                    if s == SMALL_AT:
                        prep_small(t)

                def square_sum(g):
                    squares = [sq[g % 3]]
                    if g < G - 1:
                        pe.wait_ge(s_pair.sem, s_pair.at(t, g))
                    else:
                        pe.wait_ge(s_sq.sem, s_sq.at(t, NX - 1))
                        squares.append(sq_odd[g % 2])
                    if g % GH == 0:
                        pe.wait_ge(s_m.sem, s_m.at(t, Q * G - 1))
                    for q in range(Q):
                        k = q * GH + g % GH
                        for part in squares:
                            last = mm(acc_bank[g // GH][:, k:k + 1], part[:, span(q)], one[:, 0:1], start=part is squares[0],
                                      stop=part is squares[-1], skip_group_check=True)
                    last.then_inc(s_gs.sem, 1)

                def spread_norm(g):
                    if g % GH == 0:
                        pe.wait_ge(d_done.sem, d_done.at(t, f"rt{g // GH}"))
                    b = d_slot(t, ("rb", g))
                    mm(b[:, :], sel[GH][:, g % GH:g % GH + 1].broadcast_to([3 * GH, P]), rstdb[g // GH][0:3 * GH, :],
                       start=True, stop=True).then_inc(d_full.sem, 1)

                for n in range(2, NX):
                    in_block(t, ("z", n), n)
                    if n in SUM_AFTER:
                        square_sum(SUM_AFTER[n])
                    if n == 13:
                        turn_parts(t, "rt0", GH, s_rp.sem, s_rp.at(t, 0))
                square_sum(G - 3)
                spread_norm(0)
                spread_norm(1)
                square_sum(G - 2)
                square_sum(G - 1)
                pe.wait_ge(s_gv.sem, s_gv.at(t, 1))
                for n in range(NX):
                    pe.wait_ge(s_yh.sem, s_yh.at(t, n))
                    pe.wait_ge(s_yl.sem, s_yl.at(t, n))
                    for c in range(KC):
                        cols = slice(c * P, (c + 1) * P)
                        last = pairs(acc_bank[c][:, :], wo_h[:, n, cols], wo_l[:, n, cols], yh[n % NY], yl[n % NY],
                                     start=n == 0, stop=n == NX - 1)
                    last.then_inc(s_wo.sem, 1)
                    if n % 2 == 1 and n // 2 + 2 < G:
                        spread_norm(n // 2 + 2)
                    if n == 3:
                        turn_parts(t, "rt1", GH, s_rp.sem, s_rp.at(t, 1))
                    if n == NX - 3:
                        turn_parts(t, "comb", E + 1, s_parts["cmb"], t + 2)
                    if n == NX - 2:
                        decay_sums(t, t + 1)
                turn_parts(t, "cum", H, s_parts["cum"], t + 2)
                blocks_ahead(t)
                pe.wait_ge(s_out_t.sem, s_out_t.at(t, "out"))
                for j in range(2):
                    b = d_slot(t, f"ot{j}")
                    for k in range(2):
                        for c in range(KC):
                            last = nc.tensor.transpose(b[:, k * D + c * P:k * D + (c + 1) * P],
                                                       out_t[:, c, span(2 * j + k)], ident)
                    last.then_inc(d_full.sem, 1)

        @block.scalar
        def _(act):
            fn = nc.scalar.activation
            done = [0]

            def high_quarter(j, i, raw, hi, scaled):
                n = raw.shape[1] // 4
                c = slice(i * n, (i + 1) * n)
                if scaled:
                    done[0] += 1
                    fn(raw[:, c], raw[:, c], ACT.Copy, scale=up_s[:, j:j + 1]).then_inc(s_scaled, 1)
                    act.wait_ge(s_scaled, done[0])
                    fn(hi[:, c], raw[:, c], ACT.Copy).then_inc(s_hi, 1)
                else:
                    fn(hi[:, c], raw[:, c], ACT.Copy, scale=up_s[:, j:j + 1]).then_inc(s_hi, 1)

            act.wait_ge(s_up, 1)
            for i in (3, 0, 1, 2):
                high_quarter(0, i, raw_in, win_h[:, :, :].rearrange("p c n -> p (c n)"), i == 3)
            act.wait_ge(s_alog, 1)
            fn(neg_a[:, :], row[:, 3, :], ACT.Exp).then_inc(a_done.sem, 1)
            act.wait_ge(s_raw_out, 16)
            for n in range(NX):
                c = slice(n * D, (n + 1) * D)
                ins = fn(raw_out[:, c], raw_out[:, c], ACT.Copy, scale=norm_w[:, n:n + 1])
            ins.then_inc(a_done.sem, 1)
            act.wait_ge(s_up, 2)
            for i in (3, 0, 1, 2):
                high_quarter(1, i, raw_gu, gu_h[:, :, :, :].rearrange("p c j n -> p (c j n)"), i == 3)

            def prep_high(t):
                act.wait_ge(d_done.sem, d_done.at(t, "xn1"))
                for c in range(KC):
                    fn(xh[:, c, :], x32[:, c, :], ACT.Copy).then_inc(s_xh.sem, 1)

            def prep(k):
                act.wait_ge(s_exi, k + 1)
                fn(ex[:, :, :], exi[:, :, :], ACT.Exp).then_inc(s_ex, 1)

            prep_high(None)
            prep(0)
            act.wait_ge(s_up, 4)
            for i in range(4):
                high_quarter(3, i, raw_down, wd_h[:, :, :].rearrange("p n d -> p (n d)"), True)
            for i in range(4):
                high_quarter(2, i, raw_out, wo_h[:, :, :].rearrange("p n d -> p (n d)"), True)
            with act.Fori(0, TILES) as t:
                def conv_silu(n):
                    if n == NCONV - 1:
                        act.wait_ge(s_crow, 16 * (t + 1))
                    if n == 0:
                        act.wait_ge(s_lo_out, 4)
                    if n == 2 * NB:
                        act.wait_ge(s_lo_out, 8)
                    act.wait_ge(s_conv.sem, s_conv.at(t, n))
                    fn(xbc[:, CONV_ORDER[n], :], acc[n % 3], ACT.Silu).then_inc(s_silu.sem, 1)

                def inner_high(f):
                    act.wait_ge(d_done.sem, d_done.at(t, ("bc", f)))
                    if f >= 2:
                        act.wait_ge(s_down.sem, s_down.at(t, f - 2))
                    m = rows_of(f)
                    fn(hh[f % 2][0:m, :], hin[f % 2][0:m, :], ACT.Copy).then_inc(s_hh.sem, 1)

                for f in range(NF):
                    for n in conv_blocks(f):
                        k = NX + CONV_ORDER[n]
                        act.wait_ge(a_full.sem, a_full.at(made_in(t, n), ("u", n)))
                        if n >= 3:
                            act.wait_ge(s_conv.sem, s_conv.at(t, n - 3))
                            act.wait_ge(s_hist.sem, s_hist.at(t, ("hist", n - 3)))
                        fn(u[n % 3][:, TAPS - 1:UW], a_bank[a_full.pos[("u", n)] % RA][:, :], ACT.Identity,
                           bias=ev_bias[:, k:k + 1], scale=ev_scale[:, k:k + 1]).then_inc(a_done.sem, 1)
                        if n >= 2:
                            conv_silu(n - 2)
                    if f == NF - 2:
                        conv_silu(NCONV - 2)
                    if f == NF - 1:
                        conv_silu(NCONV - 1)
                    if f == 2:
                        act.wait_ge(s_tmp, t + 1)
                        fn(w_end[:, :, :], tmp[:, :, :], ACT.Exp).then_inc(s_wend, 1)
                    m = rows_of(f)
                    act.wait_ge(a_full.sem, a_full.at(t, ("gate", f)))
                    if f >= 2:
                        act.wait_ge(d_done.sem, d_done.at(t, ("up", f - 2)))
                    fn(gact[f % 2][0:m, :], a_bank[a_full.pos[("gate", f)] % RA][0:m, :], ACT.Silu,
                       scale=down_s[0:m, 1:2]).then_inc(a_done.sem, 1)
                    if f:
                        inner_high(f - 1)
                inner_high(NF - 1)

                def decay(q, b):
                    act.wait_ge(a_full.sem, a_full.at(t, ("E", q, b)))
                    if q == 0 and b == 0:
                        act.wait_ge(s_hist.sem, s_hist.at(t, ("hist", NCONV - 1)))
                    if q:
                        act.wait_ge(s_cs.sem, s_cs.at(t, (q - 1, b)))
                        act.wait_ge(d_done.sem, d_done.at(t, ("st", q - 1)))
                    fn(eb[:, 4 * b:4 * b + 4, :], a_bank[a_full.pos[("E", q, b)] % RA][:, :], ACT.Exp).then_inc(a_done.sem, 1)

                def decays(s):
                    act.wait_ge(a_full.sem, a_full.at(t, ("diff", s)))
                    if s >= 2:
                        act.wait_ge(s_m.sem, s_m.at(t, s - 2))
                    elif s == 0:
                        act.wait_ge(d_done.sem, d_done.at(t, ("up", NF - 1)))
                    q, g = divmod(s, G)
                    b = a_bank[a_full.pos[("diff", s)] % RA]
                    for h in range(4):
                        ins = fn(lb[s % 2][:, span(h)], b[:, span(h)], ACT.Exp, bias=da[:, q, 4 * g + h:4 * g + h + 1])
                    ins.then_inc(a_done.sem, 1)

                def gate(n):
                    act.wait_ge(a_full.sem, a_full.at(t, ("z", n)))
                    if n >= 2:
                        act.wait_ge(s_y.sem, s_y.at(t, n - 2))
                    fn(sz[n % 2], a_bank[a_full.pos[("z", n)] % RA][:, :], ACT.Silu, bias=ev_bias[:, n:n + 1],
                       scale=ev_scale[:, n:n + 1]).then_inc(a_done.sem, 1)

                decay(0, 0)
                decays(0)
                decays(1)
                for s in range(Q * G):
                    q, g = divmod(s, G)
                    if s + 2 < Q * G:
                        decays(s + 2)
                    else:
                        gate(s + 2 - Q * G)
                    if g == 1:
                        decay(q, 1)
                    if q + 1 < Q and g == 5:
                        decay(q + 1, 0)
                    if s == SMALL_AT + 1:
                        prep(t + 1)
                def square(n):
                    act.wait_ge(s_y.sem, s_y.at(t, n))
                    if n % 2:
                        act.wait_ge(s_pair.sem, s_pair.at(t, n // 2 - 2))
                    elif n >= 6:
                        act.wait_ge(s_gs.sem, s_gs.at(t, n // 2 - 3))
                    fn(sq_odd[n // 2 % 2] if n % 2 else sq[n // 2 % 3], xbc[:, n, :], ACT.Square).then_inc(s_sq.sem, 1)

                act.wait_ge(s_cs.sem, s_cs.at(t, (Q - 1, 1)))
                square(0)
                for n in range(2, NX):
                    gate(n)
                    if n - 1 in SQUARED:
                        square(n - 1)
                square(NX - 1)
                for n in range(NX):
                    if n == 6:
                        prep_high(t)
                    if n % 2 == 0:
                        act.wait_ge(s_yn.sem, s_yn.at(t, n))
                    else:
                        act.wait_ge(d_done.sem, d_done.at(t, ("rb", n // 2)))
                    if n >= NY:
                        act.wait_ge(s_wo.sem, s_wo.at(t, n - NY))
                    fn(yh[n % NY], xbc[:, n, :], ACT.Copy).then_inc(s_yh.sem, 1)

        @block.gpsimd
        def _(pool):
            gp = nc.gpsimd
            gp.memset(half[:, :], -0.5)
            gp.memset(one[:, :], 1.0)
            gp.memset(keep_p[:, :], 0.0)
            gp.memset(hist[:, :, :], 0.0).then_inc(s_hist.sem, 1)
            gp.memset(sc[:, :, :], 0.0)
            gp.memset(w_end[:, :, :], 0.0).then_inc(s_zero, 1)

            def largest(j):
                pool.wait_ge(s_mag, j + 1)
                gp.partition_all_reduce(gmax[:, j:j + 1], amax[:, j:j + 1], P, ABSMAX).then_inc(s_gmax, 1)

            def low_quarter(i, raw, hi, lo, done):
                n = raw.shape[1] // 4
                c = slice(i * n, (i + 1) * n)
                gp.tensor_tensor(lo[:, c], raw[:, c], hi[:, c], ALU.subtract).then_inc(done, 1)

            largest(0)
            pool.wait_ge(s_hi, 1)
            low_quarter(3, raw_in, win_h[:, :, :].rearrange("p c n -> p (c n)"),
                        win_l[:, :, :].rearrange("p c n -> p (c n)"), s_lo_last)
            largest(1)
            largest(2)
            pool.wait_ge(s_hi, 5)
            low_quarter(3, raw_gu, gu_h[:, :, :, :].rearrange("p c j n -> p (c j n)"),
                        gu_l[:, :, :, :].rearrange("p c j n -> p (c j n)"), s_lo_last)
            pool.wait_ge(s_lo, 6)
            pool.wait_ge(s_lo_last, 2)
            gp.memset(sbd, 0.0).then_inc(s_sbd.sem, 1)

            def prep(t, k):
                pool.wait_ge(s_var, k + 1)
                gp.tensor_tensor(rstd[:, :], veps[:, :], half[:, 0:1].broadcast_to([P, Q]), ALU.pow).then_inc(s_pow.sem, 1)

            def prep_low(t):
                for c in range(KC):
                    pool.wait_ge(s_xh.sem, s_xh.at(t, c))
                    gp.tensor_tensor(xl[:, c, :], x32[:, c, :], xh[:, c, :], ALU.subtract).then_inc(s_xl.sem, 1)

            largest(3)
            prep(None, 0)
            prep_low(None)
            for j, raw, hi, lo in ((2, raw_down, wd_h, wd_l), (3, raw_out, wo_h, wo_l)):
                for i in range(4):
                    pool.wait_ge(s_hi, 4 * j + i + 1)
                    low_quarter(i, raw, hi[:, :, :].rearrange("p n d -> p (n d)"),
                                lo[:, :, :].rearrange("p n d -> p (n d)"), s_lo_out)
            with pool.Fori(0, TILES) as t:
                def pad(n):
                    if n >= 3:
                        pool.wait_ge(s_conv.sem, s_conv.at(t, n - 3))
                    elif n == 0:
                        pool.wait_ge(s_hist.sem, s_hist.n0 + s_hist.n * t)
                        pool.wait_ge(s_zero, t + 1)
                    gp.tensor_tensor(u[n % 3][:, 0:TAPS - 1], hist[:, CONV_ORDER[n], :],
                                     keep_p[:, 0:1].broadcast_to([P, TAPS - 1]), ALU.mult).then_inc(s_u.sem, 1)

                def keep_history(n):
                    pool.wait_ge(a_done.sem, a_done.at(made_in(t, n), ("u", n)))
                    pool.wait_ge(s_u.sem, s_u.at(t, ("pad", n)))
                    gp.tensor_tensor(hist[:, CONV_ORDER[n], :], u[n % 3][:, TT:UW],
                                     one[:, 0:1].broadcast_to([P, TAPS - 1]), ALU.mult).then_inc(s_hist.sem, 1)

                def inner_low(f):
                    m = rows_of(f)
                    pool.wait_ge(s_hh.sem, s_hh.at(t, f))
                    gp.tensor_tensor(hl[f % 2][0:m, :], hin[f % 2][0:m, :], hh[f % 2][0:m, :], ALU.subtract).then_inc(s_hl.sem, 1)

                for f in range(NF):
                    for n in conv_blocks(f):
                        pad(n)
                        if n:
                            keep_history(n - 1)
                    if f:
                        inner_low(f - 1)
                keep_history(NCONV - 1)
                inner_low(NF - 1)
                pool.wait_ge(s_u.sem, s_u.at(t, ("pad", NCONV - 1)))
                gp.tensor_tensor(keep_p[:, :], one[:, :], keep_p[:, :], ALU.subtract).then_inc(s_zero, 1)

                pool.wait_ge(s_silu.sem, s_silu.at(t, NCONV - 1))
                pool.wait_ge(s_hist.sem, s_hist.at(t, ("hist", NCONV - 1)))

                def own_rows(q, b):
                    if q:
                        pool.wait_ge(s_g.sem, s_g.at(t, (q - 1, b)))
                    gp.tensor_tensor(cm[:, 4 * b:4 * b + 4, :], xbc[:, NX + NB + b, span(q)].unsqueeze(1).broadcast_to([P, 4, P]),
                                     ownrow.unsqueeze(2).broadcast_to([P, 4, P]), ALU.mult).then_inc(s_cm.sem, 1)

                def scale_c(q, b):
                    pool.wait_ge(s_crep[b], 4 * 16 * (t * Q + q + 1))
                    pool.wait_ge(a_done.sem, a_done.at(t, ("E", q, b)))
                    v = crep[:, 4 * b:4 * b + 4, :]
                    gp.tensor_tensor(v, v, eb[:, 4 * b:4 * b + 4, :], ALU.mult).then_inc(s_cs.sem, 1)
                    pool.wait_ge(s_cs.sem, s_cs.at(t, (q, b)))

                def spread(q, b):
                    if q + 1 < Q:
                        pool.wait_ge(d_done.sem, d_done.at(t, ("st", q)))
                    else:
                        pool.wait_ge(s_carry, t + 1)
                    pool.wait_ge(d_full.sem, d_full.at(t, ("y", G * q + 4 * b + 3)))
                    gp.tensor_tensor(sbd[:, 4 * b:4 * b + 4, :].rearrange("p g (h w) -> p g h w", h=4),
                                     sc[:, 4 * b:4 * b + 4, :].unsqueeze(2).broadcast_to([P, 4, 4, HP]),
                                     ownrow.unsqueeze(1).unsqueeze(3).broadcast_to([P, 4, 4, HP]),
                                     ALU.mult).then_inc(s_sbd.sem, 1)

                own_rows(0, 0)
                own_rows(0, 1)
                scale_c(0, 0)
                scale_c(0, 1)
                for q in range(Q):
                    if q + 1 < Q:
                        own_rows(q + 1, 0)
                    spread(q, 0)
                    if q == 0:
                        prep(t, t + 1)
                    if q + 1 < Q:
                        scale_c(q + 1, 0)
                        own_rows(q + 1, 1)
                    spread(q, 1)
                    if q + 1 < Q:
                        scale_c(q + 1, 1)

                def add_pair(g):
                    if g < GH:
                        pool.wait_ge(s_odd.sem, s_odd.at(t, g))
                        pool.wait_ge(s_sq.sem, s_sq.at(t, 2 * g))
                    else:
                        pool.wait_ge(s_sq.sem, s_sq.at(t, 2 * g + 1))
                    gp.tensor_tensor(sq[g % 3], sq[g % 3], sq_odd[g % 2], ALU.add).then_inc(s_pair.sem, 1)

                def group_roots(k):
                    pool.wait_ge(s_gv.sem, s_gv.at(t, k))
                    gp.tensor_tensor(gv[:, :], gv[:, :], half[:, 0:1].broadcast_to([P, Q * GH]), ALU.pow).then_inc(s_pow.sem, 1)

                def y_low(n):
                    pool.wait_ge(s_yh.sem, s_yh.at(t, n))
                    gp.tensor_tensor(yl[n % NY], xbc[:, n, :], yh[n % NY], ALU.subtract).then_inc(s_yl.sem, 1)

                for g in range(G - 1):
                    add_pair(g)
                    if g == GH - 1:
                        group_roots(0)
                y_low(0)
                y_low(1)
                group_roots(1)
                for n in range(2, NX):
                    y_low(n)
                    if n == 7:
                        prep_low(t)

        @block.vector
        def _(dve):
            v = nc.vector
            links = [0]
            base = [0]

            def link(ins):
                links[0] += 1
                ins.then_inc(s_chain, 1)
                dve.wait_ge(s_chain, base[0] + links[0])

            def magnitude(j, raw):
                v.tensor_reduce(amax[:, j:j + 1], raw, AX.X, ALU.max, apply_absolute_value=True).then_inc(s_mag, 1)

            def scale(j):
                dve.wait_ge(s_gmax, j + 1)
                g, p2, up = gmax[:, j:j + 1], pow2[:, j:j + 1], up_s[:, j:j + 1]
                link(v.tensor_scalar(g, g, 1e-30, 1e36, ALU.max, ALU.min))
                link(v.tensor_scalar(p2.bitcast(U32), g.bitcast(U32), 0x7F800000, None, ALU.bitwise_and))
                link(v.reciprocal(up, p2))
                link(v.tensor_scalar(down_s[:, j:j + 1], p2, 1.0 / UP, None, ALU.mult))
                v.tensor_scalar(up, up, UP, None, ALU.mult).then_inc(s_up, 1)

            def low(j, raw, hi, lo):
                n = raw.shape[1] // 4
                dve.wait_ge(s_up, j + 1)
                for i in range(3):
                    dve.wait_ge(s_hi, 4 * j + i + 2)
                    c = slice(i * n, (i + 1) * n)
                    v.scalar_tensor_tensor(lo[:, c], raw[:, c], up_s[:, j:j + 1], hi[:, c],
                                           ALU.mult, ALU.subtract).then_inc(s_lo, 1)

            v.memset(keep_v[:, :], 1.0).then_inc(s_out_t.sem, 1)
            v.memset(carrier[:, :], 0.0).then_inc(s_out, 16)
            n_in = raw_in.shape[1] // 4
            for i in range(4):
                dve.wait_ge(s_quarter[i], 16)
                ins = v.tensor_reduce(amax_q[:, i:i + 1], raw_in[:, i * n_in:(i + 1) * n_in], AX.X, ALU.max,
                                      apply_absolute_value=True)
            link(ins)
            magnitude(0, amax_q[:, :])
            dve.wait_ge(s_par, 2 * 16)
            v.tensor_scalar(row[:, 3, :], row[:, 3, :], A_LOG_TOP, None, ALU.min).then_inc(s_alog, 1)
            scale(0)
            link(v.tensor_scalar(ev_scale[:, :], mup, down_s[:, 0:1], None, ALU.mult))
            link(v.tensor_tensor(ev_bias[:, :], mup, b_in, ALU.mult))
            low(0, raw_in, win_h[:, :, :].rearrange("p c n -> p (c n)"), win_l[:, :, :].rearrange("p c n -> p (c n)"))
            dve.wait_ge(s_raw_gu, 4 * 16)
            magnitude(1, raw_gu)
            dve.wait_ge(a_done.sem, a_done.at(None, "a_log"))
            link(v.tensor_scalar(neg_a[:, :], neg_a[:, :], -1.0, None, ALU.mult))
            scale(1)
            dve.wait_ge(a_done.sem, a_done.at(None, "normed"))
            magnitude(2, raw_out)
            low(1, raw_gu, gu_h[:, :, :, :].rearrange("p c j n -> p (c j n)"),
                gu_l[:, :, :, :].rearrange("p c j n -> p (c j n)"))
            dve.wait_ge(s_raw_down, 16)
            magnitude(3, raw_down)
            scale(2)
            scale(3)
            v.tensor_scalar(in_scale[:, :], up_s[:, 1:2], 1.0 / (8 * UP * UP), None, ALU.mult)
            link(v.tensor_scalar(out_scale[:, :], pow2[:, 1:2], pow2[:, 1:2], 8.0, ALU.mult, ALU.mult))
            link(v.tensor_scalar(out_scale[:, :], out_scale[:, :], down_s[:, 3:4], None, ALU.mult))

            def taken(t, item):
                dve.wait_ge(d_full.sem, d_full.at(t, item))
                return d_bank[(d_full.first[item] if t is None else d_full.pos[item]) % RD]

            def split3(src, n):
                parts, left = parts_of[n], left_of[n]
                link(v.tensor_copy(parts[:, :, 0, :], src))
                link(v.tensor_tensor(left, src, parts[:, :, 0, :], ALU.subtract))
                link(v.tensor_copy(parts[:, :, 1, :], left))
                return v.tensor_tensor(parts[:, :, 2, :], left, parts[:, :, 1, :], ALU.subtract)

            def take_parts(t, item, n, dst):
                b = taken(t, item)
                v.tensor_copy(dst[0:3 * n, :], b[0:3 * n, :]).then_inc(d_done.sem, 1)

            def prep_stats(k):
                dve.wait_ge(s_x, 16 * (k + 1))
                for q in range(Q):
                    ins = v.bn_stats(stat[:, q, :], xld[:, q, :])
                link(ins)
                carry_vector()
                for q in range(Q):
                    ins = v.bn_aggr(mv[:, q, :], stat[:, q, :])
                link(ins)
                v.tensor_scalar(veps[:, :], mv[:, :, 1], EPS, None, ALU.add).then_inc(s_var, 1)

            def prep_norm(t):
                dve.wait_ge(s_pow.sem, s_pow.at(t, "ln"))
                for q in range(Q):
                    ins = v.tensor_scalar(xld[:, q, :], xld[:, q, :], mv[:, q, 0:1], rstd[:, q:q + 1],
                                          ALU.subtract, ALU.mult)
                ins.then_inc(s_xn, 1)

            def prep_turned(t):
                taken(t, "xn1")
                for c in range(KC):
                    b = taken(t, f"xn{c}")
                    v.tensor_copy(x32[:, c, :], b[:, :]).then_inc(d_done.sem, 1)

            def prep_exp(t):
                w = H + E + 1
                b = taken(t, "small")[:, 0:Q * w].rearrange("p (q w) -> p q w", q=Q)
                link(v.tensor_reduce(lmax[:, :], b[:, :, H:H + E], AX.X, ALU.max))
                v.tensor_tensor(exi[:, :, H:H + E], b[:, :, H:H + E], lmax[:, :].unsqueeze(2).broadcast_to([P, Q, E]),
                                ALU.subtract)
                v.tensor_scalar(exi[:, :, w - 1], b[:, :, w - 1], -1.0, None, ALU.mult)

                def on_heads(k):
                    return row[:, k, :].unsqueeze(1).broadcast_to([P, Q, H])

                v.tensor_tensor(v_dt[:, :, :], b[:, :, 0:H], on_heads(0), ALU.add).then_inc(d_done.sem, 1)
                dve.wait_ge(d_done.sem, d_done.at(t, "small"))
                link(v.tensor_tensor(v_dt[:, :, :], v_dt[:, :, :], on_heads(1), ALU.mult))
                link(v.tensor_tensor(v_dt[:, :, :], v_dt[:, :, :], on_heads(2), ALU.add))
                v.scalar_tensor_tensor(exi[:, :, 0:H], v_dt[:, :, :], -1.0, v_dt[:, :, :], ALU.mult,
                                       ALU.min).then_inc(s_exi, 1)

            def route():
                link(v.tensor_reduce(lsum[:, :], ex[:, :, H:H + E], AX.X, ALU.add))
                link(v.reciprocal(lsum[:, :], lsum[:, :]))
                link(v.tensor_tensor(probs[:, :, :], ex[:, :, H:H + E], lsum[:, :].unsqueeze(2).broadcast_to([P, Q, E]),
                                     ALU.mult))

            def route_chunk(q):
                other = probs[:, q, :].unsqueeze(1).broadcast_to([P, E, E])
                own = probs[:, q, :].unsqueeze(2).broadcast_to([P, E, E])
                link(v.tensor_tensor(big[0], other, own, ALU.is_equal))
                link(v.tensor_tensor(big[0], big[0], lower, ALU.mult))
                link(v.tensor_tensor(big[1], other, own, ALU.is_gt))
                link(v.tensor_tensor(big[1], big[1], big[0], ALU.add))
                link(v.tensor_reduce(rank, big[1], AX.X, ALU.add))
                link(v.scalar_tensor_tensor(cmb[:, q, 0:E], rank, 1.5, probs[:, q, :], ALU.is_lt, ALU.mult))
                if q == Q - 1:
                    link(v.tensor_scalar(lmax[:, :], ex[:, :, H + E], 1.0, None, ALU.add))
                    v.reciprocal(cmb[:, :, E], lmax[:, :]).then_inc(s_route, 1)

            e, series = ex[:, :, 0:H], exi[:, :, 0:H]

            def steps_ratio():
                link(v.tensor_scalar(tmp[:, :, :], e, 2.0, None, ALU.add))
                link(v.reciprocal(tmp[:, :, :], tmp[:, :, :]))
                link(v.tensor_tensor(tmp[:, :, :], tmp[:, :, :], e, ALU.mult))
                link(v.tensor_tensor(e, tmp[:, :, :], tmp[:, :, :], ALU.mult))
                link(v.tensor_scalar(series, e, 1.0 / 15, None, ALU.mult))

            def steps_series():
                for k in (13, 11, 9, 7, 5, 3):
                    link(v.scalar_tensor_tensor(series, series, 1.0 / k, e, ALU.add, ALU.mult))

            def steps_softplus():
                link(v.scalar_tensor_tensor(series, series, 1.0, tmp[:, :, :], ALU.add, ALU.mult))
                link(v.tensor_scalar(v_dt[:, :, :], v_dt[:, :, :], 0.0, None, ALU.max))
                link(v.scalar_tensor_tensor(v_dt[:, :, :], series, 2.0, v_dt[:, :, :], ALU.mult, ALU.add))

            def steps():
                v.tensor_copy(dt[:, :, :], v_dt[:, :, :])
                link(v.tensor_tensor(da[:, :, :], v_dt[:, :, :], neg_a[:, :].unsqueeze(1).broadcast_to([P, Q, H]),
                                     ALU.mult))
                v.tensor_scalar(da[:, :, :], da[:, :, :], DECAY_FLOOR, None, ALU.max).then_inc(s_da, 1)

            def split_cmb():
                split3(cmb[:, :, :], E + 1).then_inc(s_parts["cmb"], 1)

            def take_sums(t):
                b = taken(t, "sums")
                v.tensor_copy(tmp[:, :, :], b[:, 0:Q * H]).then_inc(s_tmp, 1)
                cum = b[:, Q * H:2 * Q * H].rearrange("p (q h) -> p q h", q=Q)
                split3(cum, H).then_inc(s_parts["cum"], 1)
                v.tensor_scalar(da[:, :, :], cum, -1.0, None, ALU.mult).then_inc(d_done.sem, 1)

            prep_stats(0)
            prep_norm(None)
            prep_turned(None)
            prep_exp(None)
            dve.wait_ge(s_ex, 1)
            route()
            for q in range(Q):
                route_chunk(q)
            steps_ratio()
            steps_series()
            steps_softplus()
            steps()
            dve.wait_ge(s_zero, 1)
            dve.wait_ge(s_route, 1)
            split_cmb()
            take_parts(None, "comb", E + 1, cmbb)
            take_sums(None)
            take_parts(None, "cum", H, cumb)
            before = links[0]
            with dve.Fori(0, TILES) as t:
                links[0] = 0
                base[0] = before + t * V_LINKS

                def conv(n):
                    k = CONV_ORDER[n]
                    uu, a = u[n % 3], acc[n % 3]
                    w = conv_w[:, TAPS * k:TAPS * (k + 1)]
                    dve.wait_ge(a_done.sem, a_done.at(made_in(t, n), ("u", n)))
                    dve.wait_ge(s_u.sem, s_u.at(t, ("pad", n)))
                    if n >= 3:
                        dve.wait_ge(s_silu.sem, s_silu.at(t, n - 3))
                    link(v.tensor_scalar(a, uu[:, TAPS - 1:UW], w[:, TAPS - 1:TAPS], conv_b[:, k:k + 1],
                                         ALU.mult, ALU.add))
                    for j in range(TAPS - 1):
                        ins = v.scalar_tensor_tensor(a, uu[:, j:j + TT], w[:, j:j + 1], a, ALU.mult, ALU.add)
                        if j < TAPS - 2:
                            link(ins)
                    ins.then_inc(s_conv.sem, 1)

                def inner(n):
                    m = rows_of(n)
                    h = hin[n % 2][0:m, :]
                    b = taken(t, ("up", n))
                    dve.wait_ge(a_done.sem, a_done.at(t, ("gate", n)))
                    if n >= 2:
                        dve.wait_ge(s_hl.sem, s_hl.at(t, n - 2))
                    v.scalar_tensor_tensor(h, b[0:m, :], in_scale[0:m, 0:1], gact[n % 2][0:m, :], ALU.mult,
                                           ALU.mult).then_inc(d_done.sem, 1)
                    b = taken(t, ("bc", n))
                    dve.wait_ge(d_done.sem, d_done.at(t, ("up", n)))
                    v.tensor_tensor(h, h, b[0:m, :], ALU.mult).then_inc(d_done.sem, 1)

                def steps_x(q, r):
                    b = taken(t, ("xt", q, r))
                    v.tensor_tensor(xd[:, r * TT:(r + 1) * TT].rearrange("p (h w) -> p h w", h=8),
                                    b[:, :].rearrange("p (h w) -> p h w", h=8),
                                    dt[:, q, 8 * r:8 * r + 8].unsqueeze(2).broadcast_to([P, 8, HP]),
                                    ALU.mult).then_inc(d_done.sem, 1)

                def decayed_b(q):
                    b = taken(t, ("bt", q))
                    if q == 0:
                        dve.wait_ge(s_wend, t + 1)
                    v.tensor_tensor(bp, b[:, 0:G * S].rearrange("p (g s) -> p g s", g=G).unsqueeze(2).broadcast_to([P, G, 4, S]),
                                    w_end[:, q, :].rearrange("p (g h) -> p g h", g=G).unsqueeze(3).broadcast_to([P, G, 4, S]),
                                    ALU.mult).then_inc(d_done.sem, 1)

                for k in range(NF):
                    for n in conv_blocks(k):
                        conv(n)
                    inner(k)
                    if k == NF - 2:
                        dve.wait_ge(s_out, 16 * (t + 1))
                        steps_x(0, 0)
                        steps_x(0, 1)
                        decayed_b(0)
                    if k == NF - 1:
                        steps_x(0, 2)
                        steps_x(0, 3)
                for c in range(KC):
                    dve.wait_ge(s_down.sem, s_down.at(t, (NF - 1, c)))
                    v.tensor_scalar(out_t[:, c, :], acc_bank[c][:, :], out_scale[:, 0:1], b_out[:, c:c + 1],
                                    ALU.mult, ALU.add).then_inc(s_ffn.sem, 1)

                def new_states(q):
                    dve.wait_ge(a_done.sem, a_done.at(t, ("E", q, 1)))
                    if q:
                        dve.wait_ge(s_sbd.sem, s_sbd.at(t, (q - 1, 1)))
                    else:
                        dve.wait_ge(s_sbd.sem, s_sbd.n0 + t * s_sbd.n)
                    link(v.tensor_tensor(sc[:, :, :], sc[:, :, :], eb[:, :, P - 1:P].broadcast_to([P, G, HP]), ALU.mult))
                    b = taken(t, ("st", q))
                    v.tensor_tensor(sc[:, :, :], sc[:, :, :], b[:, :].rearrange("p (g w) -> p g w", g=G),
                                    ALU.add).then_inc(d_done.sem, 1)
                    if q == Q - 1:
                        dve.wait_ge(d_done.sem, d_done.at(t, ("st", q)))
                        v.tensor_scalar(sc[:, :, :], sc[:, :, :], keep_v[:, 0:1], None, ALU.mult).then_inc(s_carry, 1)
                        dve.wait_ge(s_carry, t + 1)
                        link(v.tensor_scalar(keep_v[:, :], keep_v[:, :], -1.0, 1.0, ALU.mult, ALU.add))

                def weigh(s):
                    q, g = divmod(s, G)
                    dve.wait_ge(a_done.sem, a_done.at(t, ("diff", s)))
                    dve.wait_ge(s_g.sem, s_g.at(t, (q, g // 4)))
                    if s >= 2:
                        dve.wait_ge(d_full.sem, d_full.at(t, ("y", s - 2)))
                    k = g % 4
                    v.tensor_tensor(mb[s % 2].rearrange("p (h i) -> p h i", h=4),
                                    lb[s % 2].rearrange("p (h i) -> p h i", h=4),
                                    acc_bank[g // 4][:, span(k)].unsqueeze(1).broadcast_to([P, 4, P]),
                                    ALU.mult).then_inc(s_m.sem, 1)

                def take_y(s):
                    q, g = divmod(s, G)
                    b = taken(t, ("y", s))
                    for k in range(2):
                        xx = xbc[:, 2 * g + k, span(q)]
                        ins = v.scalar_tensor_tensor(xx, xx, d_par[:, 2 * g + k:2 * g + k + 1], b[:, span(k)],
                                                     ALU.mult, ALU.add)
                    ins.then_inc(d_done.sem, 1)

                weigh(0)
                weigh(1)
                for s in range(Q * G):
                    q, g = divmod(s, G)
                    take_y(s)
                    if s + 2 < Q * G:
                        weigh(s + 2)
                    if g == 2:
                        new_states(q)
                    if q + 1 < Q:
                        if g in (2, 4, 6):
                            steps_x(q + 1, g // 2 - 1)
                        if g == 5:
                            decayed_b(q + 1)
                        if g == 7:
                            steps_x(q + 1, 3)
                    if s == STATS_AT:
                        prep_stats(t + 1)
                    if s == NORM_AT:
                        prep_norm(t)
                    if s == TURN_AT:
                        prep_turned(t)
                    if s == SMALL_AT:
                        prep_exp(t)
                    if s == ROUTE_AT:
                        dve.wait_ge(s_ex, t + 2)
                        route()
                    if s in ROUTE_CHUNK_AT:
                        route_chunk(ROUTE_CHUNK_AT[s])
                    if s == STEPS_AT:
                        steps_ratio()
                    if s == STEPS_AT + 1:
                        steps_series()
                    if s == STEPS_AT + 2:
                        steps_softplus()

                def group_squares(k):
                    dve.wait_ge(s_gs.sem, s_gs.at(t, GH * k + GH - 1))
                    v.tensor_scalar(gv[:, :], acc_bank[k][:, 0:Q * GH], float(G) / DS, EPS, ALU.mult, ALU.add).then_inc(s_gv.sem, 1)

                def split_roots(k):
                    dve.wait_ge(s_pow.sem, s_pow.at(t, f"g{k}"))
                    split3(gv[:, :].rearrange("p (q g) -> p q g", q=Q), GH).then_inc(s_rp.sem, 1)

                def normalise(n):
                    b = taken(t, ("rb", n // 2))
                    ins = v.tensor_tensor(xbc[:, n, :], xbc[:, n, :], b[:, :], ALU.mult)
                    ins.then_inc(s_yn.sem if n % 2 == 0 else d_done.sem, 1)

                dve.wait_ge(d_done.sem, d_done.at(t, ("y", Q * G - 1)))
                for n in range(NX):
                    dve.wait_ge(a_done.sem, a_done.at(t, ("z", n)))
                    v.tensor_tensor(xbc[:, n, :], xbc[:, n, :], sz[n % 2], ALU.mult).then_inc(s_y.sem, 1)
                    if n % 2 and n < NX // 2:
                        g = n // 2
                        dve.wait_ge(s_y.sem, s_y.at(t, n))
                        if g >= 2:
                            dve.wait_ge(s_pair.sem, s_pair.at(t, g - 2))
                        v.tensor_tensor(sq_odd[g % 2], xbc[:, n, :], xbc[:, n, :], ALU.mult).then_inc(s_odd.sem, 1)
                    if n == 9:
                        group_squares(0)
                    if n == 12:
                        split_roots(0)
                    if n == 14:
                        take_parts(t, "rt0", GH, rstdb[0])
                for n in range(NX):
                    normalise(n)
                    if n == 1:
                        group_squares(1)
                    if n == 5:
                        split_roots(1)
                    if n == 7:
                        take_parts(t, "rt1", GH, rstdb[1])
                    if n == 8:
                        split_cmb()
                    if n == 9:
                        steps()
                take_parts(t, "comb", E + 1, cmbb)
                take_sums(t)
                take_parts(t, "cum", H, cumb)
                dve.wait_ge(s_wo.sem, s_wo.at(t, NX - 1))
                for c in range(KC):
                    ins = v.scalar_tensor_tensor(out_t[:, c, :], acc_bank[c][:, :], down_s[:, 2:3], out_t[:, c, :],
                                                 ALU.mult, ALU.add)
                ins.then_inc(s_out_t.sem, 1)
                dve.wait_ge(s_xres, 16 * (t + 1))
                for j in range(2):
                    b = taken(t, f"ot{j}")
                    res = xres[:, 2 * j:2 * j + 2, :]
                    v.tensor_tensor(res, res, b[:, :].rearrange("p (q d) -> p q d", q=2), ALU.add).then_inc(d_done.sem, 1)
                assert links[0] == V_LINKS, links[0]


def kernel(L0_attn_hidden_states, L0_attn_W_in, L0_attn_b_in, L0_attn_conv_w, L0_attn_conv_b, L0_attn_A_log,
           L0_attn_D_param, L0_attn_dt_bias, L0_attn_norm_w, L0_attn_W_out, L0_attn_b_out, L0_attn_mup_vector,
           L0_ffn_W_router, L0_ffn_W_sgate, L0_ffn_Ws_gate_up, L0_ffn_Ws_down, L0_ffn_We_gate_up, L0_ffn_We_down):
    import numpy as np
    import concourse.bacc as bacc
    from concourse.bass_utils import run_bass_kernel_spmd

    f = np.float32

    def on_p(a):
        a = np.asarray(a)
        return a.reshape((-1, P) + a.shape[1:]).swapaxes(0, 1)

    def flat(a):
        return np.ascontiguousarray(a.reshape(P, -1))

    x = np.asarray(L0_attn_hidden_states)
    shape = x.shape
    x = x.reshape(TILES, Q, P, D).transpose(0, 2, 1, 3)
    x = np.ascontiguousarray(np.concatenate([x, x[:1]]))
    w_in = np.asarray(L0_attn_W_in)
    wide = 2 * DS + 2 * G * S
    mup, b_in = np.asarray(L0_attn_mup_vector), np.asarray(L0_attn_b_in)
    w_small = np.concatenate([w_in[:, wide:], np.asarray(L0_ffn_W_router).T, np.asarray(L0_ffn_W_sgate).T], axis=1)
    gu_s, gu_e = np.asarray(L0_ffn_Ws_gate_up), np.asarray(L0_ffn_We_gate_up)

    main = I_MOE - TAIL

    def inner(k):
        experts = [gu_e[e][:, k * I_MOE:(k + 1) * I_MOE] for e in range(E)]
        return np.concatenate([gu_s[:, k * I_SH:(k + 1) * I_SH]] + [w[:, :main] for w in experts]
                              + [w[:, main:] for w in experts], axis=1)

    w_gu = np.stack([inner(0), inner(1)], axis=1)
    down_e = np.asarray(L0_ffn_We_down)
    down = np.concatenate([np.asarray(L0_ffn_Ws_down), down_e[:, :main].reshape(-1, D), down_e[:, main:].reshape(-1, D),
                           np.zeros((NF * P - FI, D), f)])
    par = np.concatenate([flat(on_p(mup[:wide])), flat(on_p(b_in[:wide])), flat(on_p(L0_attn_conv_w)),
                          flat(on_p(L0_attn_conv_b)), flat(on_p(np.repeat(np.asarray(L0_attn_D_param), HP))),
                          flat(on_p(L0_attn_norm_w)), flat(on_p(L0_attn_b_out))], axis=1)
    rows = np.stack([b_in[wide:], mup[wide:], np.asarray(L0_attn_dt_bias), np.asarray(L0_attn_A_log)])
    rows = np.ascontiguousarray(np.broadcast_to(rows, (P,) + rows.shape))

    i = np.arange(P)
    lower = np.broadcast_to(np.tril(np.ones((E, E)), -1), (P, E, E)).reshape(P, -1)
    constf = np.concatenate([np.eye(P), i[:, None] <= i, i[:, None] > i, i[:, None] // S == np.arange(4), lower], axis=1).astype(f)
    sel = [(i[:, None] % n == np.arange(n)) & (i[:, None] < 3 * n) for n in (H, E + 1, GH)]
    tail = (i[:, None] % (E + 1) == i // TAIL) & (i[:, None] < 3 * (E + 1))
    constb = np.concatenate([np.eye(P), np.where(i[:, None] > i, -32768.0, 0.0)] + sel + [tail], axis=1)
    constb = np.ascontiguousarray(constb.astype(f).view(np.uint32) >> 16).astype(np.uint16)

    arrays = {"x": x, "w_in": flat(on_p(w_in[:, :wide])), "w_small": np.ascontiguousarray(on_p(w_small)),
              "w_gu": flat(on_p(w_gu)), "w_out": flat(on_p(L0_attn_W_out)), "w_down": np.ascontiguousarray(on_p(down)),
              "par": np.ascontiguousarray(par), "rows": rows, "constf": constf, "constb": constb}
    nc = bacc.Bacc("TRN2", target_bir_lowering=False, num_devices=1)
    args = [nc.dram_tensor(k, a.shape, mybir.dt.from_np(a.dtype), kind="ExternalInput").ap() for k, a in arrays.items()]
    out = nc.dram_tensor("out", (TILES, P, Q, D), F32, kind="ExternalOutput").ap()
    c_rows = nc.dram_tensor("c_rows", (NB, P, TT), F32, kind="Internal").ap()
    layer_program(nc, *args, c_rows, out)
    r = run_bass_kernel_spmd(nc, [arrays], core_ids=[0])
    return r.results[0]["out"].transpose(0, 2, 1, 3).reshape(shape)
```
